# Optimizing a Trainium2 kernel written in Bass

```python
import numpy as np
import jax
import jax.numpy as jnp

def _softmax(x, axis=-1):
    return jax.nn.softmax(x, axis=axis)

def _gelu(x):
    return jax.nn.gelu(x, approximate=True)

def _silu(x):
    return jax.nn.silu(x)

def _sigmoid(x):
    return jax.nn.sigmoid(x)

def _layernorm(x, axis=-1, eps=1e-05):
    m = jnp.mean(x, axis=axis, keepdims=True)
    v = jnp.var(x, axis=axis, keepdims=True)
    return (x - m) / jnp.sqrt(v + eps)

def _scatter_add(tgt, idx, src, axis=0):
    return tgt.at[idx].add(src)

def _segment_sum(src, seg, n):
    return jax.ops.segment_sum(src, seg, n)
kernel_name = 'mk_decoder_postln_d2_seqx_r8_f475ed'

def setup_inputs(seed: int=0):
    np.random.seed(seed)
    _w = jnp.asarray

    def _rec_inputs():
        import jax
        import jax.numpy as jnp
        _rk = jax.random.key(seed)
        x = -0.0002928 + 1 * jax.random.normal(jax.random.fold_in(_rk, 1), (16, 128, 128), jnp.float32)
        _lenS = 128 - jax.random.randint(jax.random.fold_in(_rk, 7), (16,), 0, max(1, 128 // 4) + 1, jnp.int32)
        _lenS2 = 77 - jax.random.randint(jax.random.fold_in(_rk, 8), (16,), 0, max(1, 77 // 4) + 1, jnp.int32)
        _ctx_1024P = jax.random.normal(jax.random.fold_in(_rk, 11), (16, 16, 128), jnp.float32)
        _ctx_1024c = jax.random.dirichlet(jax.random.fold_in(_rk, 511), 0.3 * jnp.ones((16,), jnp.float32), (16, 77))
        _ctx_1024t = jnp.einsum('bsk,bkd->bsd', _ctx_1024c, _ctx_1024P)
        _ctx_1024t = _ctx_1024t * jax.lax.rsqrt(jnp.mean(jnp.square(_ctx_1024t)) + 1e-12) * 0.953939
        ctx_1024 = -1.39393e-06 + 0.999914 * (_ctx_1024t + 0.3 * jax.random.normal(jax.random.fold_in(_rk, 611), (16, 77, 128), jnp.float32))
        return (x, ctx_1024)
    x, ctx_1024 = _rec_inputs()

    def _L0_attn_setup():
        import jax, jax.numpy as jnp
        import numpy as np
        EMBED_DIM = 128
        N_HEADS = 16
        HEAD_DIM = EMBED_DIM // N_HEADS
        MAX_REL = 64
        B, S = (4, 128)
        key = jax.random.key(seed)
        ks = jax.random.split(key, 10)
        sc = 1.0 / np.sqrt(EMBED_DIM)
        return {'q': jax.random.normal(ks[0], (B, S, EMBED_DIM), jnp.float32), 'Wq': jax.random.normal(ks[1], (EMBED_DIM, EMBED_DIM), jnp.float32) * sc, 'bq': jax.random.normal(ks[2], (EMBED_DIM,), jnp.float32) * 0.02, 'Wk': jax.random.normal(ks[3], (EMBED_DIM, EMBED_DIM), jnp.float32) * sc, 'bk': jax.random.normal(ks[4], (EMBED_DIM,), jnp.float32) * 0.02, 'Wv': jax.random.normal(ks[5], (EMBED_DIM, EMBED_DIM), jnp.float32) * sc, 'bv': jax.random.normal(ks[6], (EMBED_DIM,), jnp.float32) * 0.02, 'Wo': jax.random.normal(ks[7], (EMBED_DIM, EMBED_DIM), jnp.float32) * sc, 'bo': jax.random.normal(ks[8], (EMBED_DIM,), jnp.float32) * 0.02, 'rel_table': jax.random.normal(ks[9], (2 * MAX_REL + 1, HEAD_DIM), jnp.float32) * 0.02}
    _L0_attn_all = _L0_attn_setup()
    _L0_attn_in = {k: v for k, v in _L0_attn_all.items() if k in ('Wq', 'bq', 'Wk', 'bk', 'Wv', 'bv', 'Wo', 'bo', 'rel_table')}
    del _L0_attn_all

    def _L0_xattn_setup():
        import jax, jax.numpy as jnp
        import numpy as np
        HEADS = 16
        DIM_HEAD = 64
        QUERY_DIM = 128
        INNER = HEADS * DIM_HEAD
        SCALE = DIM_HEAD ** (-0.5)
        key = jax.random.key(seed)
        ks = jax.random.split(key, 6)
        B, N, M = (2, 256, 256)
        x = jax.random.normal(ks[0], (B, N, QUERY_DIM), dtype=jnp.float32)
        context = jax.random.normal(ks[1], (B, M, QUERY_DIM), dtype=jnp.float32)
        s = QUERY_DIM ** (-0.5)
        Wq = jax.random.normal(ks[2], (QUERY_DIM, INNER), dtype=jnp.float32) * s
        Wk = jax.random.normal(ks[3], (QUERY_DIM, INNER), dtype=jnp.float32) * s
        Wv = jax.random.normal(ks[4], (QUERY_DIM, INNER), dtype=jnp.float32) * s
        Wo = jax.random.normal(ks[5], (INNER, QUERY_DIM), dtype=jnp.float32) * INNER ** (-0.5)
        return {'x': x, 'context': context, 'Wq': Wq, 'Wk': Wk, 'Wv': Wv, 'Wo': Wo}
    _L0_xattn_all = _L0_xattn_setup()
    _L0_xattn_in = {k: v for k, v in _L0_xattn_all.items() if k in ('Wq', 'Wk', 'Wv', 'Wo')}
    del _L0_xattn_all

    def _L0_ffn_setup():
        import math
        import jax, jax.numpy as jnp
        import numpy as np
        NUM_EXPERTS = 8
        TOP_K = 2
        CAPACITY_FACTOR = 1.0
        B, S, H, I = (4, 256, 128, 512)
        key = jax.random.key(seed)
        k_x, k_rw, k_wi, k_wo = jax.random.split(key, 4)
        x = jax.random.normal(k_x, (B, S, H), dtype=jnp.float32)
        lim = math.sqrt(6.0 / (H + NUM_EXPERTS))
        router_w = jax.random.uniform(k_rw, (NUM_EXPERTS, H), minval=-lim, maxval=lim, dtype=jnp.float32)
        router_b = jnp.zeros((NUM_EXPERTS,), dtype=jnp.float32)
        experts_inter = jax.random.normal(k_wi, (NUM_EXPERTS - 1, H, I), dtype=jnp.float32) / math.sqrt(H)
        experts_out = jax.random.normal(k_wo, (NUM_EXPERTS - 1, I, H), dtype=jnp.float32) / math.sqrt(I)
        return {'x': x, 'router_w': router_w, 'router_b': router_b, 'experts_inter': experts_inter, 'experts_out': experts_out}
    _L0_ffn_all = _L0_ffn_setup()
    _L0_ffn_in = {k: v for k, v in _L0_ffn_all.items() if k in ('router_w', 'router_b', 'experts_inter', 'experts_out')}
    del _L0_ffn_all

    def _L1_attn_setup():
        import jax, jax.numpy as jnp
        import numpy as np
        B, T, HS, H, R = (4, 256, 128, 16, 16)
        D = HS // H
        LOGIT_01 = float(np.log(0.1 / 0.9))
        LOGIT_098 = float(np.log(0.98 / 0.02))

        def _rope_cos_sin(seq_len, dim, base=10000.0):
            half = dim // 2
            inv_freq = 1.0 / base ** (jnp.arange(half, dtype=jnp.float32) / half)
            freqs = jnp.arange(seq_len, dtype=jnp.float32)[:, None] * inv_freq[None, :]
            return (jnp.cos(freqs), jnp.sin(freqs))

        def _apply_rope(x, cos, sin):
            c = cos[None, :, None, :]
            s = sin[None, :, None, :]
            x1 = x[..., 0::2]
            x2 = x[..., 1::2]
            r1 = x1 * c - x2 * s
            r2 = x1 * s + x2 * c
            return jnp.stack((r1, r2), axis=-1).reshape(x.shape)
        key = jax.random.key(seed)
        ks = jax.random.split(key, 10)

        def rn(k, shape, s=0.02):
            return jax.random.normal(k, shape, dtype=jnp.float32) * s
        return {'x': jax.random.normal(ks[0], (B, T, HS), dtype=jnp.float32), 'q_w': rn(ks[1], (HS, HS)), 'k_w': rn(ks[2], (HS, HS)), 'v_w': rn(ks[3], (HS, HS)), 'Wq': rn(ks[4], (H, R, D), 0.05), 'Wk': rn(ks[5], (H, R, D), 0.05), 'g_w': rn(ks[6], (H * R, HS)), 'g_b': jnp.full((H * R,), LOGIT_01, dtype=jnp.float32), 'base_decay_logits': jnp.full((H, R), LOGIT_098, dtype=jnp.float32), 'out_w': rn(ks[7], (HS, HS)), 'out_b': jnp.zeros((HS,), dtype=jnp.float32), 'ln_g': jnp.ones((HS,), dtype=jnp.float32), 'ln_b': jnp.zeros((HS,), dtype=jnp.float32)}
    _L1_attn_all = _L1_attn_setup()
    _L1_attn_in = {k: v for k, v in _L1_attn_all.items() if k in ('q_w', 'k_w', 'v_w', 'Wq', 'Wk', 'g_w', 'g_b', 'base_decay_logits', 'out_w', 'out_b', 'ln_g', 'ln_b')}
    del _L1_attn_all

    def _L1_xattn_setup():
        import jax, jax.numpy as jnp
        import numpy as np
        EMBED_DIM = 128
        NUM_HEADS = 16
        HEAD_DIM = EMBED_DIM // NUM_HEADS
        key = jax.random.key(seed)
        ks = jax.random.split(key, 5)
        B, S, E = (2, 256, EMBED_DIM)
        scale_w = 1.0 / np.sqrt(E)
        return {'query': jax.random.normal(ks[0], (B, S, E), dtype=jnp.float32), 'key': jax.random.normal(ks[1], (B, S, E), dtype=jnp.float32), 'value': jax.random.normal(ks[2], (B, S, E), dtype=jnp.float32), 'in_proj_weight': jax.random.normal(ks[3], (3 * E, E), dtype=jnp.float32) * scale_w, 'in_proj_bias': jnp.zeros((3 * E,), dtype=jnp.float32), 'out_proj_weight': jax.random.normal(ks[4], (E, E), dtype=jnp.float32) * scale_w, 'out_proj_bias': jnp.zeros((E,), dtype=jnp.float32)}
    _L1_xattn_all = _L1_xattn_setup()
    _L1_xattn_in = {k: v for k, v in _L1_xattn_all.items() if k in ('in_proj_weight', 'in_proj_bias', 'out_proj_weight', 'out_proj_bias')}
    del _L1_xattn_all

    def _L1_ffn_setup():
        import jax, jax.numpy as jnp
        import numpy as np
        B, S, D_MODEL, D_HIDDEN = (4, 256, 128, 512)

        def act_quant(x):
            scale = 127.0 / jnp.clip(jnp.max(jnp.abs(x), axis=-1, keepdims=True), 1e-05)
            return jnp.clip(jnp.round(x * scale), -128, 127) / scale

        def weight_quant(w):
            scale = 1.0 / jnp.clip(jnp.mean(jnp.abs(w)), 1e-05)
            return jnp.clip(jnp.round(w * scale), -1, 1) / scale

        def bit_linear(x, w):
            xq = x + jax.lax.stop_gradient(act_quant(x) - x)
            wq = w + jax.lax.stop_gradient(weight_quant(w) - w)
            return jnp.einsum('bsd,hd->bsh', xq, wq)

        def depthwise_conv1d(x_bcl, w, b):
            y = jax.lax.conv_general_dilated(x_bcl, w, window_strides=(1,), padding=[(1, 1)], dimension_numbers=('NCH', 'OIH', 'NCH'), feature_group_count=x_bcl.shape[1])
            return y + b[None, :, None]
        key = jax.random.key(seed)
        ks = jax.random.split(key, 5)
        lim1 = 1.0 / np.sqrt(D_MODEL)
        lim2 = 1.0 / np.sqrt(D_HIDDEN)
        limc = 1.0 / np.sqrt(3.0)
        return {'x': jax.random.normal(ks[0], (B, S, D_MODEL), dtype=jnp.float32), 'w1': jax.random.uniform(ks[1], (D_HIDDEN, D_MODEL), jnp.float32, -lim1, lim1), 'conv_w': jax.random.uniform(ks[2], (D_HIDDEN, 1, 3), jnp.float32, -limc, limc), 'conv_b': jax.random.uniform(ks[3], (D_HIDDEN,), jnp.float32, -limc, limc), 'w2': jax.random.uniform(ks[4], (D_MODEL, D_HIDDEN), jnp.float32, -lim2, lim2)}
    _L1_ffn_all = _L1_ffn_setup()
    _L1_ffn_in = {k: v for k, v in _L1_ffn_all.items() if k in ('w1', 'conv_w', 'conv_b', 'w2')}
    del _L1_ffn_all
    return {'x': x, 'ctx_1024': ctx_1024, 'L0_attn_Wq': _L0_attn_in['Wq'], 'L0_attn_bq': _L0_attn_in['bq'], 'L0_attn_Wk': _L0_attn_in['Wk'], 'L0_attn_bk': _L0_attn_in['bk'], 'L0_attn_Wv': _L0_attn_in['Wv'], 'L0_attn_bv': _L0_attn_in['bv'], 'L0_attn_Wo': _L0_attn_in['Wo'], 'L0_attn_bo': _L0_attn_in['bo'], 'L0_attn_rel_table': _L0_attn_in['rel_table'], 'L0_xattn_Wq': _L0_xattn_in['Wq'], 'L0_xattn_Wk': _L0_xattn_in['Wk'], 'L0_xattn_Wv': _L0_xattn_in['Wv'], 'L0_xattn_Wo': _L0_xattn_in['Wo'], 'L0_ffn_router_w': _L0_ffn_in['router_w'], 'L0_ffn_router_b': _L0_ffn_in['router_b'], 'L0_ffn_experts_inter': _L0_ffn_in['experts_inter'], 'L0_ffn_experts_out': _L0_ffn_in['experts_out'], 'L1_attn_q_w': _L1_attn_in['q_w'], 'L1_attn_k_w': _L1_attn_in['k_w'], 'L1_attn_v_w': _L1_attn_in['v_w'], 'L1_attn_Wq': _L1_attn_in['Wq'], 'L1_attn_Wk': _L1_attn_in['Wk'], 'L1_attn_g_w': _L1_attn_in['g_w'], 'L1_attn_g_b': _L1_attn_in['g_b'], 'L1_attn_base_decay_logits': _L1_attn_in['base_decay_logits'], 'L1_attn_out_w': _L1_attn_in['out_w'], 'L1_attn_out_b': _L1_attn_in['out_b'], 'L1_attn_ln_g': _L1_attn_in['ln_g'], 'L1_attn_ln_b': _L1_attn_in['ln_b'], 'L1_xattn_in_proj_weight': _L1_xattn_in['in_proj_weight'], 'L1_xattn_in_proj_bias': _L1_xattn_in['in_proj_bias'], 'L1_xattn_out_proj_weight': _L1_xattn_in['out_proj_weight'], 'L1_xattn_out_proj_bias': _L1_xattn_in['out_proj_bias'], 'L1_ffn_w1': _L1_ffn_in['w1'], 'L1_ffn_conv_w': _L1_ffn_in['conv_w'], 'L1_ffn_conv_b': _L1_ffn_in['conv_b'], 'L1_ffn_w2': _L1_ffn_in['w2']}

def reference(x, ctx_1024, L0_attn_Wq, L0_attn_bq, L0_attn_Wk, L0_attn_bk, L0_attn_Wv, L0_attn_bv, L0_attn_Wo, L0_attn_bo, L0_attn_rel_table, L0_xattn_Wq, L0_xattn_Wk, L0_xattn_Wv, L0_xattn_Wo, L0_ffn_router_w, L0_ffn_router_b, L0_ffn_experts_inter, L0_ffn_experts_out, L1_attn_q_w, L1_attn_k_w, L1_attn_v_w, L1_attn_Wq, L1_attn_Wk, L1_attn_g_w, L1_attn_g_b, L1_attn_base_decay_logits, L1_attn_out_w, L1_attn_out_b, L1_attn_ln_g, L1_attn_ln_b, L1_xattn_in_proj_weight, L1_xattn_in_proj_bias, L1_xattn_out_proj_weight, L1_xattn_out_proj_bias, L1_ffn_w1, L1_ffn_conv_w, L1_ffn_conv_b, L1_ffn_w2):
    import jax
    import jax.numpy as jnp

    def _L0_attn_ref(q, Wq, bq, Wk, bk, Wv, bv, Wo, bo, rel_table):
        import jax, jax.numpy as jnp
        import numpy as np
        EMBED_DIM = 128
        N_HEADS = 16
        HEAD_DIM = EMBED_DIM // N_HEADS
        MAX_REL = 64
        B, S = (4, 128)
        b, s, e = q.shape
        h, d = (N_HEADS, HEAD_DIM)
        Q = (q @ Wq + bq).reshape(b, s, h, d).transpose(0, 2, 1, 3)
        K = (q @ Wk + bk).reshape(b, s, h, d).transpose(0, 2, 1, 3)
        V = (q @ Wv + bv).reshape(b, s, h, d).transpose(0, 2, 1, 3)
        scores = jnp.einsum('bhid,bhjd->bhij', Q, K) / jnp.sqrt(jnp.asarray(d, q.dtype))
        pos = jnp.arange(s)
        rel_idx = jnp.clip(pos[None, :] - pos[:, None] + MAX_REL, 0, 2 * MAX_REL)
        rel_emb = rel_table[rel_idx]
        scores = scores + jnp.einsum('bhid,ijd->bhij', Q, rel_emb)
        attn = jax.nn.softmax(scores, axis=-1)
        ctx = jnp.einsum('bhij,bhjd->bhid', attn, V)
        ctx = ctx.transpose(0, 2, 1, 3).reshape(b, s, e)
        return ctx @ Wo + bo

    def _L0_xattn_ref(x, context, Wq, Wk, Wv, Wo):
        import jax, jax.numpy as jnp
        import numpy as np
        HEADS = 16
        DIM_HEAD = 64
        QUERY_DIM = 128
        INNER = HEADS * DIM_HEAD
        SCALE = DIM_HEAD ** (-0.5)
        B, N, _ = x.shape
        M = context.shape[1]
        q = (x @ Wq).reshape(B, N, HEADS, DIM_HEAD)
        k = (context @ Wk).reshape(B, M, HEADS, DIM_HEAD)
        v = (context @ Wv).reshape(B, M, HEADS, DIM_HEAD)
        sim = jnp.einsum('bihd,bjhd->bhij', q, k) * SCALE
        attn = jax.nn.softmax(sim, axis=-1)
        out = jnp.einsum('bhij,bjhd->bihd', attn, v)
        out = out.reshape(B, N, INNER)
        return out @ Wo

    def _L0_ffn_ref(x, router_w, router_b, experts_inter, experts_out):
        import math
        import jax, jax.numpy as jnp
        import numpy as np
        NUM_EXPERTS = 8
        TOP_K = 2
        CAPACITY_FACTOR = 1.0
        B, S, H, I = (4, 256, 128, 512)
        batch, seq, hidden = x.shape
        n_exp = router_w.shape[0]
        n_tok = batch * seq
        cap = math.ceil(n_tok / n_exp * CAPACITY_FACTOR)
        logits = jnp.einsum('bsh,eh->bse', x, router_w) + router_b
        weights_flat = jax.nn.softmax(logits, axis=-1).reshape(n_tok, n_exp)
        x_flat = x.reshape(n_tok, hidden)
        topk_vals, topk_idx = jax.lax.top_k(weights_flat, TOP_K)
        rows = jnp.arange(n_tok)[:, None]
        topk_flat = jnp.zeros_like(weights_flat).at[rows, topk_idx].set(topk_vals)
        routing_mask = (topk_flat > 0).astype(jnp.int32)
        noop_w = topk_flat[:, -1]
        noop_mask = routing_mask[:, -1].astype(x.dtype)
        expert_w = topk_flat[:, :-1]
        expert_mask = routing_mask[:, :-1]
        sorted_indices = jnp.argsort(-expert_mask, axis=0)[:cap]
        sorted_mask = jnp.take_along_axis(expert_mask, sorted_indices, axis=0)
        used_idx = (sorted_indices * sorted_mask).reshape(-1)
        inputs = x_flat[used_idx] * sorted_mask.reshape(-1).astype(x.dtype)[:, None]
        inputs = inputs.reshape(cap, n_exp - 1, hidden)
        in_w = jnp.take_along_axis(expert_w, sorted_indices, axis=0)
        h = jax.nn.relu(jnp.einsum('ceh,ehi->cei', inputs, experts_inter))
        out = jnp.einsum('cei,eih->ceh', h, experts_out) * in_w[..., None]
        combined = jnp.zeros_like(x_flat).at[used_idx].add(out.reshape(-1, hidden))
        combined = combined + x_flat * (noop_w * noop_mask)[:, None]
        return combined.reshape(batch, seq, hidden)

    def _L1_attn_ref(x, q_w, k_w, v_w, Wq, Wk, g_w, g_b, base_decay_logits, out_w, out_b, ln_g, ln_b):
        import jax, jax.numpy as jnp
        import numpy as np
        B, T, HS, H, R = (4, 256, 128, 16, 16)
        D = HS // H
        LOGIT_01 = float(np.log(0.1 / 0.9))
        LOGIT_098 = float(np.log(0.98 / 0.02))

        def _rope_cos_sin(seq_len, dim, base=10000.0):
            half = dim // 2
            inv_freq = 1.0 / base ** (jnp.arange(half, dtype=jnp.float32) / half)
            freqs = jnp.arange(seq_len, dtype=jnp.float32)[:, None] * inv_freq[None, :]
            return (jnp.cos(freqs), jnp.sin(freqs))

        def _apply_rope(x, cos, sin):
            c = cos[None, :, None, :]
            s = sin[None, :, None, :]
            x1 = x[..., 0::2]
            x2 = x[..., 1::2]
            r1 = x1 * c - x2 * s
            r2 = x1 * s + x2 * c
            return jnp.stack((r1, r2), axis=-1).reshape(x.shape)
        b, t, hs = x.shape
        h, r, d = Wq.shape
        q = (x @ q_w.T).reshape(b, t, h, d)
        k = (x @ k_w.T).reshape(b, t, h, d)
        v = (x @ v_w.T).reshape(b, t, h, d)
        cos, sin = _rope_cos_sin(t, d)
        q = _apply_rope(q, cos, sin)
        k = _apply_rope(k, cos, sin)
        q_r = jnp.einsum('bthd,hrd->bthr', q, Wq)
        k_r = jnp.einsum('bthd,hrd->bthr', k, Wk)
        g = jax.nn.sigmoid((x @ g_w.T + g_b).reshape(b, t, h, r))
        decay = jax.nn.sigmoid(base_decay_logits)[None, :, :, None]
        scale = 1.0 / jnp.sqrt(jnp.asarray(d, dtype=x.dtype))

        def step(M, inp):
            q_t, k_t, v_t, g_t = inp
            M = M * decay + jnp.einsum('bhr,bhd->bhrd', g_t * k_t * scale, v_t)
            y = jnp.einsum('bhr,bhrd->bhd', q_t, M)
            return (M, y)
        xs = (q_r.transpose(1, 0, 2, 3), k_r.transpose(1, 0, 2, 3), v.transpose(1, 0, 2, 3), g.transpose(1, 0, 2, 3))
        M0 = jnp.zeros((b, h, r, d), dtype=x.dtype)
        _, Y = jax.lax.scan(step, M0, xs)
        Y = Y.transpose(1, 0, 2, 3).reshape(b, t, hs)
        out = Y @ out_w.T + out_b
        hres = x + out
        mu = jnp.mean(hres, axis=-1, keepdims=True)
        var = jnp.mean((hres - mu) ** 2, axis=-1, keepdims=True)
        return (hres - mu) / jnp.sqrt(var + 1e-05) * ln_g + ln_b

    def _L1_xattn_ref(query, key, value, in_proj_weight, in_proj_bias, out_proj_weight, out_proj_bias):
        import jax, jax.numpy as jnp
        import numpy as np
        EMBED_DIM = 128
        NUM_HEADS = 16
        HEAD_DIM = EMBED_DIM // NUM_HEADS
        B, Sq, E = query.shape
        Sk = key.shape[1]
        H, D = (NUM_HEADS, HEAD_DIM)
        scale = 1.0 / np.sqrt(D)
        wq, wk, wv = jnp.split(in_proj_weight, 3, axis=0)
        bq, bk, bv = jnp.split(in_proj_bias, 3, axis=0)
        q = jnp.einsum('bse,fe->bsf', query, wq) + bq
        k = jnp.einsum('bse,fe->bsf', key, wk) + bk
        v = jnp.einsum('bse,fe->bsf', value, wv) + bv
        q = q.reshape(B, Sq, H, D).transpose(0, 2, 1, 3)
        k = k.reshape(B, Sk, H, D).transpose(0, 2, 1, 3)
        v = v.reshape(B, Sk, H, D).transpose(0, 2, 1, 3)
        scores = jnp.einsum('bhqd,bhkd->bhqk', q, k) * scale
        attn = jax.nn.softmax(scores, axis=-1)
        out = jnp.einsum('bhqk,bhkd->bhqd', attn, v)
        out = out.transpose(0, 2, 1, 3).reshape(B, Sq, E)
        out = jnp.einsum('bse,fe->bsf', out, out_proj_weight) + out_proj_bias
        return out

    def _L1_ffn_ref(x, w1, conv_w, conv_b, w2):
        import jax, jax.numpy as jnp
        import numpy as np
        B, S, D_MODEL, D_HIDDEN = (4, 256, 128, 512)

        def act_quant(x):
            scale = 127.0 / jnp.clip(jnp.max(jnp.abs(x), axis=-1, keepdims=True), 1e-05)
            return jnp.clip(jnp.round(x * scale), -128, 127) / scale

        def weight_quant(w):
            scale = 1.0 / jnp.clip(jnp.mean(jnp.abs(w)), 1e-05)
            return jnp.clip(jnp.round(w * scale), -1, 1) / scale

        def bit_linear(x, w):
            xq = x + jax.lax.stop_gradient(act_quant(x) - x)
            wq = w + jax.lax.stop_gradient(weight_quant(w) - w)
            return jnp.einsum('bsd,hd->bsh', xq, wq)

        def depthwise_conv1d(x_bcl, w, b):
            y = jax.lax.conv_general_dilated(x_bcl, w, window_strides=(1,), padding=[(1, 1)], dimension_numbers=('NCH', 'OIH', 'NCH'), feature_group_count=x_bcl.shape[1])
            return y + b[None, :, None]
        h = bit_linear(x, w1)
        h = depthwise_conv1d(h.transpose(0, 2, 1), conv_w, conv_b)
        h = h.transpose(0, 2, 1)
        h = jax.nn.silu(h)
        return bit_linear(h, w2)
    x = _layernorm(x + _L0_attn_ref(x, L0_attn_Wq, L0_attn_bq, L0_attn_Wk, L0_attn_bk, L0_attn_Wv, L0_attn_bv, L0_attn_Wo, L0_attn_bo, L0_attn_rel_table), axis=-1)
    x = _layernorm(x + _L0_xattn_ref(x, ctx_1024, L0_xattn_Wq, L0_xattn_Wk, L0_xattn_Wv, L0_xattn_Wo), axis=-1)
    x = _layernorm(x + _L0_ffn_ref(x, L0_ffn_router_w, L0_ffn_router_b, L0_ffn_experts_inter, L0_ffn_experts_out), axis=-1)
    x = _layernorm(x + _L1_attn_ref(x, L1_attn_q_w, L1_attn_k_w, L1_attn_v_w, L1_attn_Wq, L1_attn_Wk, L1_attn_g_w, L1_attn_g_b, L1_attn_base_decay_logits, L1_attn_out_w, L1_attn_out_b, L1_attn_ln_g, L1_attn_ln_b), axis=-1)
    x = _layernorm(x + _L1_xattn_ref(x, ctx_1024, ctx_1024, L1_xattn_in_proj_weight, L1_xattn_in_proj_bias, L1_xattn_out_proj_weight, L1_xattn_out_proj_bias), axis=-1)
    x = _layernorm(x + _L1_ffn_ref(x, L1_ffn_w1, L1_ffn_conv_w, L1_ffn_conv_b, L1_ffn_w2), axis=-1)
    return x

_drawn_inputs = setup_inputs


def setup_inputs(seed=0):
    import zlib

    import numpy as np

    out = dict(_drawn_inputs(seed))
    spreads = {'L0_ffn_router_b': (0.0, 0.1),
     'L1_attn_g_b': (-2.1972246170043945, 0.6),
     'L1_attn_base_decay_logits': (3.891820192337036, 0.6),
     'L1_attn_out_b': (0.0, 2.0),
     'L1_attn_ln_g': (1.0, 0.2),
     'L1_attn_ln_b': (0.0, 0.1),
     'L1_xattn_in_proj_bias': (0.0, 0.1),
     'L1_xattn_out_proj_bias': (0.0, 0.1)}
    factors = {'L0_attn_bq': 4.585,
     'L0_attn_bk': 200.0,
     'L0_attn_rel_table': 4.522,
     'L1_attn_q_w': 8.0,
     'L1_attn_k_w': 8.0,
     'L1_attn_v_w': 8.0,
     'L1_attn_Wq': 8.0,
     'L1_attn_Wk': 8.0,
     'L1_attn_g_w': 8.0,
     'L1_attn_out_w': 8.0}
    for name, (base, spread) in spreads.items():
        noise = np.random.default_rng([zlib.crc32(name.encode()), seed]).standard_normal(out[name].shape)
        drawn = base * np.exp(spread * noise) if base else spread * noise
        out[name] = jnp.asarray(drawn.astype(out[name].dtype))
    for name, factor in factors.items():
        out[name] = (out[name] * factor).astype(out[name].dtype)
    return out
```

```python
from contextlib import ExitStack

import numpy as np

import concourse.bass as bass
from concourse import mybir

F32 = mybir.dt.float32
BF16 = mybir.dt.bfloat16
U32 = mybir.dt.uint32
ALU = mybir.AluOpType
ACT = mybir.ActivationFunctionType
AX = mybir.AxisListType

P = 128
B = 16
NP = B // 2
C = 77
H = 16
DH = P // H
XH = 64
XC = H * XH // P
MAX_REL = 64
M = 2 * P - 1
RROW = H * M
E = 7
HID = 512
HC = HID // P
CAP = B * P // (E + 1)
R = 16
MID = P // 2
EPS = 1e-5
ROUND = 1.5 * 2.0 ** 23
QMAX = 127.0

WEIGHTS = {
    "a0_wq": P, "a0_wk": P, "a0_wv": P, "a0_wo": P, "a0_rel": 4 * P, "a0_rel_last": 4 * H,
    "c0_wq": H * XH, "c0_wk": H * XH, "c0_wv": H * XH, "c0_wo": XC * P,
    "m_router": E + 1, "m_w1": E * HID, "m_w2": E * HC * P,
    "a1_wq": P, "a1_wqs": P, "a1_wk": P, "a1_wks": P, "a1_wv": P, "a1_wg": H * R,
    "a1_rq": 2 * P, "a1_rk": 2 * P, "a1_wo": P,
    "c1_wq": P, "c1_wk": P, "c1_wv": P, "c1_wo": P,
    "f_w1": HID, "f_w2": HC * P,
}
COLUMNS = {"a0_bq": 1, "a0_bk": 1, "c1_bq": 1, "c1_bk": 1, "a1_gb": 2, "a1_decay": 2,
           "f_conv": 3 * HC, "f_convb": HC}
ROWS = {"a0_bv": P, "a0_bo": P, "m_rb": E + 1, "a1_bo": P, "a1_lng": P, "a1_lnb": P,
        "c1_bv": P, "c1_bo": P}
CONSTS = {"ident": P, "tri": P, "causal": P, "cos": P, "sin": P, "time": P,
          "head8": 4, "group32": 4, "head16": 2, "expert": E + 1, "cap": E + 1}


def offsets(sizes):
    at, found = 0, {}
    for name, n in sizes.items():
        found[name] = (at, at + n)
        at += n
    return found, at


W_AT, W_N = offsets(WEIGHTS)
C_AT, C_N = offsets(COLUMNS)
R_AT, R_N = offsets(ROWS)
K_AT, K_N = offsets(CONSTS)


def decoder(nc, x_in, xT_in, cT_in, weights, columns, rows, consts, out, rel_scores):
    with ExitStack() as ctx:
        def sb(name, shape, dt=F32):
            return ctx.enter_context(nc.sbuf_tensor(name, shape, dt))

        def per_seq(name, shape, dt=F32):
            return [sb(f"{name}{s}", shape, dt) for s in range(2)]

        def sem(name):
            return ctx.enter_context(nc.semaphore(name))

        def sems(name, n):
            return [sem(f"{name}{i}") for i in range(n)]

        bank = [[ctx.enter_context(nc.psum_tensor(f"bank{s}{i}", [P, 512], F32)) for i in range(4)]
                for s in range(2)]

        w_sb = sb("w_sb", [P, W_N])
        col_sb = sb("col_sb", [P, C_N])
        row_sb = sb("row_sb", [P, R_N])
        k_sb = sb("k_sb", [P, K_N])
        ident_bf = sb("ident_bf", [P, P], BF16)
        ones = sb("ones", [P, P])
        eps = sb("eps", [P, 1])
        bqm0 = sb("bqm0", [P, 4])
        bqm1 = sb("bqm1", [P, 4])
        head8s = sb("head8s", [P, 4])
        ngb = sb("ngb", [P, 2])
        loglam = sb("loglam", [P, 2])
        nloglam = sb("nloglam", [P, 2])
        dq = sb("dq", [P, 2, P])
        dqm = sb("dqm", [P, 2, 2, P])
        dk = sb("dk", [P, 2, P])
        w1q = sb("w1q", [P, HID], BF16)
        w2q = sb("w2q", [P, HC * P], BF16)
        wabs = sb("wabs", [P, 2])
        wmean = sb("wmean", [P, 2])
        wscale = sb("wscale", [P, 2])
        wtmp = sb("wtmp", [P, HID])
        routed = sb("routed", [P, E + 1])

        def w(name, a=0, b=None):
            lo, hi = W_AT[name]
            return w_sb[:, lo + a:(hi if b is None else lo + b)]

        def col(name, i=0):
            return col_sb[:, C_AT[name][0] + i:C_AT[name][0] + i + 1]

        def row(name):
            return row_sb[:, R_AT[name][0]:R_AT[name][1]]

        def const(name, a=0, b=None):
            lo, hi = K_AT[name]
            return k_sb[:, lo + a:(hi if b is None else lo + b)]

        ident = const("ident")

        x_ld = per_seq("x_ld", [P, P])
        xT_ld = per_seq("xT_ld", [P, P])
        cT = per_seq("cT", [P, C])
        rel = per_seq("rel", [P, H, P])
        big = per_seq("big", [P, 2 * H * P])
        qm = per_seq("qm", [P, 4, P])
        kbd = per_seq("kbd", [P, 4, P])
        v9 = per_seq("v9", [P, H, DH + 1])
        k0bd = per_seq("k0bd", [P, XC, 2, C])
        v65 = per_seq("v65", [C, H, XH + 1])
        k1bd = per_seq("k1bd", [P, 4, C])
        c9 = per_seq("c9", [C, H, DH + 1])
        mx = per_seq("mx", [P, H])
        rsum = per_seq("rsum", [P, H])
        q0 = per_seq("q0", [P, XC, P])
        o_sb = per_seq("o_sb", [P, XC, P])
        oT = per_seq("oT", [P, XC, P])
        xb = per_seq("xb", [P, P])
        xb2 = per_seq("xb2", [P, P])
        y = per_seq("y", [P, P])
        y2 = per_seq("y2", [P, P])
        x = per_seq("x", [P, P])
        out_sb = per_seq("out_sb", [P, P])
        xT = per_seq("xT", [P, P])
        stats = per_seq("stats", [P, 6])
        mv = per_seq("mv", [P, 2])
        lnv = per_seq("lnv", [P, 1])
        rstd = per_seq("rstd", [P, 1])
        lg = per_seq("lg", [P, 8])
        top = per_seq("top", [P, 8])
        nmax = per_seq("nmax", [P, 1])
        esum = per_seq("esum", [P, 1])
        wts = per_seq("wts", [P, 8])
        topi = per_seq("topi", [P, 8], U32)
        topf = per_seq("topf", [P, 2])
        sel = per_seq("sel", [P, 8])
        sel2 = per_seq("sel2", [P, 8])
        picked = per_seq("picked", [P, 8])
        keep = per_seq("keep", [P, 8])
        wpass = per_seq("wpass", [P, 1])
        hid = [per_seq("hid0", [P, HID]),
               [oT[s][:, 4:8, :].rearrange("p c i -> p (c i)") for s in range(2)]]
        scol = per_seq("scol", [P, 8])
        xq = per_seq("xq", [P, P], BF16)
        xqT = per_seq("xqT", [P, P], BF16)
        diag = per_seq("diag", [P, P])
        scbc = per_seq("scbc", [P, P])
        hp = per_seq("hp", [P, HC, P + 2])
        hq = per_seq("hq", [P, HID], BF16)
        hqT = per_seq("hqT", [P, HID], BF16)

        sc = [big[s][:, 0:H * P].rearrange("p (h j) -> p h j", h=H) for s in range(2)]
        scx = [big[s][:, 0:H * C].rearrange("p (h j) -> p h j", h=H) for s in range(2)]
        pT = [big[s][:, H * P:2 * H * P].rearrange("p (h j) -> p h j", h=H) for s in range(2)]
        rext = [big[s][:, 0:RROW].rearrange("p (h m) -> p h m", h=H) for s in range(2)]
        t1 = [q0[s][:, 0:2, :] for s in range(2)]
        t2 = [q0[s][:, 2:4, :] for s in range(2)]
        qk = [q0[s][:, 4:6, :] for s in range(2)]
        eg = [q0[s][:, 6:8, :] for s in range(2)]
        qd = [kbd[s].rearrange("p (c a) t -> p c a t", c=2) for s in range(2)]
        kdm = [o_sb[s][:, :, :].rearrange("p (g c) t -> p g c t", g=4) for s in range(2)]
        vr = [diag[s] for s in range(2)]

        ld_w, ld_rel_x = sem("ld_w"), sems("ld_rel_x", 2)
        ld_x, ld_xT, ld_c, ld_rel = sems("ld_x", 2), sems("ld_xT", 2), sems("ld_c", 2), sems("ld_rel", 2)
        st_rel, st_out = sems("st_rel", 2), sems("st_out", 2)
        pre_pool, pre_dve, pre_act, pre_pe = sem("pre_pool"), sem("pre_dve"), sem("pre_act"), sem("pre_pe")
        r_q, r_qm, r_s, r_mid, r_last, r_left, r_right = (sem(n) for n in (
            "r_q", "r_qm", "r_s", "r_mid", "r_last", "r_left", "r_right"))
        x_kv0, x_k0, x_v0, x_kv1, x_kv1_ready = (sem(n) for n in (
            "x_kv0", "x_k0", "x_v0", "x_kv1", "x_kv1_ready"))
        a_qkv, a_qm, a_kv = sem("a_qkv"), sem("a_qm"), sem("a_kv")
        scores = {k: sem(f"{k}_scores") for k in "abe"}
        shifted = {k: sem(f"{k}_shifted") for k in "abe"}
        probs = {k: sem(f"{k}_probs") for k in "abe"}
        probsT = {k: sem(f"{k}_probsT") for k in "abe"}
        probsT_even = {k: sem(f"{k}_probsT_even") for k in "abe"}
        probsT_odd = {k: sem(f"{k}_probsT_odd") for k in "abe"}
        pv = {k: sem(f"{k}_pv") for k in "abe"}
        o_ready = {k: sem(f"{k}_o_ready") for k in "abe"}
        oT_ps = {k: sem(f"{k}_oT_ps") for k in "abed"}
        oT_ready = {k: sem(f"{k}_oT_ready") for k in "abed"}
        oT_ready2 = sem("b_oT_ready2")
        proj = {k: sem(f"{k}_proj") for k in "abdef"}
        b_q, b_q_lo, b_q_hi = sem("b_q"), sem("b_q_lo"), sem("b_q_hi")
        e_q, e_qm = sem("e_q"), sem("e_qm")
        var = {k: sem(f"{k}_var") for k in "abcdDef"}
        inv = {k: sem(f"{k}_inv") for k in "abcdDef"}
        normed = {k: sem(f"{k}_normed") for k in "abcDef"}
        xT_ps = {k: sem(f"{k}_xT_ps") for k in "abcD"}
        xT_ready = {k: sem(f"{k}_xT_ready") for k in "abcD"}
        xb_ready = {k: sem(f"{k}_xb") for k in "ade"}
        c_logits, c_shift, c_exp, c_pick, c_rank = (sem(n) for n in (
            "c_logits", "c_shift", "c_exp", "c_pick", "c_rank"))
        c_keep, c_up, c_hid, c_down = sem("c_keep"), sems("c_up", E), sems("c_hid", E), sems("c_down", 2)
        d_qk, d_gv, d_gate, d_v, d_rope, d_rank, d_qkd = (sem(n) for n in (
            "d_qk", "d_gv", "d_gate", "d_v", "d_rope", "d_rank", "d_qkd"))
        d_att, d_masked, d_y, d_ysb = sem("d_att"), sem("d_masked"), sem("d_y"), sem("d_ysb")
        (f_xq, f_xqT, f_xqT_sb, f_sc_sb, f_h, f_hp, f_conv0, f_conv, f_exp, f_silu, f_hT, f_hq,
         f_hqT, f_hqT_sb) = (sem(n) for n in (
             "f_xq", "f_xqT", "f_xqT_sb", "f_sc_sb", "f_h", "f_hp", "f_conv0", "f_conv", "f_exp",
             "f_silu", "f_hT", "f_hq", "f_hqT", "f_hqT_sb"))
        dve_step, act_step = sem("dve_step"), sem("act_step")

        block = ctx.enter_context(nc.Block())

        @block.sync
        def _(sp):
            sp.dma_start(k_sb[:], consts).then_inc(ld_w, 16)
            sp.dma_start(col_sb[:], columns).then_inc(ld_w, 16)
            sp.dma_start(row_sb[:], rows.partition_broadcast(P)).then_inc(ld_w, 16)
            sp.dma_start(w_sb[:], weights).then_inc(ld_w, 16)
            with sp.Fori(0, NP) as it:
                before, after = sp.snap(it * 2), sp.snap(it * 2 + 2)
                for s in range(2):
                    sp.wait_ge(r_q, before)
                    sp.dma_start(xT_ld[s][:], xT_in[it, s]).then_inc(ld_rel_x[s], 16)
                sp.wait_ge(r_left, after)
                sp.wait_ge(r_right, after)
                for s in range(2):
                    sp.dma_start(rel_scores[it, s].rearrange("(i c) -> i c", c=RROW),
                                 big[s][:, 0:RROW]).then_inc(st_rel[s], 16)
            for s in range(2):
                sp.wait_ge(st_rel[s], 16 * NP)
            with sp.Fori(0, NP) as it:
                before, shifted_before = sp.snap(it * 2), sp.snap(it * 8)
                for s in range(2):
                    sp.wait_ge(x_kv1, before)
                    sp.dma_start(cT[s][:], cT_in[it, s]).then_inc(ld_c[s], 16)
                    sp.wait_ge(a_qkv, before)
                    sp.dma_start(xT_ld[s][:], xT_in[it, s]).then_inc(ld_xT[s], 16)
                    sp.wait_ge(xb_ready["a"], before)
                    sp.dma_start(x_ld[s][:], x_in[it, s]).then_inc(ld_x[s], 16)
                    sp.wait_ge(shifted["a"], shifted_before)
                    skewed = rel_scores[it, s, P - 1:P - 1 + P * (RROW - 1)].rearrange(
                        "(i c) -> i c", c=RROW - 1)
                    sp.dma_start(rel[s][:, 0:H - 1, :], skewed[:, 0:(H - 1) * M].rearrange(
                        "i (h m) -> i h m", m=M)[:, :, 0:P]).then_inc(ld_rel[s], 16)
                    sp.dma_start(rel[s][:, H - 1, :], skewed[:, (H - 1) * M:(H - 1) * M + P]
                                 ).then_inc(ld_rel[s], 16)

        @block.gpsimd
        def _(pool):
            nc.gpsimd.memset(ones[:], 1.0).then_inc(pre_pool, 1)
            nc.gpsimd.memset(eps[:], EPS).then_inc(pre_pool, 1)
            nc.gpsimd.memset(routed[:], 0.0).then_inc(pre_pool, 1)
            for s in range(2):
                nc.gpsimd.memset(v9[s][:], 1.0).then_inc(pre_pool, 1)
                nc.gpsimd.memset(c9[s][:], 1.0).then_inc(pre_pool, 1)
                nc.gpsimd.memset(v65[s][:], 1.0).then_inc(pre_pool, 1)
                nc.gpsimd.memset(k0bd[s][:], 0.0).then_inc(pre_pool, 1)
                nc.gpsimd.memset(hp[s][:], 0.0).then_inc(pre_pool, 1)
            pool.wait_ge(pre_pool, 1)
            with pool.Fori(0, NP) as it:
                n = [pool.snap(it * 2 + 1), pool.snap(it * 2 + 2)]
                for s in range(2):
                    pool.wait_ge(r_mid, n[s])
                    lo = rext[s][:, :, MAX_REL - 1:MAX_REL].broadcast_to([P, H, MAX_REL - 1])
                    nc.gpsimd.tensor_tensor(rext[s][:, :, 0:MAX_REL - 1], lo, ones[:, 0:1].unsqueeze(2).broadcast_to(
                        [P, H, MAX_REL - 1]), ALU.mult).then_inc(r_left, 1)
            pool.wait_ge(ld_w, 64)
            with pool.Fori(0, NP) as it:
                n = [pool.snap(it * 2 + 1), pool.snap(it * 2 + 2)]
                before = pool.snap(it * 2)
                loaded = pool.snap(it * 16 + 16)
                for s in range(2):
                    pool.wait_ge(ld_x[s], loaded)
                    pool.wait_ge(var["e"], before)
                    nc.gpsimd.tensor_tensor(xb[s][:], x_ld[s][:], row("a0_bo"), ALU.add
                                            ).then_inc(xb_ready["a"], 1)
                for s in range(2):
                    pool.wait_ge(normed["c"], n[s])
                    nc.gpsimd.tensor_tensor(xb[s][:], x[s][:], row("a1_bo"), ALU.add
                                            ).then_inc(xb_ready["d"], 1)
                    nc.gpsimd.tensor_tensor(xb2[s][:], x[s][:], row("a1_lnb"), ALU.add
                                            ).then_inc(xb_ready["d"], 1)
                for s in range(2):
                    pool.wait_ge(normed["D"], n[s])
                    nc.gpsimd.tensor_tensor(xb[s][:], x[s][:], row("c1_bo"), ALU.add
                                            ).then_inc(xb_ready["e"], 1)
                for s in range(2):
                    pool.wait_ge(normed["f"], n[s])
                    nc.gpsimd.dma_start(out[it, s], out_sb[s][:]).then_inc(st_out[s], 16)
            for s in range(2):
                pool.wait_ge(st_out[s], 16 * NP)

        @block.tensor
        def _(pe):
            def mm(out_, lhsT, rhs, start=True, stop=True):
                return pe.matmul(out_, lhsT, rhs, start=start, stop=stop)

            pe.wait_ge(pre_pool, 1)
            pe.wait_ge(pre_dve, 1)
            mm(bank[0][0][:, 0:2], ones[:], wabs[:]).then_inc(pre_pe, 1)
            pe.wait_ge(pre_dve, 2)

            with pe.Fori(0, NP) as it:
                n = [pe.snap(it * 2 + 1), pe.snap(it * 2 + 2)]
                before = pe.snap(it * 2)
                loaded = pe.snap(it * 16 + 16)
                for s in range(2):
                    pe.wait_ge(ld_rel_x[s], loaded)
                    pe.wait_ge(r_right, before)
                    mm(bank[s][0][:, 0:P], w("a0_wq"), xT_ld[s][:]).then_inc(r_q, 1)
                for s in range(2):
                    pe.wait_ge(r_qm, n[s])
                    for g in range(4):
                        last = mm(bank[s][g][:], qm[s][:, g, :], w("a0_rel"))
                    last.then_inc(r_s, 1)
                for s in range(2):
                    pe.wait_ge(r_mid, n[s])
                    for g in range(4):
                        last = mm(bank[s][0][:, 0:H], qm[s][:, g, :], w("a0_rel_last", g * H, (g + 1) * H),
                                  start=(g == 0), stop=(g == 3))
                    last.then_inc(r_last, 1)

            def step8(g, s):
                return eights[2 * g + s]

            def step4(i, s):
                return fours[s]

            def transpose_x(k, n, b):
                for s in range(2):
                    pe.wait_ge(normed[k], n[s])
                    pe.transpose(bank[s][b][:, 0:P], x[s][:], ident).then_inc(xT_ps[k], 1)

            def softmax_products(k, n, nk, v, width, per_bank):
                for g in range(4):
                    for s in range(2):
                        pe.wait_ge(probs[k], step8(g, s))
                        src = sc[s] if nk == P else scx[s]
                        for a in range(4):
                            last = pe.transpose(bank[s][g][0:nk, a * P:(a + 1) * P],
                                                src[:, 4 * g + a, :], ident)
                        last.then_inc(probsT[k], 1)
                for s in range(2):
                    pe.wait_ge(probsT_even[k], step4(1, s))
                    pe.wait_ge(probsT_odd[k], step4(1, s))
                    for h in range(H):
                        at = (h % per_bank) * width
                        last = mm(bank[s][h // per_bank][:, at:at + width], pT[s][0:nk, h, :],
                                  v[s][0:nk, h, :])
                    last.then_inc(pv[k], 1)

            def project(k, n, b_T, b_out, weight):
                for s in range(2):
                    pe.wait_ge(o_ready[k], n[s])
                    pe.transpose(bank[s][b_T][:, 0:P], o_sb[s][:, 0, :], ident).then_inc(oT_ps[k], 1)
                for s in range(2):
                    pe.wait_ge(oT_ready[k], n[s])
                    mm(bank[s][b_out][:, 0:P], oT[s][:, 0, :], weight).then_inc(proj[k], 1)

            with pe.Fori(0, NP) as it:
                n = [pe.snap(it * 2 + 1), pe.snap(it * 2 + 2)]
                before = pe.snap(it * 2)
                loaded = pe.snap(it * 16 + 16)
                eights = [pe.snap(it * 8 + i + 1) for i in range(8)]
                fours = [pe.snap(it * 4 + i + 3) for i in range(2)]
                for s in range(2):
                    pe.wait_ge(ld_c[s], loaded)
                    pe.wait_ge(var["f"], before)
                    for c in range(XC):
                        mm(bank[s][c // 4][:, (c % 4) * C:(c % 4 + 1) * C],
                           w("c0_wk", c * P, (c + 1) * P), cT[s][:])
                    for c in range(2):
                        last = mm(bank[s][2 + c][0:C, :], cT[s][:], w("c0_wv", c * 512, (c + 1) * 512))
                    last.then_inc(x_kv0, 1)
                for s in range(2):
                    pe.wait_ge(x_k0, n[s])
                    mm(bank[s][0][:, 0:C], w("c1_wk"), cT[s][:])
                    mm(bank[s][0][0:C, P:2 * P], cT[s][:], w("c1_wv")).then_inc(x_kv1, 1)
                for s in range(2):
                    pe.wait_ge(ld_xT[s], loaded)
                    pe.wait_ge(x_v0, n[s])
                    pe.wait_ge(x_kv1_ready, n[s])
                    mm(bank[s][0][:, 0:P], w("a0_wq"), xT_ld[s][:])
                    mm(bank[s][1][:, 0:P], w("a0_wk"), xT_ld[s][:])
                    mm(bank[s][2][:, 0:P], xT_ld[s][:], w("a0_wv")).then_inc(a_qkv, 1)
                for g in range(4):
                    for s in range(2):
                        if g == 0:
                            pe.wait_ge(a_qm, n[s])
                            pe.wait_ge(a_kv, n[s])
                        mm(bank[s][g][:], qm[s][:, g, :], kbd[s][:, :, :]).then_inc(scores["a"], 1)
                softmax_products("a", n, P, v9, DH + 1, H)
                project("a", n, 1, 2, w("a0_wo"))
                transpose_x("a", n, 3)
                for s in range(2):
                    pe.wait_ge(xT_ready["a"], n[s])
                    for c in range(XC):
                        last = mm(bank[s][c // 4][:, (c % 4) * P:(c % 4 + 1) * P],
                                  w("c0_wq", c * P, (c + 1) * P), xT[s][:])
                    last.then_inc(b_q, 1)
                for g in range(4):
                    for s in range(2):
                        if g == 0:
                            pe.wait_ge(b_q_lo, n[s])
                            pe.wait_ge(b_q_hi, n[s])
                        for c in (2 * g, 2 * g + 1):
                            last = mm(bank[s][g][:, (c % 2) * 2 * C:(c % 2 + 1) * 2 * C],
                                      q0[s][:, c, :], k0bd[s][:, c, :, :])
                        last.then_inc(scores["b"], 1)
                softmax_products("b", n, C, v65, XH + 1, 4)
                for s in range(2):
                    pe.wait_ge(o_ready["b"], n[s])
                    for c in range(XC):
                        last = pe.transpose(bank[s][c // 4][:, (c % 4) * P:(c % 4 + 1) * P],
                                            o_sb[s][:, c, :], ident)
                    last.then_inc(oT_ps["b"], 1)
                for s in range(2):
                    pe.wait_ge(oT_ready["b"], n[s])
                    pe.wait_ge(oT_ready2, n[s])
                    for c in range(XC):
                        last = mm(bank[s][2][:, 0:P], oT[s][:, c, :], w("c0_wo", c * P, (c + 1) * P),
                                  start=(c == 0), stop=(c == XC - 1))
                    last.then_inc(proj["b"], 1)
                transpose_x("b", n, 3)
                for s in range(2):
                    pe.wait_ge(xT_ready["b"], n[s])
                    mm(bank[s][3][:, 0:E + 1], xT[s][:], w("m_router")).then_inc(c_logits, 1)

                def up(e, s):
                    for c in range(HC):
                        last = mm(bank[s][e % 2][:, c * P:(c + 1) * P],
                                  w("m_w1", e * HID + c * P, e * HID + (c + 1) * P), xT[s][:])
                    last.then_inc(c_up[e], 1)

                for s in range(2):
                    up(0, s)
                for e in range(E):
                    if e + 1 < E:
                        for s in range(2):
                            up(e + 1, s)
                    if e == 2:
                        for s in range(2):
                            pe.wait_ge(c_pick, n[s])
                            mm(bank[s][3][:, 0:E + 1], const("tri"), picked[s][:], stop=False)
                            if s == 1:
                                mm(bank[s][3][:, 0:E + 1], ones[:], picked[0][:], start=False, stop=False)
                            mm(bank[s][3][:, 0:E + 1], ones[:], routed[:], start=False
                               ).then_inc(c_rank, 1)
                    for s in range(2):
                        pe.wait_ge(c_hid[e], n[s])
                        if e == 4:
                            pe.wait_ge(c_keep, n[s])
                        for c in range(HC):
                            last = mm(bank[s][2 + e // 4][:, (e % 4) * P:(e % 4 + 1) * P],
                                      hid[e % 2][s][:, c * P:(c + 1) * P],
                                      w("m_w2", (e * HC + c) * P, (e * HC + c + 1) * P),
                                      start=(c == 0), stop=(c == HC - 1))
                        if e in (3, E - 1):
                            last.then_inc(c_down[e // 4], 1)
                transpose_x("c", n, 0)
                for s in range(2):
                    pe.wait_ge(xT_ready["c"], n[s])
                    mm(bank[s][1][:, 0:P], w("a1_wg", 0, P), xT[s][:])
                    mm(bank[s][1][:, P:2 * P], w("a1_wg", P, 2 * P), xT[s][:])
                    mm(bank[s][1][:, 2 * P:3 * P], xT[s][:], w("a1_wv")).then_inc(d_gv, 1)
                    for i, name in enumerate(("a1_wq", "a1_wk", "a1_wqs", "a1_wks")):
                        last = mm(bank[s][0][:, i * P:(i + 1) * P], w(name), xT[s][:])
                    last.then_inc(d_qk, 1)
                for s in range(2):
                    pe.wait_ge(d_rope, n[s])
                    for i, name in enumerate(("a1_rq", "a1_rk")):
                        for c in range(2):
                            last = mm(bank[s][2][:, (2 * i + c) * P:(2 * i + c + 1) * P],
                                      w(name, c * P, (c + 1) * P), qk[s][:, i, :])
                    last.then_inc(d_rank, 1)
                for g in range(4):
                    for s in range(2):
                        if g == 0:
                            pe.wait_ge(d_qkd, n[s])
                            pe.wait_ge(d_v, n[s])
                        for c in range(2):
                            last = mm(bank[s][g][:, c * 2 * P:(c + 1) * 2 * P], kdm[s][:, g, c, :],
                                      qd[s][:, c, :, :])
                        last.then_inc(d_att, 1)
                for s in range(2):
                    pe.wait_ge(d_masked, step8(3, s))
                    for h in range(H):
                        c, g, a = h // 8, h % 8 // 2, h % 2
                        last = mm(bank[s][0][:, h * DH:(h + 1) * DH], sc[s][:, 4 * g + 2 * c + a, :],
                                  vr[s][:, h * DH:(h + 1) * DH])
                    last.then_inc(d_y, 1)
                for s in range(2):
                    pe.wait_ge(d_ysb, n[s])
                    pe.transpose(bank[s][1][:, 0:P], o_sb[s][:, 0, :], ident).then_inc(oT_ps["d"], 1)
                for s in range(2):
                    pe.wait_ge(oT_ready["d"], n[s])
                    mm(bank[s][2][:, 0:P], oT[s][:, 0, :], w("a1_wo")).then_inc(proj["d"], 1)
                transpose_x("D", n, 3)
                for s in range(2):
                    pe.wait_ge(xT_ready["D"], n[s])
                    mm(bank[s][0][:, 0:P], w("c1_wq"), xT[s][:]).then_inc(e_q, 1)
                for g in range(4):
                    for s in range(2):
                        if g == 0:
                            pe.wait_ge(e_qm, n[s])
                        mm(bank[s][g][:, 0:4 * C], qm[s][:, g, :], k1bd[s][:, :, :]
                           ).then_inc(scores["e"], 1)
                softmax_products("e", n, C, c9, DH + 1, H)
                project("e", n, 1, 2, w("c1_wo"))
                for s in range(2):
                    pe.wait_ge(f_xq, n[s])
                    mm(bank[s][1][:, 0:P], ones[:], diag[s][:])
                    pe.transpose(bank[s][0][:].bitcast(BF16)[:, 0:P], xq[s][:], ident_bf[:]
                                 ).then_inc(f_xqT, 1)
                for s in range(2):
                    pe.wait_ge(f_xqT_sb, n[s])
                    for c in range(HC):
                        last = mm(bank[s][2][:, c * P:(c + 1) * P], w1q[:, c * P:(c + 1) * P], xqT[s][:])
                    last.then_inc(f_h, 1)
                for s in range(2):
                    pe.wait_ge(f_silu, n[s])
                    for c in range(HC):
                        last = pe.transpose(bank[s][3][:, c * P:(c + 1) * P],
                                            hid[0][s][:, c * P:(c + 1) * P], ident)
                    last.then_inc(f_hT, 1)
                for s in range(2):
                    pe.wait_ge(f_hq, n[s])
                    for c in range(HC):
                        last = pe.transpose(bank[s][0][:].bitcast(BF16)[:, c * P:(c + 1) * P],
                                            hq[s][:, c * P:(c + 1) * P], ident_bf[:])
                    last.then_inc(f_hqT, 1)
                for s in range(2):
                    pe.wait_ge(f_hqT_sb, n[s])
                    for c in range(HC):
                        last = mm(bank[s][1][:, 0:P], hqT[s][:, c * P:(c + 1) * P],
                                  w2q[:, c * P:(c + 1) * P], start=(c == 0), stop=(c == HC - 1))
                    last.then_inc(proj["f"], 1)

        @block.scalar
        def _(act):
            act.preload_act_table_set("natural_log_exp_and_others")
            steps = [0]

            def step(ins):
                steps[0] += 1
                ins.then_inc(act_step, 1)
                act.wait_ge(act_step, steps[0])

            act.wait_ge(ld_w, 64)
            act.wait_ge(pre_dve, 3)
            dlo = C_AT["a1_decay"][0]
            step(nc.scalar.activation(loglam[:], col_sb[:, dlo:dlo + 2], ACT.Exp, scale=-1.0))
            step(nc.scalar.activation(nloglam[:], loglam[:], ACT.Ln, bias=1.0))
            step(nc.scalar.activation(loglam[:], nloglam[:], ACT.Copy, scale=-1.0))
            for c in range(2):
                nc.scalar.activation(dq[:, c, :], const("time"), ACT.Exp, scale=loglam[:, c:c + 1])
                last = nc.scalar.activation(dk[:, c, :], const("time"), ACT.Exp,
                                            scale=nloglam[:, c:c + 1])
            last.then_inc(pre_act, 1)

            def queries(s, q, ready, biases):
                for g in range(4):
                    last = nc.scalar.activation(qm[s][:, g, :], q, ACT.Identity,
                                                bias=biases[:, g:g + 1], scale=const("group32", g, g + 1))
                last.then_inc(ready, 1)

            with act.Fori(0, NP) as it:
                n = [act.snap(it * 2 + 1), act.snap(it * 2 + 2)]
                stored = act.snap(it * 16)
                for s in range(2):
                    act.wait_ge(r_q, n[s])
                    queries(s, bank[s][0][:, 0:P], r_qm, bqm0)
                for s in range(2):
                    act.wait_ge(r_s, n[s])
                    act.wait_ge(st_rel[s], stored)
                    for g in range(4):
                        last = nc.scalar.activation(
                            rext[s][:, 4 * g:4 * g + 4, MAX_REL - 1:MAX_REL - 1 + P],
                            bank[s][g][:].rearrange("p (a r) -> p a r", a=4), ACT.Copy)
                    last.then_inc(r_mid, 1)

            def exps(k, n, scale):
                for g in range(4):
                    for s in range(2):
                        act.wait_ge(shifted[k], eights[2 * g + s])
                        src = (sc if k == "a" else scx)[s][:, 4 * g:4 * g + 4, :]
                        nc.scalar.activation(src, src, ACT.Exp, scale=scale).then_inc(probs[k], 1)

            def copy_probsT(k, n, nk):
                for g in (0, 2):
                    for s in range(2):
                        act.wait_ge(probsT[k], eights[2 * g + s])
                        nc.scalar.activation(pT[s][0:nk, 4 * g:4 * g + 4, :], bank[s][g][0:nk, :].rearrange(
                            "p (a i) -> p a i", a=4), ACT.Copy).then_inc(probsT_even[k], 1)

            def copy_T(ps, n, dst, b, ready):
                for s in range(2):
                    act.wait_ge(ps, n[s])
                    nc.scalar.activation(dst(s), bank[s][b][:, 0:P], ACT.Copy).then_inc(ready, 1)

            def deviations(k, n):
                for s in range(2):
                    act.wait_ge(var[k], n[s])
                    step(nc.scalar.activation(lnv[s][:], mv[s][:, 1:2], ACT.Ln, bias=eps[:]))
                    nc.scalar.activation(rstd[s][:], lnv[s][:], ACT.Exp, scale=-0.5).then_inc(inv[k], 1)

            act.wait_ge(pre_pool, N_POOL)
            with act.Fori(0, NP) as it:
                n = [act.snap(it * 2 + 1), act.snap(it * 2 + 2)]
                eights = [act.snap(it * 8 + i + 1) for i in range(8)]
                act.sem_clear(act_step)
                steps[0] = 0
                for s in range(2):
                    act.wait_ge(x_kv0, n[s])
                    for half in range(2):
                        rows_ = slice(half * XH, half * XH + XH)
                        for b in range(2):
                            last = nc.scalar.activation(
                                k0bd[s][rows_, 4 * b:4 * b + 4, half, :],
                                bank[s][b][rows_, 0:4 * C].rearrange("p (c j) -> p c j", c=4), ACT.Copy)
                    last.then_inc(x_k0, 1)
                for s in range(2):
                    act.wait_ge(a_qkv, n[s])
                    queries(s, bank[s][0][:, 0:P], a_qm, bqm0)
                exps("a", n, 1.0)
                copy_probsT("a", n, P)
                copy_T(oT_ps["a"], n, lambda s: oT[s][:, 0, :], 1, oT_ready["a"])
                deviations("a", n)
                copy_T(xT_ps["a"], n, lambda s: xT[s][:], 3, xT_ready["a"])
                for s in range(2):
                    act.wait_ge(b_q, n[s])
                    nc.scalar.activation(q0[s][:, 0:4, :], bank[s][0][:].rearrange("p (c i) -> p c i", c=4),
                                         ACT.Copy).then_inc(b_q_lo, 1)
                exps("b", n, XH ** -0.5)
                copy_probsT("b", n, C)
                for s in range(2):
                    act.wait_ge(oT_ps["b"], n[s])
                    nc.scalar.activation(oT[s][:, 0:4, :], bank[s][0][:].rearrange("p (c i) -> p c i", c=4),
                                         ACT.Copy).then_inc(oT_ready["b"], 1)
                deviations("b", n)
                copy_T(xT_ps["b"], n, lambda s: xT[s][:], 3, xT_ready["b"])
                for e in range(0, E, 2):
                    for s in range(2):
                        act.wait_ge(c_up[e], n[s])
                        nc.scalar.activation(hid[0][s][:], bank[s][0][:], ACT.Relu).then_inc(c_hid[e], 1)
                    if e == 0:
                        for s in range(2):
                            act.wait_ge(c_shift, n[s])
                            nc.scalar.activation(lg[s][:], lg[s][:], ACT.Exp, bias=nmax[s][:],
                                                 accum_out=esum[s][:]).then_inc(c_exp, 1)
                deviations("c", n)
                copy_T(xT_ps["c"], n, lambda s: xT[s][:], 0, xT_ready["c"])
                for s in range(2):
                    act.wait_ge(d_gv, n[s])
                    for c in range(2):
                        last = nc.scalar.activation(eg[s][:, c, :], bank[s][1][:, c * P:(c + 1) * P], ACT.Exp,
                                                    bias=ngb[:, c:c + 1], scale=-1.0)
                    last.then_inc(d_gate, 1)
                    nc.scalar.activation(vr[s][:], bank[s][1][:, 2 * P:3 * P], ACT.Copy).then_inc(d_v, 1)
                copy_T(d_y, n, lambda s: o_sb[s][:, 0, :], 0, d_ysb)
                copy_T(oT_ps["d"], n, lambda s: oT[s][:, 0, :], 1, oT_ready["d"])
                deviations("d", n)
                deviations("D", n)
                copy_T(xT_ps["D"], n, lambda s: xT[s][:], 3, xT_ready["D"])
                for s in range(2):
                    act.wait_ge(e_q, n[s])
                    queries(s, bank[s][0][:, 0:P], e_qm, bqm1)
                exps("e", n, 1.0)
                copy_probsT("e", n, C)
                copy_T(oT_ps["e"], n, lambda s: oT[s][:, 0, :], 1, oT_ready["e"])
                deviations("e", n)
                for s in range(2):
                    act.wait_ge(f_xqT, n[s])
                    nc.scalar.activation(scbc[s][:], bank[s][1][:, 0:P], ACT.Copy, scale=wmean[:, 0:1])
                    nc.scalar.activation(xqT[s][:], bank[s][0][:].bitcast(BF16)[:, 0:P], ACT.Copy
                                         ).then_inc(f_xqT_sb, 1)
                for s in range(2):
                    act.wait_ge(f_hp, n[s])
                    for c in range(HC):
                        last = nc.scalar.activation(hid[0][s][:, c * P:(c + 1) * P], hp[s][:, c, 1:P + 1],
                                                    ACT.Identity, bias=col("f_convb", c),
                                                    scale=col("f_conv", 3 * c + 1))
                    last.then_inc(f_conv0, 1)
                for s in range(2):
                    act.wait_ge(f_conv, n[s])
                    nc.scalar.activation(hid[1][s][:], hid[0][s][:], ACT.Exp, scale=-1.0).then_inc(f_exp, 1)
                for s in range(2):
                    act.wait_ge(f_hqT, n[s])
                    nc.scalar.activation(hqT[s][:], bank[s][0][:].bitcast(BF16)[:, 0:HID], ACT.Copy
                                         ).then_inc(f_hqT_sb, 1)
                deviations("f", n)

        @block.vector
        def _(dve):
            steps = [0]

            def mark(ins):
                steps[0] += 1
                ins.then_inc(dve_step, 1)
                return steps[0]

            def after(count):
                dve.wait_ge(dve_step, count)

            def step(ins):
                after(mark(ins))

            V = nc.vector
            dve.wait_ge(ld_w, 64)
            for i, name in enumerate(("f_w1", "f_w2")):
                step(V.tensor_reduce(wabs[:, i:i + 1], w(name), AX.X, ALU.add, apply_absolute_value=True))
            V.tensor_copy(ident_bf[:], ident).then_inc(pre_dve, 1)
            dve.wait_ge(pre_pe, 1)
            V.tensor_scalar(wmean[:], bank[0][0][:, 0:2], 1.0 / (P * HID), 1e-5, ALU.mult, ALU.max
                            ).then_inc(pre_dve, 1)
            dve.wait_ge(pre_dve, 2)
            step(V.reciprocal(wscale[:], wmean[:]))
            for i, (name, dst) in enumerate((("f_w1", w1q), ("f_w2", w2q))):
                step(V.tensor_scalar(wtmp[:], w(name), wscale[:, i:i + 1], ROUND, ALU.mult, ALU.add))
                step(V.tensor_scalar(wtmp[:], wtmp[:], ROUND, 1.0, ALU.subtract, ALU.min))
                step(V.tensor_scalar(dst[:], wtmp[:], -1.0, None, ALU.max))
            step(V.tensor_scalar(ngb[:], col_sb[:, C_AT["a1_gb"][0]:C_AT["a1_gb"][1]], -1.0, None, ALU.mult))
            step(V.tensor_scalar(bqm0[:], const("group32"), col("a0_bq"), None, ALU.mult))
            step(V.tensor_scalar(bqm1[:], const("group32"), col("c1_bq"), None, ALU.mult))
            V.tensor_scalar(head8s[:], const("head8"), DH ** -0.5, None, ALU.mult).then_inc(pre_dve, 1)
            dve.wait_ge(pre_act, 1)
            for c in range(2):
                for a in range(2):
                    V.tensor_scalar(dqm[:, c, a, :], dq[:, c, :], const("head16", a, a + 1), None, ALU.mult)
            step(V.tensor_scalar(dk[:], dk[:], DH ** -0.5, None, ALU.mult))
            dve.wait_ge(pre_dve, 3)

            with dve.Fori(0, NP) as it:
                n = [dve.snap(it * 2 + 1), dve.snap(it * 2 + 2)]
                for s in range(2):
                    dve.wait_ge(r_last, n[s])
                    V.tensor_copy(rext[s][:, :, MAX_REL - 1 + P:M], bank[s][0][:, 0:H].unsqueeze(2)
                                  .broadcast_to([P, H, MAX_REL])).then_inc(r_right, 1)

            def add_and_shift(k, n):
                src = {}
                for g in range(4):
                    cnt = [0, 0]
                    for s in range(2):
                        nk = P if k == "a" else C
                        dst = (sc if k == "a" else scx)[s][:, 4 * g:4 * g + 4, :]
                        ps = bank[s][g][:, 0:4 * nk].rearrange("p (a j) -> p a j", a=4)
                        dve.wait_ge(scores[k], eights[2 * g + s])
                        if k == "a":
                            dve.wait_ge(ld_rel[s], rel_loaded)
                            cnt[s] = mark(V.tensor_tensor(dst, ps, rel[s][:, 4 * g:4 * g + 4, :], ALU.add))
                            ps = dst
                        src[s] = (dst, ps)
                    for s in range(2):
                        if k == "a":
                            after(cnt[s])
                        cnt[s] = mark(V.tensor_reduce(mx[s][:, 4 * g:4 * g + 4], src[s][1], AX.X, ALU.max))
                    for s in range(2):
                        after(cnt[s])
                        V.tensor_tensor(src[s][0], src[s][1], mx[s][:, 4 * g:4 * g + 4].unsqueeze(2)
                                        .broadcast_to([P, 4, P if k == "a" else C]), ALU.subtract
                                        ).then_inc(shifted[k], 1)

            def copy_probsT(k, n, nk):
                for g in (1, 3):
                    for s in range(2):
                        dve.wait_ge(probsT[k], eights[2 * g + s])
                        V.tensor_copy(pT[s][0:nk, 4 * g:4 * g + 4, :], bank[s][g][0:nk, :].rearrange(
                            "p (a i) -> p a i", a=4)).then_inc(probsT_odd[k], 1)

            def normalise(k, n, per_bank, width):
                d = width - 1
                for s in range(2):
                    dve.wait_ge(pv[k], n[s])
                    ps = [bank[s][b][:, 0:per_bank * width].rearrange("p (h d) -> p h d", d=width)
                          for b in range(H // per_bank)]
                    for b, t in enumerate(ps):
                        last = mark(V.reciprocal(rsum[s][:, b * per_bank:(b + 1) * per_bank], t[:, :, d]))
                    after(last)
                    o = o_sb[s][:, :, :].rearrange("p c i -> p (c i)")
                    for b, t in enumerate(ps):
                        last = V.tensor_tensor(
                            o[:, b * per_bank * d:(b + 1) * per_bank * d].rearrange("p (h d) -> p h d", d=d),
                            t[:, :, 0:d], rsum[s][:, b * per_bank:(b + 1) * per_bank].unsqueeze(2)
                            .broadcast_to([P, per_bank, d]), ALU.mult)
                    last.then_inc(o_ready[k], 1)

            def moments(k, s):
                step(V.bn_stats(stats[s][:], y[s][:]))
                V.bn_aggr(mv[s][:], stats[s][:]).then_inc(var[k], 1)

            def add_residual(k, n, other):
                for s in range(2):
                    dve.wait_ge(proj[k], n[s])
                    step(V.tensor_tensor(y[s][:], bank[s][2][:, 0:P], other[s][:], ALU.add))
                    moments(k, s)

            def norm(k, n, dst):
                for s in range(2):
                    dve.wait_ge(inv[k], n[s])
                    V.tensor_scalar(dst[s][:], y[s][:], mv[s][:, 0:1], rstd[s][:, 0:1], ALU.subtract,
                                    ALU.mult).then_inc(normed[k], 1)

            def quantise(s, src, c0, dst):
                step(V.tensor_reduce(scol[s][:, c0:c0 + 1], src, AX.X, ALU.max,
                                     apply_absolute_value=True))
                step(V.tensor_scalar(scol[s][:, c0:c0 + 1], scol[s][:, c0:c0 + 1], 1e-5, None, ALU.max))
                step(V.reciprocal(scol[s][:, c0 + 2:c0 + 3], scol[s][:, c0:c0 + 1]))
                step(V.tensor_scalar(scol[s][:, c0 + 2:c0 + 3], scol[s][:, c0 + 2:c0 + 3], QMAX, None, ALU.mult))
                step(V.tensor_scalar(scol[s][:, c0 + 1:c0 + 2], scol[s][:, c0:c0 + 1], 1.0 / QMAX, None,
                                     ALU.mult))
                tmp = big[s][:, 0:HID][:, 0:dst.shape[-1]]
                step(V.tensor_scalar(tmp, src, scol[s][:, c0 + 2:c0 + 3], ROUND, ALU.mult, ALU.add))
                return V.tensor_scalar(dst, tmp, ROUND, None, ALU.subtract)

            dve.wait_ge(pre_pool, N_POOL)
            with dve.Fori(0, NP) as it:
                n = [dve.snap(it * 2 + 1), dve.snap(it * 2 + 2)]
                rel_loaded = dve.snap(it * 32 + 32)
                two = [dve.snap(it * 4 + 2), dve.snap(it * 4 + 4)]
                stored = dve.snap(it * 16)
                eights = [dve.snap(it * 8 + i + 1) for i in range(8)]
                dve.sem_clear(dve_step)
                steps[0] = 0
                for s in range(2):
                    dve.wait_ge(x_kv0, n[s])
                    for c in range(2):
                        last = V.tensor_copy(v65[s][:, 8 * c:8 * c + 8, 0:XH], bank[s][2 + c][0:C, :].rearrange(
                            "p (h d) -> p h d", d=XH))
                    last.then_inc(x_v0, 1)
                for s in range(2):
                    dve.wait_ge(x_kv1, n[s])
                    for a in range(4):
                        V.tensor_scalar(k1bd[s][:, a, :], bank[s][0][:, 0:C], col("c1_bk"),
                                        head8s[:, a:a + 1], ALU.add, ALU.mult)
                    V.tensor_tensor(c9[s][:, :, 0:DH], bank[s][0][0:C, P:2 * P].rearrange(
                        "p (h d) -> p h d", d=DH), row("c1_bv")[0:C, :].rearrange("p (h d) -> p h d", d=DH),
                        ALU.add).then_inc(x_kv1_ready, 1)
                for s in range(2):
                    dve.wait_ge(a_qkv, n[s])
                    for a in range(4):
                        V.tensor_scalar(kbd[s][:, a, :], bank[s][1][:, 0:P], col("a0_bk"),
                                        head8s[:, a:a + 1], ALU.add, ALU.mult)
                    V.tensor_tensor(v9[s][:, :, 0:DH], bank[s][2][:, 0:P].rearrange(
                        "p (h d) -> p h d", d=DH), row("a0_bv").rearrange("p (h d) -> p h d", d=DH),
                        ALU.add).then_inc(a_kv, 1)
                add_and_shift("a", n)
                copy_probsT("a", n, P)
                normalise("a", n, H, DH + 1)
                dve.wait_ge(xb_ready["a"], n[1])
                add_residual("a", n, xb)
                norm("a", n, x)
                for s in range(2):
                    dve.wait_ge(b_q, n[s])
                    V.tensor_copy(q0[s][:, 4:8, :], bank[s][1][:].rearrange("p (c i) -> p c i", c=4)
                                  ).then_inc(b_q_hi, 1)
                add_and_shift("b", n)
                copy_probsT("b", n, C)
                normalise("b", n, 4, XH + 1)
                for s in range(2):
                    dve.wait_ge(oT_ps["b"], n[s])
                    V.tensor_copy(oT[s][:, 4:8, :], bank[s][1][:].rearrange("p (c i) -> p c i", c=4)
                                  ).then_inc(oT_ready2, 1)
                dve.wait_ge(normed["a"], n[1])
                add_residual("b", n, x)
                norm("b", n, x)
                for s in range(2):
                    dve.wait_ge(c_logits, n[s])
                    step(V.tensor_tensor(lg[s][:], bank[s][3][:, 0:E + 1], row("m_rb"), ALU.add))
                    step(V.max(top[s][:], lg[s][:]))
                    V.tensor_scalar(nmax[s][:], top[s][:, 0:1], -1.0, None, ALU.mult).then_inc(c_shift, 1)
                def hidden(e):
                    for s in range(2):
                        dve.wait_ge(c_up[e], n[s])
                        V.tensor_scalar(hid[1][s][:], bank[s][1][:], 0.0, None, ALU.max).then_inc(c_hid[e], 1)

                hidden(1)
                for s in range(2):
                    dve.wait_ge(c_exp, n[s])
                    step(V.reciprocal(esum[s][:], esum[s][:]))
                    step(V.tensor_scalar(wts[s][:], lg[s][:], esum[s][:, 0:1], None, ALU.mult))
                    step(V.max(top[s][:], wts[s][:]))
                    step(V.max_index(topi[s][:], top[s][:], wts[s][:]))
                    step(V.tensor_copy(topf[s][:], topi[s][:, 0:2]))
                    mark(V.tensor_scalar(sel[s][:], const("expert"), topf[s][:, 0:1], None, ALU.is_equal))
                    step(V.tensor_scalar(sel2[s][:], const("expert"), topf[s][:, 1:2], None, ALU.is_equal))
                    step(V.tensor_tensor(sel[s][:], sel[s][:], sel2[s][:], ALU.add))
                    V.scalar_tensor_tensor(out=picked[s][:], in0=wts[s][:], scalar=0.0, in1=sel[s][:],
                                           op0=ALU.is_gt, op1=ALU.mult).then_inc(c_pick, 1)
                dve.wait_ge(c_pick, n[1])
                for s in range(2):
                    step(V.tensor_tensor(sel2[s][:], wts[s][:], picked[s][:], ALU.mult))
                hidden(3)
                for s in range(2):
                    dve.wait_ge(c_rank, n[s])
                    V.tensor_tensor(keep[s][:], bank[s][3][:, 0:E + 1], const("cap"), ALU.is_lt
                                    ).then_inc(c_keep, 1)
                dve.wait_ge(c_keep, n[1])
                for s in range(2):
                    step(V.tensor_tensor(routed[:], routed[:], picked[s][:], ALU.add))
                    step(V.tensor_tensor(keep[s][:], keep[s][:], sel2[s][:], ALU.mult))
                    step(V.tensor_scalar(wpass[s][:], keep[s][:, E:E + 1], 1.0, None, ALU.add))
                    step(V.tensor_scalar(y[s][:], x[s][:], wpass[s][:, 0:1], None, ALU.mult))

                def combine(e0, e1):
                    cnt = [steps[0]] * 2
                    for e in range(e0, e1):
                        for s in range(2):
                            if e == e0:
                                dve.wait_ge(c_down[e // 4], n[s])
                            after(cnt[s])
                            cnt[s] = mark(V.scalar_tensor_tensor(
                                out=y[s][:], in0=bank[s][2 + e // 4][:, (e % 4) * P:(e % 4 + 1) * P],
                                scalar=keep[s][:, e:e + 1], in1=y[s][:], op0=ALU.mult, op1=ALU.add))

                hidden(5)
                combine(0, 4)
                combine(4, E)
                after(steps[0])
                for s in range(2):
                    moments("c", s)
                norm("c", n, x)
                for s in range(2):
                    dve.wait_ge(d_gate, n[s])
                    step(V.tensor_scalar(eg[s][:], eg[s][:], 1.0, None, ALU.add))
                    step(V.reciprocal(eg[s][:], eg[s][:]))
                    step(V.tensor_tensor(eg[s][:], eg[s][:], dk[:], ALU.mult))
                    dve.wait_ge(d_qk, n[s])
                    for i, (t, table) in enumerate(((t1, "cos"), (t2, "sin"))):
                        last = V.tensor_tensor(t[s][:], bank[s][0][:, i * 2 * P:(i + 1) * 2 * P].rearrange(
                            "p (a t) -> p a t", a=2), const(table).unsqueeze(1).broadcast_to([P, 2, P]),
                            ALU.mult)
                    step(last)
                    V.tensor_tensor(qk[s][:], t1[s][:], t2[s][:], ALU.add).then_inc(d_rope, 1)
                for s in range(2):
                    dve.wait_ge(d_rank, n[s])
                    kr = bank[s][2][:, 2 * P:4 * P].rearrange("p (c t) -> p c t", c=2)
                    for g in range(4):
                        V.scalar_tensor_tensor(out=kdm[s][:, g, :, :], in0=kr, scalar=const("group32", g, g + 1),
                                               in1=eg[s][:], op0=ALU.mult, op1=ALU.mult)
                    for c in range(2):
                        last = V.tensor_tensor(qd[s][:, c, :, :], bank[s][2][:, c * P:(c + 1) * P].unsqueeze(1)
                                               .broadcast_to([P, 2, P]), dqm[:, c, :, :], ALU.mult)
                    last.then_inc(d_qkd, 1)
                for g in range(4):
                    for s in range(2):
                        dve.wait_ge(d_att, eights[2 * g + s])
                        V.tensor_tensor(sc[s][:, 4 * g:4 * g + 4, :], bank[s][g][:].rearrange(
                            "p (a t) -> p a t", a=4), const("causal").unsqueeze(1).broadcast_to([P, 4, P]),
                            ALU.mult).then_inc(d_masked, 1)
                dve.wait_ge(xb_ready["d"], two[1])
                add_residual("d", n, xb)
                for s in range(2):
                    dve.wait_ge(inv["d"], n[s])
                    step(V.tensor_scalar(y2[s][:], y[s][:], mv[s][:, 0:1], rstd[s][:, 0:1], ALU.subtract,
                                         ALU.mult))
                    step(V.tensor_tensor(y2[s][:], y2[s][:], row("a1_lng"), ALU.mult))
                    step(V.tensor_tensor(y[s][:], y2[s][:], xb2[s][:], ALU.add))
                    moments("D", s)
                norm("D", n, x)
                add_and_shift("e", n)
                copy_probsT("e", n, C)
                normalise("e", n, H, DH + 1)
                dve.wait_ge(xb_ready["e"], n[1])
                add_residual("e", n, xb)
                norm("e", n, x)
                dve.wait_ge(normed["e"], n[1])
                for s in range(2):
                    step(quantise(s, x[s][:], 0, xq[s][:]))
                    V.tensor_scalar(diag[s][:], ident, scol[s][:, 1:2], None, ALU.mult).then_inc(f_xq, 1)
                for s in range(2):
                    dve.wait_ge(f_h, n[s])
                    V.tensor_tensor(hp[s][:, :, 1:P + 1], bank[s][2][:].rearrange("p (c t) -> p c t", c=HC),
                                    scbc[s][:].unsqueeze(1).broadcast_to([P, HC, P]), ALU.mult
                                    ).then_inc(f_hp, 1)
                for s in range(2):
                    dve.wait_ge(f_hp, n[s])
                    dve.wait_ge(f_conv0, n[s])
                    for tap in (0, 2):
                        for c in range(HC):
                            hc = hid[0][s][:, c * P:(c + 1) * P]
                            last = V.scalar_tensor_tensor(
                                out=hc, in0=hp[s][:, c, tap:tap + P], scalar=col("f_conv", 3 * c + tap),
                                in1=hc, op0=ALU.mult, op1=ALU.add)
                        if tap == 0:
                            step(last)
                    last.then_inc(f_conv, 1)
                for s in range(2):
                    dve.wait_ge(f_exp, n[s])
                    step(V.tensor_scalar(hid[1][s][:], hid[1][s][:], 1.0, None, ALU.add))
                    step(V.reciprocal(hid[1][s][:], hid[1][s][:]))
                    V.tensor_tensor(hid[0][s][:], hid[0][s][:], hid[1][s][:], ALU.mult).then_inc(f_silu, 1)
                for s in range(2):
                    dve.wait_ge(f_hT, n[s])
                    quantise(s, bank[s][3][:], 3, hq[s][:]).then_inc(f_hq, 1)
                for s in range(2):
                    dve.wait_ge(f_hq, n[s])
                    step(V.tensor_tensor(scol[s][:, 6:7], scol[s][:, 4:5], wmean[:, 1:2], ALU.mult))
                    dve.wait_ge(proj["f"], n[s])
                    step(V.scalar_tensor_tensor(out=y[s][:], in0=bank[s][1][:, 0:P], scalar=scol[s][:, 6:7],
                                                in1=x[s][:], op0=ALU.mult, op1=ALU.add))
                    moments("f", s)
                for s in range(2):
                    dve.wait_ge(st_out[s], stored)
                norm("f", n, out_sb)


N_POOL = 3 + 2 * 5


def tables():
    p, t = np.arange(P)[:, None], np.arange(P)[None, :]
    half = DH // 2
    freq = (1.0 / 10000.0 ** (np.arange(half, dtype=np.float32) / np.float32(half))).astype(np.float32)
    angle = (np.arange(P, dtype=np.float32)[None, :] * freq[(np.arange(P) % DH) // 2][:, None]).astype(np.float32)
    sign = np.where(p % 2 == 0, -1.0, 1.0)
    parts = {
        "ident": p == t,
        "tri": p < t,
        "causal": p <= t,
        "cos": np.cos(angle), "sin": np.sin(angle) * sign,
        "time": np.broadcast_to(t - MID, (P, P)),
        "head8": (p // DH) % 4 == np.arange(4),
        "group32": p // 32 == np.arange(4),
        "head16": (p // R) % 2 == np.arange(2),
        "expert": np.broadcast_to(np.arange(E + 1), (P, E + 1)),
        "cap": np.broadcast_to(np.where(np.arange(E + 1) < E, CAP, 2 * B * P), (P, E + 1)),
    }
    return np.concatenate([np.asarray(parts[k], np.float32) for k in CONSTS], axis=1)


def kernel(**inputs):
    import concourse.bacc as bacc
    from concourse.bass_utils import run_bass_kernel_spmd

    g = {k: np.asarray(v) for k, v in inputs.items()}

    def by_rows(a, chunk=P):
        return a.reshape(-1, chunk, a.shape[1]).transpose(1, 0, 2).reshape(chunk, -1)

    tab = g["L0_attn_rel_table"]
    rel_bd = np.zeros((4, 4, DH, 4, P), np.float32)
    rel_last = np.zeros((4, 4, DH, 4, H), np.float32)
    for grp in range(4):
        for a in range(4):
            rel_bd[grp, a, :, a, :] = tab[:2 * MAX_REL].T
            rel_last[grp, a, :, grp, 4 * grp + a] = tab[2 * MAX_REL]
    rank = {}
    for name in ("Wq", "Wk"):
        bd = np.zeros((H, DH, H, R), np.float32)
        for h in range(H):
            bd[h, :, h, :] = g[f"L1_attn_{name}"][h].T
        rank[name] = bd.reshape(P, H * R)
    swap = np.arange(P) ^ 1
    inw = g["L1_xattn_in_proj_weight"]
    weights = {
        "a0_wq": g["L0_attn_Wq"], "a0_wk": g["L0_attn_Wk"], "a0_wv": g["L0_attn_Wv"],
        "a0_wo": g["L0_attn_Wo"], "a0_rel": rel_bd.reshape(P, 4 * P), "a0_rel_last": rel_last.reshape(P, 4 * H),
        "c0_wq": g["L0_xattn_Wq"], "c0_wk": g["L0_xattn_Wk"], "c0_wv": g["L0_xattn_Wv"],
        "c0_wo": by_rows(g["L0_xattn_Wo"]),
        "m_router": g["L0_ffn_router_w"].T,
        "m_w1": g["L0_ffn_experts_inter"].transpose(1, 0, 2).reshape(P, -1),
        "m_w2": by_rows(g["L0_ffn_experts_out"].reshape(E * HID, P)),
        "a1_wq": g["L1_attn_q_w"].T, "a1_wqs": g["L1_attn_q_w"][swap].T,
        "a1_wk": g["L1_attn_k_w"].T, "a1_wks": g["L1_attn_k_w"][swap].T,
        "a1_wv": g["L1_attn_v_w"].T, "a1_wg": g["L1_attn_g_w"].T,
        "a1_rq": rank["Wq"], "a1_rk": rank["Wk"], "a1_wo": g["L1_attn_out_w"].T,
        "c1_wq": inw[0:P].T, "c1_wk": inw[P:2 * P].T, "c1_wv": inw[2 * P:3 * P].T,
        "c1_wo": g["L1_xattn_out_proj_weight"].T,
        "f_w1": g["L1_ffn_w1"].T, "f_w2": by_rows(g["L1_ffn_w2"].T),
    }
    inb = g["L1_xattn_in_proj_bias"]
    columns = {
        "a0_bq": g["L0_attn_bq"].reshape(P, 1), "a0_bk": g["L0_attn_bk"].reshape(P, 1),
        "c1_bq": inb[0:P].reshape(P, 1), "c1_bk": inb[P:2 * P].reshape(P, 1),
        "a1_gb": g["L1_attn_g_b"].reshape(2, P).T,
        "a1_decay": g["L1_attn_base_decay_logits"].reshape(2, P).T,
        "f_conv": by_rows(g["L1_ffn_conv_w"].reshape(HID, 3)),
        "f_convb": g["L1_ffn_conv_b"].reshape(HC, P).T,
    }
    rows = {
        "a0_bv": g["L0_attn_bv"], "a0_bo": g["L0_attn_bo"], "m_rb": g["L0_ffn_router_b"],
        "a1_bo": g["L1_attn_out_b"], "a1_lng": g["L1_attn_ln_g"], "a1_lnb": g["L1_attn_ln_b"],
        "c1_bv": inb[2 * P:3 * P], "c1_bo": g["L1_xattn_out_proj_bias"],
    }
    arrays = {
        "x": g["x"].reshape(NP, 2, P, P),
        "xT": g["x"].transpose(0, 2, 1).reshape(NP, 2, P, P),
        "cT": g["ctx_1024"].transpose(0, 2, 1).reshape(NP, 2, P, C),
        "weights": np.concatenate([weights[k] for k in WEIGHTS], axis=1),
        "columns": np.concatenate([columns[k] for k in COLUMNS], axis=1),
        "rows": np.concatenate([rows[k] for k in ROWS]),
        "consts": tables(),
    }
    arrays = {k: np.ascontiguousarray(v) for k, v in arrays.items()}
    nc = bacc.Bacc("TRN2", target_bir_lowering=False, num_devices=1)
    args = [nc.dram_tensor(k, v.shape, F32, kind="ExternalInput").ap() for k, v in arrays.items()]
    out = nc.dram_tensor("out", (NP, 2, P, P), F32, kind="ExternalOutput").ap()
    rel_scores = nc.dram_tensor("rel_scores", (NP, 2, P * RROW), F32, kind="Internal").ap()
    decoder(nc, *args, out, rel_scores)
    r = run_bass_kernel_spmd(nc, [arrays], core_ids=[0])
    return r.results[0]["out"].reshape(B, P, P)
```

```python
from contextlib import ExitStack

import numpy as np

import concourse.bass as bass
from concourse import mybir

F32 = mybir.dt.float32
BF16 = mybir.dt.bfloat16
U32 = mybir.dt.uint32
ALU = mybir.AluOpType
ACT = mybir.ActivationFunctionType
AX = mybir.AxisListType

P = 128
B = 16
NP = B // 2
C = 77
H = 16
DH = P // H
XH = 64
XC = H * XH // P
MAX_REL = 64
M = 2 * P - 1
RROW = H * M
E = 7
HID = 512
HC = HID // P
CAP = B * P // (E + 1)
R = 16
MID = P // 2
EPS = 1e-5
CP = 96
EXP_MAX = 1e18
KEY_BANK = (1, 3)
REL_BANK = (3, 0, 1, 3)
ROUND = 1.5 * 2.0 ** 23
QMAX = 127.0

WEIGHTS = {
    "a0_wq": P, "a0_wk": P, "a0_wv": P, "a0_rel": 4 * P, "a0_rel_last": 4 * H,
    "c0_wk": H * XH, "c0_wv": H * XH, "c1_wk": P, "c1_wv": P,
    "a0_wo": P, "c0_wq": H * XH, "c0_wo": XC * P,
    "m_router": E + 1, "m_w1": E * HID, "m_w2": E * HC * P,
    "a1_wq": P, "a1_wqs": P, "a1_wk": P, "a1_wks": P, "a1_wv": P, "a1_wg": H * R,
    "a1_rq": 2 * P, "a1_rk": 2 * P, "a1_wo": P,
    "c1_wq": P, "c1_wo": P, "f_w1": HID, "f_w2": HC * P,
}
PARTS = ("a0_wq", "a0_wo", "m_router")
COLUMNS = {"a0_bq": 1, "a0_bk": 1, "c1_bq": 1, "c1_bk": 1, "a1_gb": 2, "a1_decay": 2,
           "f_conv": 3 * HC, "f_convb": HC}
ROWS = {"a0_bv": P, "a0_bo": P, "m_rb": E + 1, "a1_bo": P, "a1_lng": P, "a1_lnb": P,
        "c1_bv": P, "c1_bo": P}
CONSTS = {"ident": P, "tri": P, "causal": P, "cos": P, "sin": P, "time": P, "headsel": P,
          "head8": 4, "group32": 4, "head16": 2, "expert": E + 1, "cap": E + 1}


def offsets(sizes):
    at, found = 0, {}
    for name, n in sizes.items():
        found[name] = (at, at + n)
        at += n
    return found, at


W_AT, W_N = offsets(WEIGHTS)
C_AT, C_N = offsets(COLUMNS)
R_AT, R_N = offsets(ROWS)
K_AT, K_N = offsets(CONSTS)



SECOND = ("d_qkv d_rank d_s0 d_s1 d_s2 d_s3 d_values a_qkv d_out rel0 rel1 rel2 rel3 d_norm e_q "
          "rel_last e_s0 e_s1 e_s2 e_t0 e_s3 e_t1 e_t2 e_t3 e_sums e_values e_out keys_k f_in "
          "keys_v f_up keys1 f_conv f_silu f_quant f_down f_norm").split()
NEXT = ["a_qkv", "rel0", "rel1", "rel2", "rel3", "rel_last", "keys_k", "keys_v", "keys1"]
HALF = ("d_qkv a_s0 a_s1 a_s2 d_rank a_t0 a_s3 d_s0 a_t1 d_s1 d_s2 a_t2 d_s3 a_t3 d_values a_sums "
        "a_qkv d_out a_values rel0 rel1 rel2 rel3 d_norm e_q a_out rel_last a_norm e_s0 e_s1 e_s2 "
        "e_t0 b_q e_s3 e_t1 e_t2 b_s0 b_s1 e_t3 e_sums b_u0 b_s2 b_u1 e_values b_t0 b_s3 b_u2 b_t1 "
        "b_u3 b_t2 b_t3 e_out b_values keys_k f_in b_out keys_v b_norm f_up c_route c_up0 c_pick "
        "c_up1 c_down0 c_up2 keys1 c_rank c_down1 c_up3 f_conv c_down2 c_up4 c_keep c_down3 c_up5 "
        "c_down4 c_up6 c_down5 c_down6 f_silu c_norm f_quant f_down f_norm").split()
FIRST = [name for name in HALF if name not in SECOND]


def stages(names, s, pair):
    return [(name, s, pair) for name in names]


def half(s, pair, other_pair):
    return [(name, s, pair + (name in NEXT)) if name in SECOND else (name, 1 - s, other_pair)
            for name in HALF]


def before_loop():
    first = [stage for stage in half(1, -1, 0) if stage[0] not in SECOND or stage[0] in NEXT]
    at = [name for name, _, _ in first].index("c_up3")
    return (stages(NEXT, 0, 0) + stages(["weights"], 1, 0) + first[:at]
            + stages(["ternary_sum", "ternary"], 0, 0) + first[at:] + stages(["ternary_over"], 0, 0))


def in_loop(it):
    return half(0, it, it) + half(1, it, it + 1)


def after_loop():
    return ([stage for stage in half(0, NP - 1, NP - 1) if stage[0] not in NEXT]
            + [stage for stage in half(1, NP - 1, NP) if stage[0] in SECOND and stage[0] not in NEXT])


def decoder(nc, x_in, xT_in, cT_in, weights, columns, rows, consts, out, rel_dram):
    with ExitStack() as ctx:
        def sb(name, shape, dt=F32):
            return ctx.enter_context(nc.sbuf_tensor(name, shape, dt))

        def per_seq(name, shape, dt=F32):
            return [sb(f"{name}{s}", shape, dt) for s in range(2)]

        def sem(name):
            return ctx.enter_context(nc.semaphore(name))

        bank = [[ctx.enter_context(nc.psum_tensor(f"bank{s}{i}", [P, 512], F32)) for i in range(4)]
                for s in range(2)]

        w_sb = sb("w_sb", [P, W_N])
        col_sb = sb("col_sb", [P, C_N])
        row_sb = sb("row_sb", [P, R_N])
        k_sb = sb("k_sb", [P, K_N])
        ident_bf = sb("ident_bf", [P, P], BF16)
        ones = sb("ones", [P, P])
        eps = sb("eps", [P, 1])
        bqm0 = sb("bqm0", [P, 4])
        bqm1 = sb("bqm1", [P, 4])
        head8s = sb("head8s", [P, 4])
        ngb = sb("ngb", [P, 2])
        loglam = sb("loglam", [P, 2])
        nloglam = sb("nloglam", [P, 2])
        dq = sb("dq", [P, 2, P])
        dqm = sb("dqm", [P, 2, 2, P])
        dk = sb("dk", [P, 2, P])
        w1q = sb("w1q", [P, HID], BF16)
        w2q = sb("w2q", [P, HC * P], BF16)
        wabs = sb("wabs", [P, 2])
        wmean = sb("wmean", [P, 2])
        wscale = sb("wscale", [P, 2])
        routed = sb("routed", [P, E + 1])
        rext = sb("rext", [P, H, M])
        rel = sb("rel", [P, H, P])

        def w(name, a=0, b=None):
            lo, hi = W_AT[name]
            return w_sb[:, lo + a:(hi if b is None else lo + b)]

        def col(name, i=0):
            return col_sb[:, C_AT[name][0] + i:C_AT[name][0] + i + 1]

        def row(name):
            return row_sb[:, R_AT[name][0]:R_AT[name][1]]

        def const(name, a=0, b=None):
            lo, hi = K_AT[name]
            return k_sb[:, lo + a:(hi if b is None else lo + b)]

        ident = const("ident")

        x_ld = per_seq("x_ld", [P, P])
        xT_ld = per_seq("xT_ld", [P, P])
        cT = per_seq("cT", [P, CP])
        probs_sb = per_seq("probs_sb", [P, H * P])
        pT = per_seq("pT", [P, H, P])
        qm = per_seq("qm", [P, 4, P])
        kbd = per_seq("kbd", [P, 4, P])
        va = per_seq("va", [P, 4, 160])
        ve = per_seq("ve", [P, 4, 160])
        k0bd = per_seq("k0bd", [P, XC, 2, C])
        v0 = per_seq("v0", [P, H, XH])
        k1bd = per_seq("k1bd", [P, 4, C])
        nmx = per_seq("nmx", [P, H])
        psum_ = per_seq("psum_", [P, H])
        rr = per_seq("rr", [P, H])
        rrT = per_seq("rrT", [H, P])
        rbc = per_seq("rbc", [P, P])
        q0 = per_seq("q0", [P, XC, P])
        oT = per_seq("oT", [P, XC, P])
        xb = per_seq("xb", [P, P])
        xb2 = per_seq("xb2", [P, P])
        y = per_seq("y", [P, P])
        y2 = per_seq("y2", [P, P])
        x = per_seq("x", [P, P])
        out_sb = per_seq("out_sb", [P, P])
        xT = per_seq("xT", [P, P])
        stats = per_seq("stats", [P, 6])
        mv = per_seq("mv", [P, 2])
        lnv = per_seq("lnv", [P, 1])
        rstd = per_seq("rstd", [P, 1])
        lg = per_seq("lg", [P, 8])
        top = per_seq("top", [P, 8])
        nmax = per_seq("nmax", [P, 1])
        esum = per_seq("esum", [P, 1])
        wts = per_seq("wts", [P, 8])
        topi = per_seq("topi", [P, 8], U32)
        topf = per_seq("topf", [P, 2])
        sel = per_seq("sel", [P, 8])
        sel2 = per_seq("sel2", [P, 8])
        picked = per_seq("picked", [P, 8])
        keep = per_seq("keep", [P, 8])
        wpass = per_seq("wpass", [P, 1])
        scol = per_seq("scol", [P, 8])
        xq = per_seq("xq", [P, P], BF16)
        xqT = per_seq("xqT", [P, P], BF16)
        hp = per_seq("hp", [P, HC, P + 2])
        hid = [[q0[s][:, 4 * i:4 * i + 4, :].rearrange("p c i -> p (c i)") for s in range(2)]
               for i in range(2)]
        sc = [probs_sb[s][:, :].rearrange("p (h j) -> p h j", h=H) for s in range(2)]
        scx = [probs_sb[s][:, 0:H * C].rearrange("p (h j) -> p h j", h=H) for s in range(2)]
        t1 = [q0[s][:, 0:2, :] for s in range(2)]
        t2 = [q0[s][:, 2:4, :] for s in range(2)]
        qk = [q0[s][:, 4:6, :] for s in range(2)]
        eg = [q0[s][:, 6:8, :] for s in range(2)]
        qd = [kbd[s].rearrange("p (c a) t -> p c a t", c=2) for s in range(2)]
        kdm = [oT[s][:, :, :].rearrange("p (g c) t -> p g c t", g=4) for s in range(2)]

        qm1 = [q0[s][:, 0:4, :] for s in range(2)]
        diag, scbc = ([pT[s][:, i, :] for s in range(2)] for i in (4, 5))
        hq, hqT = ([pT[s][:, i:i + 2, :].rearrange("p h i -> p (h i)").bitcast(BF16) for s in range(2)]
                   for i in (0, 2))

        def heads(v):
            return v.rearrange("p q (a c) -> p q a c", c=40)[:, :, :, 0:DH]

        def by_head(ap):
            return ap.rearrange("p (q a d) -> p q a d", q=4, a=4)

        ld_w = sem("ld_w")
        ld_part = [sem(f"ld_part{i}") for i in range(len(PARTS))]
        ld_x, ld_xT, ld_c = ([sem(f"{k}{s}") for s in range(2)] for k in ("ld_x", "ld_xT", "ld_c"))
        ld_rel, st_rel = sem("ld_rel"), sem("st_rel")
        st_out = [sem(f"st_out{s}") for s in range(2)]
        pre_pool, pre_dve, pre_act, pre_pe = sem("pre_pool"), sem("pre_dve"), sem("pre_act"), sem("pre_pe")
        r_s, r_mid, r_last, r_left, r_right = (sem(n) for n in (
            "r_s", "r_mid", "r_last", "r_left", "r_right"))
        x_keys, x_k0, x_values, x_v0, x_kv1, x_kv1_ready = (sem(n) for n in (
            "x_keys", "x_k0", "x_values", "x_v0", "x_kv1", "x_kv1_ready"))
        a_qkv, a_qm, a_kv = sem("a_qkv"), sem("a_qm"), sem("a_kv")
        scores = {k: sem(f"{k}_scores") for k in "abe"}
        maxed = {k: sem(f"{k}_maxed") for k in "abe"}
        exped = {k: sem(f"{k}_exped") for k in "abe"}
        b_scaled = sem("b_scaled")
        probsT = {k: sem(f"{k}_probsT") for k in "abe"}
        probsT_even = {k: sem(f"{k}_probsT_even") for k in "abe"}
        probsT_odd = {k: sem(f"{k}_probsT_odd") for k in "abe"}
        recips, recipsT, recipsT_sb, spread, spread_sb = (
            {k: sem(f"{k}_{name}") for k in "ae"}
            for name in ("recips", "recipsT", "recipsT_sb", "spread", "spread_sb"))
        values = {k: sem(f"{k}_values") for k in "abde"}
        oT_ready = {k: sem(f"{k}_oT_ready") for k in "abde"}
        oT_ready2 = sem("b_oT_ready2")
        proj = {k: sem(f"{k}_proj") for k in "abdef"}
        b_q, b_q_lo, b_q_hi = sem("b_q"), sem("b_q_lo"), sem("b_q_hi")
        e_q, e_qm = sem("e_q"), sem("e_qm")
        var = {k: sem(f"{k}_var") for k in "abcdDef"}
        inv = {k: sem(f"{k}_inv") for k in "abcdDef"}
        normed = {k: sem(f"{k}_normed") for k in "abcDef"}
        xT_ps = {k: sem(f"{k}_xT_ps") for k in "abcD"}
        xT_ready = {k: sem(f"{k}_xT_ready") for k in "abcD"}
        xb_ready = {k: sem(f"{k}_xb") for k in "ade"}
        c_logits, c_shift, c_exp, c_pick, c_rank, c_keep = (sem(n) for n in (
            "c_logits", "c_shift", "c_exp", "c_pick", "c_rank", "c_keep"))
        c_up = sem("c_up")
        c_hid = [sem("c_hid_even"), sem("c_hid_odd")]
        c_down = [sem("c_down_lo"), sem("c_down_hi")]
        d_qk, d_gv, d_gate0, d_gate1, d_gate, d_v, d_rope, d_rank, d_qkd = (sem(n) for n in (
            "d_qk", "d_gv", "d_gate0", "d_gate1", "d_gate", "d_v", "d_rope", "d_rank", "d_qkd"))
        d_att, d_masked = sem("d_att"), sem("d_masked")
        (f_xq, f_xqT, f_xqT_sb, f_h, f_hp, f_conv0, f_conv, f_exp, f_exp1, f_sig, f_silu, f_hT, f_hq,
         f_hqT, f_hqT_sb) = (sem(n) for n in (
             "f_xq", "f_xqT", "f_xqT_sb", "f_h", "f_hp", "f_conv0", "f_conv", "f_exp",
             "f_exp1", "f_sig", "f_silu", "f_hT", "f_hq", "f_hqT", "f_hqT_sb"))
        banks_free = sem("banks_free")
        dve_step, act_step = sem("dve_step"), sem("act_step")

        def counter(eng):
            held = {}

            def n(s, pair, per=1, step=None):
                value = pair * (2 * per) + (per * s + (per if step is None else step))
                if isinstance(pair, int):
                    return max(value, 0)
                key = (id(pair), per, s, step)
                if key not in held:
                    held[key] = (pair, eng.snap(value))
                return held[key][1]
            return n

        def transfers(eng, pair):
            return 16 * (pair + 1) if isinstance(pair, int) else eng.snap((pair + 1) * 16)

        def run(eng, table, clear=None):
            def go(order):
                for name, s, pair in order:
                    if name in table:
                        table[name](s, pair)
            go(before_loop())
            if clear:
                clear()
            with eng.Fori(0, NP - 1) as it:
                if clear:
                    clear()
                nxt = eng.snap(it + 1)
                pairs = {0: it, 1: nxt}
                go([(name, s, pairs[pair]) for name, s, pair in in_loop(0)])
            if clear:
                clear()
            go(after_loop())

        block = ctx.enter_context(nc.Block())

        @block.sync
        def _(sp):
            n = counter(sp)

            def loaded_before(s, pair):
                sp.wait_ge(x_kv1, n(s, pair, step=-1))
                sp.dma_start(cT[s][:, 0:C], cT_in[pair, s]).then_inc(ld_c[s], 16)
                sp.wait_ge(a_qkv, n(s, pair, step=-1))
                sp.dma_start(xT_ld[s][:], xT_in[pair, s]).then_inc(ld_xT[s], 16)
                sp.wait_ge(xb_ready["a"], n(s, pair, step=-1))
                sp.dma_start(x_ld[s][:], x_in[pair, s]).then_inc(ld_x[s], 16)

            def store_rel(s, pair):
                sp.wait_ge(r_left, n(s, pair))
                sp.wait_ge(r_right, n(s, pair))
                sp.dma_start(rel_dram[pair, s].rearrange("(i c) -> i c", c=RROW),
                             rext[:, :, :].rearrange("p h m -> p (h m)")).then_inc(st_rel, 16)

            def load_rel(s, pair):
                sp.wait_ge(maxed["a"], n(s, pair, per=4, step=0))
                sp.wait_ge(st_rel, n(s, pair, per=16))
                skewed = rel_dram[pair, s, P - 1:P - 1 + P * (RROW - 1)].rearrange(
                    "(i c) -> i c", c=RROW - 1)
                sp.dma_start(rel[:, 0:H - 1, :], skewed[:, 0:(H - 1) * M].rearrange(
                    "i (h m) -> i h m", m=M)[:, :, 0:P]).then_inc(ld_rel, 16)
                sp.dma_start(rel[:, H - 1, :], skewed[:, (H - 1) * M:(H - 1) * M + P]
                             ).then_inc(ld_rel, 16)

            sp.dma_start(xT_ld[0][:], xT_in[0, 0]).then_inc(ld_xT[0], 16)
            sp.dma_start(k_sb[:], consts).then_inc(ld_w, 16)
            sp.dma_start(col_sb[:], columns).then_inc(ld_w, 16)
            sp.dma_start(row_sb[:], rows.partition_broadcast(P)).then_inc(ld_w, 16)
            ends = [W_AT[name][0] for name in PARTS[1:]] + [W_N]
            for i, (name, end) in enumerate(zip(PARTS, ends)):
                part = slice(W_AT[name][0], end)
                sp.dma_start(w_sb[:, part], weights[:, part]).then_inc(ld_part[i], 16)
                if i == 0:
                    sp.dma_start(cT[0][:, 0:C], cT_in[0, 0]).then_inc(ld_c[0], 16)
                    sp.dma_start(x_ld[0][:], x_in[0, 0]).then_inc(ld_x[0], 16)
                    loaded_before(1, 0)
            store_rel(0, 0)
            load_rel(0, 0)
            store_rel(1, 0)
            with sp.Fori(0, NP - 1) as it:
                nxt = sp.snap(it + 1)
                for s, pair, per in ((0, nxt, 4), (0, nxt, 16), (1, it, 4), (1, it, 16)):
                    n(s, pair, per, 0 if per == 4 else None)
                loaded_before(0, nxt)
                load_rel(1, it)
                store_rel(0, nxt)
                loaded_before(1, nxt)
                load_rel(0, nxt)
                store_rel(1, nxt)
            load_rel(1, NP - 1)

        @block.gpsimd
        def _(pool):
            G = nc.gpsimd
            n = counter(pool)
            G.memset(ones[:], 1.0).then_inc(pre_pool, 1)
            G.memset(eps[:], EPS).then_inc(pre_pool, 1)
            G.memset(routed[:], 0.0).then_inc(pre_pool, 1)
            for s in range(2):
                for t in (va, ve, k0bd, v0, hp):
                    G.memset(t[s][:], 0.0).then_inc(pre_pool, 1)
                G.memset(cT[s][:, C:CP], 0.0).then_inc(pre_pool, 1)

            def rel_left(s, pair):
                pool.wait_ge(r_mid, n(s, pair, 4))
                lo = rext[:, :, MAX_REL - 1:MAX_REL].broadcast_to([P, H, MAX_REL - 1])
                G.tensor_tensor(rext[:, :, 0:MAX_REL - 1], lo, ones[:, 0:1].unsqueeze(2).broadcast_to(
                    [P, H, MAX_REL - 1]), ALU.mult).then_inc(r_left, 1)

            def residual(k, src, before, bias, dst=xb):
                def f(s, pair):
                    before(s, pair)
                    G.tensor_tensor(dst[s][:], src[s][:], row(bias), ALU.add).then_inc(xb_ready[k], 1)
                return f

            def before_a(s, pair):
                pool.wait_ge(ld_x[s], transfers(pool, pair))
                pool.wait_ge(x_kv1, n(s, pair))

            def d_residuals(s, pair):
                pool.wait_ge(normed["c"], n(s, pair))
                G.tensor_tensor(xb[s][:], x[s][:], row("a1_bo"), ALU.add).then_inc(xb_ready["d"], 1)
                G.tensor_tensor(xb2[s][:], x[s][:], row("a1_lnb"), ALU.add).then_inc(xb_ready["d"], 1)

            def store(s, pair):
                pool.wait_ge(normed["f"], n(s, pair))
                G.dma_start(out[pair, s], out_sb[s][:]).then_inc(st_out[s], 16)
                pool.wait_ge(st_out[s], transfers(pool, pair))

            pool.wait_ge(ld_w, 48)
            pool.wait_ge(pre_pool, 1)
            run(pool, {
                "rel_last": rel_left,
                "a_s0": residual("a", x_ld, before_a, "a0_bo"),
                "c_norm": d_residuals,
                "d_norm": residual("e", x, lambda s, pair: pool.wait_ge(normed["D"], n(s, pair)), "c1_bo"),
                "f_norm": store,
            })
            pool.wait_ge(st_out[0], 16 * NP)
            pool.wait_ge(st_out[1], 16 * NP)

        @block.tensor
        def _(pe):
            n = counter(pe)

            def mm(out_, lhsT, rhs, start=True, stop=True):
                return pe.matmul(out_, lhsT, rhs, start=start, stop=stop)

            pe.wait_ge(pre_pool, N_POOL)
            pe.wait_ge(ld_w, 48)
            pe.wait_ge(ld_part[0], 16)
            pe.wait_ge(pre_dve, 1)

            def more_weights(s, pair):
                pe.wait_ge(ld_part[s], 16)

            def c_weights(s, pair):
                if isinstance(pair, int) and (s, pair) == (0, 0):
                    pe.wait_ge(ld_part[2], 16)

            def ternary(s, pair):
                pe.wait_ge(pre_dve, 2)
                pe.wait_ge(r_right, 2)
                mm(bank[1][0][:, 0:2], ones[:], wabs[:]).then_inc(pre_pe, 1)

            def ternary_over(s, pair):
                pe.wait_ge(pre_dve, 4)

            def rel_scores(g):
                def f(s, pair):
                    if g == 0:
                        pe.wait_ge(a_qm, n(s, pair))
                    elif g == 2:
                        pe.wait_ge(a_kv, n(s, pair))
                    elif g == 3:
                        pe.wait_ge(r_mid, n(s, pair, 4, 1))
                    mm(bank[s][REL_BANK[g]][:], qm[s][:, g, :], w("a0_rel")).then_inc(r_s, 1)
                return f

            def rel_last(s, pair):
                pe.wait_ge(r_mid, n(s, pair, 4, 2))
                for g in range(4):
                    last = mm(bank[s][0][:, 0:H], qm[s][:, g, :], w("a0_rel_last", g * H, (g + 1) * H),
                              start=(g == 0), stop=(g == 3))
                last.then_inc(r_last, 1)

            def keys_k(s, pair):
                pe.wait_ge(ld_c[s], transfers(pe, pair))
                pe.wait_ge(r_mid, n(s, pair, 4))
                for c in range(XC):
                    last = mm(bank[s][KEY_BANK[c // 4]][:, (c % 4) * CP:(c % 4 + 1) * CP],
                              w("c0_wk", c * P, (c + 1) * P), cT[s][:])
                last.then_inc(x_keys, 1)

            def keys_v(s, pair):
                pe.wait_ge(x_k0, n(s, pair))
                for c in range(2):
                    last = mm(bank[s][KEY_BANK[c]][0:C, :], cT[s][:, 0:C],
                              w("c0_wv", c * 512, (c + 1) * 512))
                last.then_inc(x_values, 1)

            def keys1(s, pair):
                pe.wait_ge(x_v0, n(s, pair))
                mm(bank[s][3][:, 0:CP], w("c1_wk"), cT[s][:])
                mm(bank[s][3][0:C, P:2 * P], cT[s][:, 0:C], w("c1_wv")).then_inc(x_kv1, 1)

            def a_qkv_(s, pair):
                pe.wait_ge(ld_xT[s], transfers(pe, pair))
                mm(bank[s][3][:, 0:P], w("a0_wq"), xT_ld[s][:])
                mm(bank[s][1][:, P:2 * P], w("a0_wk"), xT_ld[s][:])
                mm(bank[s][1][:, 2 * P:3 * P], xT_ld[s][:], w("a0_wv")).then_inc(a_qkv, 1)

            def a_scores(g):
                def f(s, pair):
                    if g == 0:
                        pe.wait_ge(banks_free, n(s, pair))
                        pe.wait_ge(r_right, n(s, pair))
                        pe.wait_ge(x_kv1_ready, n(s, pair))
                    mm(bank[s][g][:], qm[s][:, g, :], kbd[s][:, :, :]).then_inc(scores["a"], 1)
                return f

            def transposes(k, ready, g):
                def f(s, pair):
                    nk, src = (P, sc) if k == "a" else (C, scx)
                    pe.wait_ge(ready, n(s, pair, 4, g + 1))
                    for a in range(4):
                        last = pe.transpose(bank[s][g][0:nk, a * P:(a + 1) * P],
                                            src[s][:, 4 * g + a, :], ident)
                    last.then_inc(probsT[k], 1)
                return f

            def sums(k):
                def f(s, pair):
                    pe.wait_ge(recips[k], n(s, pair))
                    pe.wait_ge(probsT_odd[k], n(s, pair, 2, 2))
                    pe.transpose(bank[s][3][0:H, 0:P], rr[s][:], ident).then_inc(recipsT[k], 1)
                return f

            def spread_out(k, s, pair):
                pe.wait_ge(recipsT_sb[k], n(s, pair))
                mm(bank[s][3][:, P:2 * P], const("headsel")[0:H, :], rrT[s][:]).then_inc(spread[k], 1)

            def head_products(s, v, src):
                for h in range(H):
                    q, a = h // 4, h % 4
                    last = mm(bank[s][0][32 * q:32 * q + 32, 0:P], v[s][:, q, 32 * a:32 * a + 32],
                              src[s][:, h, :], start=(a == 0), stop=(a == 3))
                return last

            def values_(k, v):
                def f(s, pair):
                    pe.wait_ge(probsT_even[k], n(s, pair, 2, 2))
                    pe.wait_ge(probsT_odd[k], n(s, pair, 2, 2))
                    head_products(s, v, pT).then_inc(values[k], 1)
                    spread_out(k, s, pair)
                return f

            def project(k, weight):
                def f(s, pair):
                    pe.wait_ge(oT_ready[k], n(s, pair))
                    mm(bank[s][2][:, 0:P], oT[s][:, 0, :], weight).then_inc(proj[k], 1)
                return f

            def transpose_x(k, b):
                def f(s, pair):
                    pe.wait_ge(normed[k], n(s, pair))
                    pe.transpose(bank[s][b][:, 0:P], x[s][:], ident).then_inc(xT_ps[k], 1)
                return f

            def b_q_(s, pair):
                pe.wait_ge(xT_ready["a"], n(s, pair))
                for c in range(XC):
                    last = mm(bank[s][c // 4][:, (c % 4) * P:(c % 4 + 1) * P],
                              w("c0_wq", c * P, (c + 1) * P), xT[s][:])
                last.then_inc(b_q, 1)

            def b_scores(g):
                def f(s, pair):
                    if g == 0:
                        pe.wait_ge(b_q_lo, n(s, pair))
                        pe.wait_ge(b_q_hi, n(s, pair))
                        pe.wait_ge(x_k0, n(s, pair))
                    for c in (2 * g, 2 * g + 1):
                        last = mm(bank[s][g][:, (c % 2) * 2 * C:(c % 2 + 1) * 2 * C],
                                  q0[s][:, c, :], k0bd[s][:, c, :, :])
                    last.then_inc(scores["b"], 1)
                return f

            def b_values(s, pair):
                pe.wait_ge(probsT_even["b"], n(s, pair, 2, 2))
                pe.wait_ge(probsT_odd["b"], n(s, pair, 2, 2))
                for h in range(H):
                    c, half = h // 2, h % 2
                    last = mm(bank[s][c // 4][half * XH:(half + 1) * XH, (c % 4) * P:(c % 4 + 1) * P],
                              v0[s][:, h, :], pT[s][:, h, :])
                last.then_inc(values["b"], 1)

            def b_out(s, pair):
                pe.wait_ge(oT_ready["b"], n(s, pair))
                pe.wait_ge(oT_ready2, n(s, pair))
                for c in range(XC):
                    last = mm(bank[s][2][:, 0:P], oT[s][:, c, :], w("c0_wo", c * P, (c + 1) * P),
                              start=(c == 0), stop=(c == XC - 1))
                last.then_inc(proj["b"], 1)

            def c_route(s, pair):
                pe.wait_ge(xT_ready["b"], n(s, pair))
                c_weights(s, pair)
                mm(bank[s][3][:, 0:E + 1], xT[s][:], w("m_router")).then_inc(c_logits, 1)

            def c_up_(e):
                def f(s, pair):
                    if e == 0:
                        pe.wait_ge(xT_ready["b"], n(s, pair))
                    for c in range(HC):
                        last = mm(bank[s][e % 2][:, c * P:(c + 1) * P],
                                  w("m_w1", e * HID + c * P, e * HID + (c + 1) * P), xT[s][:])
                    last.then_inc(c_up, 1)
                return f

            def c_rank_(s, pair):
                pe.wait_ge(c_pick, n(s, pair))
                mm(bank[s][3][:, 0:E + 1], const("tri"), picked[s][:], stop=False)
                mm(bank[s][3][:, 0:E + 1], ones[:], routed[:], start=False).then_inc(c_rank, 1)

            def c_down_(e):
                def f(s, pair):
                    pe.wait_ge(c_hid[e % 2], n(s, pair, (E + 1 - e % 2) // 2, e // 2 + 1))
                    if e == 4:
                        pe.wait_ge(c_keep, n(s, pair))
                    for c in range(HC):
                        last = mm(bank[s][2 + e // 4][:, (e % 4) * P:(e % 4 + 1) * P],
                                  hid[e % 2][s][:, c * P:(c + 1) * P],
                                  w("m_w2", (e * HC + c) * P, (e * HC + c + 1) * P),
                                  start=(c == 0), stop=(c == HC - 1))
                    if e in (3, E - 1):
                        last.then_inc(c_down[e // 4], 1)
                return f

            def d_qkv(s, pair):
                pe.wait_ge(xT_ready["c"], n(s, pair))
                mm(bank[s][1][:, 0:P], w("a1_wg", 0, P), xT[s][:])
                mm(bank[s][1][:, P:2 * P], w("a1_wg", P, 2 * P), xT[s][:])
                mm(bank[s][1][:, 2 * P:3 * P], xT[s][:], w("a1_wv")).then_inc(d_gv, 1)
                for i, name in enumerate(("a1_wq", "a1_wk", "a1_wqs", "a1_wks")):
                    last = mm(bank[s][0][:, i * P:(i + 1) * P], w(name), xT[s][:])
                last.then_inc(d_qk, 1)

            def d_rank_(s, pair):
                pe.wait_ge(d_rope, n(s, pair))
                for i, name in enumerate(("a1_rq", "a1_rk")):
                    for c in range(2):
                        last = mm(bank[s][2][:, (2 * i + c) * P:(2 * i + c + 1) * P],
                                  w(name, c * P, (c + 1) * P), qk[s][:, i, :])
                last.then_inc(d_rank, 1)

            def d_scores(g):
                def f(s, pair):
                    pe.wait_ge(d_qkd, n(s, pair, 4, g + 1 if g < 2 else 4))
                    if g == 0:
                        pe.wait_ge(d_v, n(s, pair))
                    for c in range(2):
                        last = mm(bank[s][g][:, c * 2 * P:(c + 1) * 2 * P], kdm[s][:, g, c, :],
                                  qd[s][:, c, :, :])
                    last.then_inc(d_att, 1)
                return f

            def d_values(s, pair):
                pe.wait_ge(d_masked, n(s, pair, 4, 4))
                for h in range(H):
                    c, g, a = h // 8, h % 8 // 2, h % 2
                    q, i = h // 4, h % 4
                    last = mm(bank[s][0][32 * q:32 * q + 32, 0:P], va[s][:, q, 32 * i:32 * i + 32],
                              sc[s][:, 4 * g + 2 * c + a, :], start=(i == 0), stop=(i == 3))
                last.then_inc(values["d"], 1)

            def e_q_(s, pair):
                pe.wait_ge(xT_ready["D"], n(s, pair))
                mm(bank[s][2][:, 0:P], w("c1_wq"), xT[s][:]).then_inc(e_q, 1)

            def e_scores(g):
                def f(s, pair):
                    if g == 0:
                        pe.wait_ge(e_qm, n(s, pair))
                        pe.wait_ge(x_kv1_ready, n(s, pair))
                        if not isinstance(pair, int):
                            pe.wait_ge(r_right, n(s, pair, step=3))
                    mm(bank[s][g][:, 0:4 * C], qm1[s][:, g, :], k1bd[s][:, :, :]).then_inc(scores["e"], 1)
                return f

            def f_in(s, pair):
                pe.wait_ge(f_xq, n(s, pair))
                mm(bank[s][2][:, 0:P], ones[:], diag[s])
                pe.transpose(bank[s][0][:].bitcast(BF16)[:, 0:P], xq[s][:], ident_bf[:]).then_inc(f_xqT, 1)

            def f_up(s, pair):
                pe.wait_ge(f_xqT_sb, n(s, pair))
                for c in range(HC):
                    last = mm(bank[s][2][:, c * P:(c + 1) * P], w1q[:, c * P:(c + 1) * P], xqT[s][:])
                last.then_inc(f_h, 1)

            def f_silu_(s, pair):
                pe.wait_ge(f_silu, n(s, pair))
                for c in range(HC):
                    last = pe.transpose(bank[s][3][:, c * P:(c + 1) * P],
                                        hid[0][s][:, c * P:(c + 1) * P], ident)
                last.then_inc(f_hT, 1)

            def f_quant(s, pair):
                pe.wait_ge(f_hq, n(s, pair))
                for c in range(HC):
                    last = pe.transpose(bank[s][0][:].bitcast(BF16)[:, c * P:(c + 1) * P],
                                        hq[s][:, c * P:(c + 1) * P], ident_bf[:])
                last.then_inc(f_hqT, 1)

            def f_down(s, pair):
                pe.wait_ge(f_hqT_sb, n(s, pair))
                for c in range(HC):
                    last = mm(bank[s][1][:, 0:P], hqT[s][:, c * P:(c + 1) * P],
                              w2q[:, c * P:(c + 1) * P], start=(c == 0), stop=(c == HC - 1))
                last.then_inc(proj["f"], 1)

            run(pe, {
                "weights": more_weights, "ternary": ternary, "ternary_over": ternary_over,
                **{f"rel{g}": rel_scores(g) for g in range(4)}, "rel_last": rel_last,
                "keys_k": keys_k, "keys_v": keys_v, "keys1": keys1, "a_qkv": a_qkv_, 
                **{f"a_s{g}": a_scores(g) for g in range(4)},
                **{f"a_t{g}": transposes("a", exped["a"], g) for g in range(4)}, "a_sums": sums("a"), "a_values": values_("a", va),
                "a_out": project("a", w("a0_wo")), "a_norm": transpose_x("a", 3),
                "b_q": b_q_, **{f"b_s{g}": b_scores(g) for g in range(4)},
                **{f"b_t{g}": transposes("b", b_scaled, g) for g in range(4)}, "b_values": b_values,
                "b_out": b_out, "b_norm": transpose_x("b", 3),
                "c_route": c_route, "c_rank": c_rank_,
                **{f"c_up{e}": c_up_(e) for e in range(E)},
                **{f"c_down{e}": c_down_(e) for e in range(E)},
                "c_norm": transpose_x("c", 0),
                "d_qkv": d_qkv, "d_rank": d_rank_, **{f"d_s{g}": d_scores(g) for g in range(4)}, "d_values": d_values,
                "d_out": project("d", w("a1_wo")), "d_norm": transpose_x("D", 2),
                "e_q": e_q_, **{f"e_s{g}": e_scores(g) for g in range(4)},
                **{f"e_t{g}": transposes("e", exped["e"], g) for g in range(4)}, "e_sums": sums("e"),
                "e_values": values_("e", ve), "e_out": project("e", w("c1_wo")),
                "f_in": f_in, "f_up": f_up, "f_silu": f_silu_, "f_quant": f_quant, "f_down": f_down,
            })

        @block.scalar
        def _(act):
            A = nc.scalar
            n = counter(act)
            act.preload_act_table_set("natural_log_exp_and_others")
            steps = [0]

            def step(ins):
                steps[0] += 1
                ins.then_inc(act_step, 1)
                act.wait_ge(act_step, steps[0])

            def clear():
                act.sem_clear(act_step)
                steps[0] = 0

            act.wait_ge(ld_w, 48)
            act.wait_ge(pre_dve, 1)
            dlo = C_AT["a1_decay"][0]
            step(A.activation(loglam[:], col_sb[:, dlo:dlo + 2], ACT.Exp, scale=-1.0))
            step(A.activation(nloglam[:], loglam[:], ACT.Ln, bias=1.0))
            step(A.activation(loglam[:], nloglam[:], ACT.Copy, scale=-1.0))
            for c in range(2):
                A.activation(dq[:, c, :], const("time"), ACT.Exp, scale=loglam[:, c:c + 1])
                last = A.activation(dk[:, c, :], const("time"), ACT.Exp, scale=nloglam[:, c:c + 1])
            last.then_inc(pre_act, 1)

            def queries(came, b, dst, ready, biases):
                def f(s, pair):
                    act.wait_ge(came, n(s, pair))
                    for g in range(4):
                        last = A.activation(dst[s][:, g, :], bank[s][b][:, 0:P], ACT.Identity,
                                            bias=biases[:, g:g + 1], scale=const("group32", g, g + 1))
                    last.then_inc(ready, 1)
                return f

            def rel_mid(g):
                def f(s, pair):
                    if g == 0:
                        act.wait_ge(st_rel, n(s, pair, per=16, step=0))
                    act.wait_ge(r_s, n(s, pair, 4, g + 1))
                    A.activation(rext[:, 4 * g:4 * g + 4, MAX_REL - 1:MAX_REL - 1 + P],
                                 bank[s][REL_BANK[g]][:].rearrange("p (a r) -> p a r", a=4),
                                 ACT.Copy).then_inc(r_mid, 1)
                return f

            def keys_k(s, pair):
                act.wait_ge(x_keys, n(s, pair))
                for half in range(2):
                    part = slice(half * XH, half * XH + XH)
                    for b in range(2):
                        last = A.activation(
                            k0bd[s][part, 4 * b:4 * b + 4, half, :],
                            bank[s][KEY_BANK[b]][part, 0:4 * CP].rearrange("p (c j) -> p c j", c=4)[:, :, 0:C],
                            ACT.Copy, scale=XH ** -0.5)
                last.then_inc(x_k0, 1)

            def exps(k, g):
                def f(s, pair):
                    act.wait_ge(maxed[k], n(s, pair, 4, g + 1))
                    for a in range(4):
                        h = 4 * g + a
                        dst = (sc if k == "a" else scx)[s][:, h, :]
                        src = dst if k == "a" else bank[s][g][:, a * C:(a + 1) * C]
                        last = A.activation(dst, src, ACT.Exp, bias=nmx[s][:, h:h + 1],
                                            accum_out=psum_[s][:, h:h + 1])
                    last.then_inc(exped[k], 1)
                return f

            def copy_probsT(k, nk, g):
                def f(s, pair):
                    act.wait_ge(probsT[k], n(s, pair, 4, g + 1))
                    A.activation(pT[s][0:nk, 4 * g:4 * g + 4, :], bank[s][g][0:nk, :].rearrange(
                        "p (a i) -> p a i", a=4), ACT.Copy).then_inc(probsT_even[k], 1)
                return f

            def sums(k):
                def f(s, pair):
                    act.wait_ge(recipsT[k], n(s, pair))
                    A.activation(rrT[s][:], bank[s][3][0:H, 0:P], ACT.Copy).then_inc(recipsT_sb[k], 1)
                return f

            def spreads(k):
                def f(s, pair):
                    act.wait_ge(spread[k], n(s, pair))
                    A.activation(rbc[s][:], bank[s][3][:, P:2 * P], ACT.Copy).then_inc(spread_sb[k], 1)
                return f

            def copy_T(ps, dst, b, ready):
                def f(s, pair):
                    act.wait_ge(ps, n(s, pair))
                    A.activation(dst(s), bank[s][b][:, 0:P], ACT.Copy).then_inc(ready, 1)
                return f

            def deviation(k):
                def f(s, pair):
                    act.wait_ge(var[k], n(s, pair))
                    step(A.activation(lnv[s][:], mv[s][:, 1:2], ACT.Ln, bias=eps[:]))
                    A.activation(rstd[s][:], lnv[s][:], ACT.Exp, scale=-0.5).then_inc(inv[k], 1)
                return f

            def f_down(s, pair):
                act.wait_ge(var["f"], n(s, pair))
                A.activation(lnv[s][:], mv[s][:, 1:2], ACT.Ln, bias=eps[:]).then_inc(banks_free, 1)
                act.wait_ge(banks_free, n(s, pair, step=3))
                A.activation(rstd[s][:], lnv[s][:], ACT.Exp, scale=-0.5).then_inc(inv["f"], 1)

            def both(*fs):
                def f(s, pair):
                    for part in fs:
                        part(s, pair)
                return f

            def copy_wide(came, dst, ready):
                def f(s, pair):
                    act.wait_ge(came, n(s, pair))
                    A.activation(dst[s][:, 0:4, :], bank[s][0][:].rearrange("p (c i) -> p c i", c=4),
                                 ACT.Copy).then_inc(ready, 1)
                return f

            def c_exp_(s, pair):
                act.wait_ge(c_shift, n(s, pair))
                A.activation(lg[s][:], lg[s][:], ACT.Exp, bias=nmax[s][:],
                             accum_out=esum[s][:]).then_inc(c_exp, 1)

            def hidden(e):
                def f(s, pair):
                    act.wait_ge(c_up, n(s, pair, E, e + 1))
                    A.activation(hid[0][s], bank[s][0][:], ACT.Relu).then_inc(c_hid[e % 2], 1)
                return f

            def d_gates(s, pair):
                act.wait_ge(d_gv, n(s, pair))
                for c in range(2):
                    last = A.activation(eg[s][:, c, :], bank[s][1][:, c * P:(c + 1) * P], ACT.Exp,
                                        bias=ngb[:, c:c + 1], scale=-1.0)
                last.then_inc(d_gate0, 1)
                A.activation(heads(va[s]), by_head(bank[s][1][:, 2 * P:3 * P]), ACT.Copy).then_inc(d_v, 1)
                act.wait_ge(d_gate1, n(s, pair))
                step(A.activation(eg[s], eg[s], ACT.Ln))
                A.activation(eg[s], eg[s], ACT.Exp, scale=-1.0).then_inc(d_gate, 1)

            def f_in(s, pair):
                act.wait_ge(f_xqT, n(s, pair))
                A.activation(scbc[s], bank[s][2][:, 0:P], ACT.Copy, scale=wmean[:, 0:1])
                A.activation(xqT[s][:], bank[s][0][:].bitcast(BF16)[:, 0:P], ACT.Copy
                             ).then_inc(f_xqT_sb, 1)

            def f_conv_(s, pair):
                act.wait_ge(f_hp, n(s, pair))
                for c in range(HC):
                    last = A.activation(hid[0][s][:, c * P:(c + 1) * P], hp[s][:, c, 1:P + 1],
                                        ACT.Identity, bias=col("f_convb", c),
                                        scale=col("f_conv", 3 * c + 1))
                last.then_inc(f_conv0, 1)

            def f_silu_(s, pair):
                act.wait_ge(f_conv, n(s, pair))
                A.activation(hid[1][s], hid[0][s], ACT.Exp, scale=-1.0).then_inc(f_exp, 1)
                act.wait_ge(f_exp1, n(s, pair))
                step(A.activation(hid[1][s], hid[1][s], ACT.Ln))
                A.activation(hid[1][s], hid[1][s], ACT.Exp, scale=-1.0).then_inc(f_sig, 1)

            def f_quant(s, pair):
                act.wait_ge(f_hqT, n(s, pair))
                A.activation(hqT[s], bank[s][0][:].bitcast(BF16)[:, 0:HID], ACT.Copy
                             ).then_inc(f_hqT_sb, 1)

            act.wait_ge(pre_pool, N_POOL)
            for s in range(2):
                A.activation(lnv[s][:], eps[:], ACT.Copy).then_inc(banks_free, 1)
            xT_of = lambda s: xT[s][:]
            run(act, {
                **{f"rel{g}": rel_mid(g) for g in range(4)}, "keys_k": keys_k, "a_qkv": queries(a_qkv, 3, qm, a_qm, bqm0),
                **{f"a_s{g}": exps("a", g) for g in range(4)}, **{f"a_t{g}": copy_probsT("a", P, g) for g in (0, 2)}, "a_sums": sums("a"),
                "a_values": spreads("a"),
                "a_out": deviation("a"), "a_norm": copy_T(xT_ps["a"], xT_of, 3, xT_ready["a"]),
                "b_q": copy_wide(b_q, q0, b_q_lo), **{f"b_s{g}": exps("b", g) for g in range(4)},
                **{f"b_t{g}": copy_probsT("b", C, g) for g in (0, 2)}, "b_values": copy_wide(values["b"], oT, oT_ready["b"]),
                "b_out": deviation("b"), "b_norm": copy_T(xT_ps["b"], xT_of, 3, xT_ready["b"]),
                "c_route": c_exp_, **{f"c_up{e}": hidden(e) for e in range(0, E, 2)},
                "c_norm": both(deviation("c"), copy_T(xT_ps["c"], xT_of, 0, xT_ready["c"])),
                "d_qkv": d_gates, "d_values": copy_T(values["d"], lambda s: oT[s][:, 0, :], 0,
                                                     oT_ready["d"]),
                "d_out": both(deviation("d"), deviation("D")),
                "d_norm": copy_T(xT_ps["D"], xT_of, 2, xT_ready["D"]),
                "e_q": queries(e_q, 2, qm1, e_qm, bqm1), **{f"e_s{g}": exps("e", g) for g in range(4)},
                **{f"e_t{g}": copy_probsT("e", C, g) for g in (0, 2)}, "e_sums": sums("e"), "e_values": spreads("e"),
                "e_out": deviation("e"),
                "ternary_over": lambda s, pair: act.wait_ge(pre_dve, 4),
                "f_in": f_in, "f_conv": f_conv_, "f_silu": f_silu_, "f_quant": f_quant,
                "f_down": f_down,
            }, clear)

        @block.vector
        def _(dve):
            V = nc.vector
            n = counter(dve)
            steps = [0]

            def mark(ins):
                steps[0] += 1
                ins.then_inc(dve_step, 1)
                return steps[0]

            def after(count):
                dve.wait_ge(dve_step, count)

            def step(ins):
                after(mark(ins))

            def clear():
                dve.sem_clear(dve_step)
                steps[0] = 0

            dve.wait_ge(ld_w, 48)
            step(V.tensor_scalar(ngb[:], col_sb[:, C_AT["a1_gb"][0]:C_AT["a1_gb"][1]], -1.0, None, ALU.mult))
            step(V.tensor_scalar(bqm0[:], const("group32"), col("a0_bq"), None, ALU.mult))
            step(V.tensor_scalar(bqm1[:], const("group32"), col("c1_bq"), None, ALU.mult))
            V.tensor_scalar(head8s[:], const("head8"), DH ** -0.5, None, ALU.mult).then_inc(pre_dve, 1)
            dve.wait_ge(pre_act, 1)
            for c in range(2):
                for a in range(2):
                    V.tensor_scalar(dqm[:, c, a, :], dq[:, c, :], const("head16", a, a + 1), None, ALU.mult)
            step(V.tensor_scalar(dk[:], dk[:], DH ** -0.5, None, ALU.mult))
            def ternary_sum(s, pair):
                dve.wait_ge(ld_part[2], 16)
                step(V.tensor_reduce(wabs[:, 0:1], w("f_w1"), AX.X, ALU.add, apply_absolute_value=True))
                V.tensor_reduce(wabs[:, 1:2], w("f_w2"), AX.X, ALU.add, apply_absolute_value=True
                                ).then_inc(pre_dve, 1)

            def ternary(s, pair):
                dve.wait_ge(pre_pe, 1)
                V.tensor_scalar(wmean[:], bank[1][0][:, 0:2], 1.0 / (P * HID), 1e-5, ALU.mult, ALU.max
                                ).then_inc(pre_dve, 1)
                dve.wait_ge(pre_dve, 3)
                step(V.reciprocal(wscale[:], wmean[:]))
                wtmp = q0[1][:, 0:4, :].rearrange("p h i -> p (h i)")
                for i, (name, dst) in enumerate((("f_w1", w1q), ("f_w2", w2q))):
                    step(V.tensor_scalar(wtmp, w(name), wscale[:, i:i + 1], ROUND, ALU.mult, ALU.add))
                    step(V.tensor_scalar(wtmp, wtmp, ROUND, 1.0, ALU.subtract, ALU.min))
                    step(V.tensor_scalar(dst[:], wtmp, -1.0, None, ALU.max))
                V.tensor_copy(ident_bf[:], ident).then_inc(pre_dve, 1)

            def rel_right(s, pair):
                dve.wait_ge(r_last, n(s, pair))
                V.tensor_copy(rext[:, :, MAX_REL - 1 + P:M], bank[s][0][:, 0:H].unsqueeze(2)
                              .broadcast_to([P, H, MAX_REL])).then_inc(r_right, 1)

            def keys_v(s, pair):
                dve.wait_ge(x_values, n(s, pair))
                for c in range(2):
                    last = V.tensor_copy(v0[s][0:C, 8 * c:8 * c + 8, :], bank[s][KEY_BANK[c]][0:C, :].rearrange(
                        "p (h d) -> p h d", d=XH))
                last.then_inc(x_v0, 1)

            def keys1(s, pair):
                dve.wait_ge(x_kv1, n(s, pair))
                for a in range(4):
                    V.tensor_scalar(k1bd[s][:, a, :], bank[s][3][:, 0:C], col("c1_bk"),
                                    head8s[:, a:a + 1], ALU.add, ALU.mult)
                V.tensor_tensor(heads(ve[s])[0:C], by_head(bank[s][3][0:C, P:2 * P]),
                                by_head(row("c1_bv")[0:C, :]), ALU.add).then_inc(x_kv1_ready, 1)

            def a_kv_(s, pair):
                dve.wait_ge(a_qkv, n(s, pair))
                for a in range(4):
                    V.tensor_scalar(kbd[s][:, a, :], bank[s][1][:, P:2 * P], col("a0_bk"),
                                    head8s[:, a:a + 1], ALU.add, ALU.mult)
                V.tensor_tensor(heads(va[s]), by_head(bank[s][1][:, 2 * P:3 * P]), by_head(row("a0_bv")),
                                ALU.add).then_inc(a_kv, 1)

            def maxima(k, g):
                def f(s, pair):
                    nk = P if k == "a" else C
                    ps = bank[s][g][:, 0:4 * nk].rearrange("p (a j) -> p a j", a=4)
                    dve.wait_ge(scores[k], n(s, pair, 4, g + 1))
                    if k == "a":
                        if g == 0:
                            dve.wait_ge(ld_rel, n(s, pair, 32))
                        dst = sc[s][:, 4 * g:4 * g + 4, :]
                        step(V.tensor_tensor(dst, ps, rel[:, 4 * g:4 * g + 4, :], ALU.add))
                        ps = dst
                    V.tensor_reduce(nmx[s][:, 4 * g:4 * g + 4], ps, AX.X, ALU.max, negate=True
                                    ).then_inc(maxed[k], 1)
                return f

            def copy_probsT(k, nk, g):
                def f(s, pair):
                    dve.wait_ge(probsT[k], n(s, pair, 4, g + 1))
                    V.tensor_copy(pT[s][0:nk, 4 * g:4 * g + 4, :], bank[s][g][0:nk, :].rearrange(
                        "p (a i) -> p a i", a=4)).then_inc(probsT_odd[k], 1)
                return f

            def b_scale(g):
                def f(s, pair):
                    dve.wait_ge(exped["b"], n(s, pair, 4, g + 1))
                    part = slice(4 * g, 4 * g + 4)
                    step(V.reciprocal(rr[s][:, part], psum_[s][:, part]))
                    V.tensor_tensor(scx[s][:, part, :], scx[s][:, part, :], rr[s][:, part].unsqueeze(2)
                                    .broadcast_to([P, 4, C]), ALU.mult).then_inc(b_scaled, 1)
                return f

            def sums(k):
                def f(s, pair):
                    dve.wait_ge(exped[k], n(s, pair, 4, 4))
                    V.reciprocal(rr[s][:], psum_[s][:]).then_inc(recips[k], 1)
                return f

            def normalise(k):
                def f(s, pair):
                    dve.wait_ge(values[k], n(s, pair))
                    dve.wait_ge(spread_sb[k], n(s, pair))
                    V.tensor_tensor(oT[s][:, 0, :], bank[s][0][:, 0:P], rbc[s][:], ALU.mult
                                    ).then_inc(oT_ready[k], 1)
                return f

            def moments(k, s):
                step(V.bn_stats(stats[s][:], y[s][:]))
                V.bn_aggr(mv[s][:], stats[s][:]).then_inc(var[k], 1)

            def norm(k, s, pair, dst):
                dve.wait_ge(inv[k], n(s, pair))
                V.tensor_scalar(dst[s][:], y[s][:], mv[s][:, 0:1], rstd[s][:, 0:1], ALU.subtract,
                                ALU.mult).then_inc(normed[k], 1)

            def add_norm(k, other, ready, per):
                def f(s, pair):
                    dve.wait_ge(ready, n(s, pair, per))
                    dve.wait_ge(proj[k], n(s, pair))
                    step(V.tensor_tensor(y[s][:], bank[s][2][:, 0:P], other[s][:], ALU.add))
                    moments(k, s)
                    if k != "d":
                        norm(k, s, pair, x)
                        return
                    dve.wait_ge(inv["d"], n(s, pair))
                    step(V.tensor_scalar(y2[s][:], y[s][:], mv[s][:, 0:1], rstd[s][:, 0:1], ALU.subtract,
                                         ALU.mult))
                    step(V.tensor_tensor(y2[s][:], y2[s][:], row("a1_lng"), ALU.mult))
                    step(V.tensor_tensor(y[s][:], y2[s][:], xb2[s][:], ALU.add))
                    moments("D", s)
                    norm("D", s, pair, x)
                return f

            def copy_wide(came, dst, ready):
                def f(s, pair):
                    dve.wait_ge(came, n(s, pair))
                    V.tensor_copy(dst[s][:, 4:8, :], bank[s][1][:].rearrange("p (c i) -> p c i", c=4)
                                  ).then_inc(ready, 1)
                return f

            def c_route(s, pair):
                dve.wait_ge(c_logits, n(s, pair))
                step(V.tensor_tensor(lg[s][:], bank[s][3][:, 0:E + 1], row("m_rb"), ALU.add))
                step(V.max(top[s][:], lg[s][:]))
                V.tensor_scalar(nmax[s][:], top[s][:, 0:1], -1.0, None, ALU.mult).then_inc(c_shift, 1)

            def hidden(e):
                def f(s, pair):
                    dve.wait_ge(c_up, n(s, pair, E, e + 1))
                    V.tensor_scalar(hid[1][s], bank[s][1][:], 0.0, None, ALU.max).then_inc(c_hid[e % 2], 1)
                return f

            def c_pick_(s, pair):
                dve.wait_ge(c_exp, n(s, pair))
                step(V.reciprocal(esum[s][:], esum[s][:]))
                step(V.tensor_scalar(wts[s][:], lg[s][:], esum[s][:, 0:1], None, ALU.mult))
                step(V.max(top[s][:], wts[s][:]))
                step(V.max_index(topi[s][:], top[s][:], wts[s][:]))
                step(V.tensor_copy(topf[s][:], topi[s][:, 0:2]))
                mark(V.tensor_scalar(sel[s][:], const("expert"), topf[s][:, 0:1], None, ALU.is_equal))
                step(V.tensor_scalar(sel2[s][:], const("expert"), topf[s][:, 1:2], None, ALU.is_equal))
                step(V.tensor_tensor(sel[s][:], sel[s][:], sel2[s][:], ALU.add))
                V.scalar_tensor_tensor(out=picked[s][:], in0=wts[s][:], scalar=0.0, in1=sel[s][:],
                                       op0=ALU.is_gt, op1=ALU.mult).then_inc(c_pick, 1)
                dve.wait_ge(c_pick, n(s, pair))
                step(V.tensor_tensor(sel2[s][:], wts[s][:], picked[s][:], ALU.mult))

            def c_keep_(s, pair):
                dve.wait_ge(c_rank, n(s, pair))
                V.tensor_tensor(keep[s][:], bank[s][3][:, 0:E + 1], const("cap"), ALU.is_lt
                                ).then_inc(c_keep, 1)
                dve.wait_ge(c_keep, n(s, pair))
                mark(V.tensor_tensor(routed[:], routed[:], picked[s][:], ALU.add))
                step(V.tensor_tensor(keep[s][:], keep[s][:], sel2[s][:], ALU.mult))
                step(V.tensor_scalar(wpass[s][:], keep[s][:, E:E + 1], 1.0, None, ALU.add))
                step(V.tensor_scalar(y[s][:], x[s][:], wpass[s][:, 0:1], None, ALU.mult))

            def combine(s, pair, e0, e1):
                dve.wait_ge(c_down[e0 // 4], n(s, pair))
                for e in range(e0, e1):
                    step(V.scalar_tensor_tensor(
                        out=y[s][:], in0=bank[s][2 + e // 4][:, (e % 4) * P:(e % 4 + 1) * P],
                        scalar=keep[s][:, e:e + 1], in1=y[s][:], op0=ALU.mult, op1=ALU.add))

            def c_norm(s, pair):
                combine(s, pair, 4, E)
                moments("c", s)
                norm("c", s, pair, x)

            def d_qkv(s, pair):
                dve.wait_ge(d_gate0, n(s, pair))
                V.tensor_scalar(eg[s], eg[s], EXP_MAX, 1.0, ALU.min, ALU.add).then_inc(d_gate1, 1)
                dve.wait_ge(d_qk, n(s, pair))
                for i, (t, table) in enumerate(((t1, "cos"), (t2, "sin"))):
                    last = V.tensor_tensor(t[s], bank[s][0][:, i * 2 * P:(i + 1) * 2 * P].rearrange(
                        "p (a t) -> p a t", a=2), const(table).unsqueeze(1).broadcast_to([P, 2, P]),
                        ALU.mult)
                step(last)
                V.tensor_tensor(qk[s], t1[s], t2[s], ALU.add).then_inc(d_rope, 1)
                dve.wait_ge(d_gate, n(s, pair))
                step(V.tensor_tensor(eg[s], eg[s], dk[:], ALU.mult))

            def d_rank_(s, pair):
                dve.wait_ge(d_rank, n(s, pair))
                kr = bank[s][2][:, 2 * P:4 * P].rearrange("p (c t) -> p c t", c=2)
                for c in range(2):
                    mark(V.tensor_tensor(qd[s][:, c, :, :], bank[s][2][:, c * P:(c + 1) * P].unsqueeze(1)
                                         .broadcast_to([P, 2, P]), dqm[:, c, :, :], ALU.mult))
                for g in range(4):
                    V.scalar_tensor_tensor(out=kdm[s][:, g, :, :], in0=kr, scalar=const("group32", g, g + 1),
                                           in1=eg[s], op0=ALU.mult, op1=ALU.mult).then_inc(d_qkd, 1)

            def d_scores(g):
                def f(s, pair):
                    dve.wait_ge(d_att, n(s, pair, 4, g + 1))
                    V.tensor_tensor(sc[s][:, 4 * g:4 * g + 4, :], bank[s][g][:].rearrange(
                        "p (a t) -> p a t", a=4), const("causal").unsqueeze(1).broadcast_to([P, 4, P]),
                        ALU.mult).then_inc(d_masked, 1)
                return f

            def quantise(s, src, c0, dst):
                step(V.tensor_reduce(scol[s][:, c0:c0 + 1], src, AX.X, ALU.max,
                                     apply_absolute_value=True))
                step(V.tensor_scalar(scol[s][:, c0 + 1:c0 + 2], scol[s][:, c0:c0 + 1], 1e-5, 1.0 / QMAX,
                                     ALU.max, ALU.mult))
                step(V.reciprocal(scol[s][:, c0 + 2:c0 + 3], scol[s][:, c0 + 1:c0 + 2]))
                tmp = probs_sb[s][:, 0:dst.shape[-1]]
                step(V.tensor_scalar(tmp, src, scol[s][:, c0 + 2:c0 + 3], ROUND, ALU.mult, ALU.add))
                return V.tensor_scalar(dst, tmp, ROUND, None, ALU.subtract)

            def f_in(s, pair):
                dve.wait_ge(normed["e"], n(s, pair))
                step(quantise(s, x[s][:], 0, xq[s][:]))
                V.tensor_scalar(diag[s], ident, scol[s][:, 1:2], None, ALU.mult).then_inc(f_xq, 1)

            def f_up(s, pair):
                dve.wait_ge(f_h, n(s, pair))
                V.tensor_tensor(hp[s][:, :, 1:P + 1], bank[s][2][:].rearrange("p (c t) -> p c t", c=HC),
                                scbc[s].unsqueeze(1).broadcast_to([P, HC, P]), ALU.mult
                                ).then_inc(f_hp, 1)

            def f_conv_(s, pair):
                dve.wait_ge(f_conv0, n(s, pair))
                for tap in (0, 2):
                    for c in range(HC):
                        hc = hid[0][s][:, c * P:(c + 1) * P]
                        last = V.scalar_tensor_tensor(
                            out=hc, in0=hp[s][:, c, tap:tap + P], scalar=col("f_conv", 3 * c + tap),
                            in1=hc, op0=ALU.mult, op1=ALU.add)
                    if tap == 0:
                        step(last)
                last.then_inc(f_conv, 1)

            def f_silu_(s, pair):
                dve.wait_ge(f_exp, n(s, pair))
                V.tensor_scalar(hid[1][s], hid[1][s], EXP_MAX, 1.0, ALU.min, ALU.add).then_inc(f_exp1, 1)
                dve.wait_ge(f_sig, n(s, pair))
                V.tensor_tensor(hid[0][s], hid[0][s], hid[1][s], ALU.mult).then_inc(f_silu, 1)

            def f_quant(s, pair):
                dve.wait_ge(f_hT, n(s, pair))
                quantise(s, bank[s][3][:], 3, hq[s]).then_inc(f_hq, 1)
                dve.wait_ge(f_hq, n(s, pair))
                step(V.tensor_tensor(scol[s][:, 6:7], scol[s][:, 4:5], wmean[:, 1:2], ALU.mult))

            def f_down(s, pair):
                dve.wait_ge(proj["f"], n(s, pair))
                step(V.scalar_tensor_tensor(out=y[s][:], in0=bank[s][1][:, 0:P], scalar=scol[s][:, 6:7],
                                            in1=x[s][:], op0=ALU.mult, op1=ALU.add))
                moments("f", s)

            def f_norm(s, pair):
                norm("f", s, pair, out_sb)

            dve.wait_ge(pre_pool, N_POOL)
            run(dve, {
                "ternary_sum": ternary_sum, "ternary": ternary, "rel_last": rel_right, "keys_v": keys_v, "keys1": keys1, "a_qkv": a_kv_,
                **{f"a_s{g}": maxima("a", g) for g in range(4)}, **{f"a_t{g}": copy_probsT("a", P, g) for g in (1, 3)}, "a_sums": sums("a"),
                "a_values": normalise("a"), "a_out": add_norm("a", xb, xb_ready["a"], 1),
                "b_q": copy_wide(b_q, q0, b_q_hi), **{f"b_s{g}": maxima("b", g) for g in range(4)}, **{f"b_t{g}": copy_probsT("b", C, g) for g in (1, 3)},
                **{f"b_u{g}": b_scale(g) for g in range(4)},
                "b_values": copy_wide(values["b"], oT, oT_ready2),
                "b_out": add_norm("b", x, normed["a"], 1),
                "c_route": c_route, "c_pick": c_pick_, "c_keep": c_keep_,
                **{f"c_up{e}": hidden(e) for e in range(1, E, 2)},
                "c_down3": lambda s, pair: combine(s, pair, 0, 4),
                "c_norm": c_norm,
                "d_qkv": d_qkv, "d_rank": d_rank_, **{f"d_s{g}": d_scores(g) for g in range(4)},
                "d_out": add_norm("d", xb, xb_ready["d"], 2),
                **{f"e_s{g}": maxima("e", g) for g in range(4)}, **{f"e_t{g}": copy_probsT("e", C, g) for g in (1, 3)}, "e_sums": sums("e"),
                "e_values": normalise("e"), "e_out": add_norm("e", xb, xb_ready["e"], 1),
                "f_in": f_in, "f_up": f_up, "f_conv": f_conv_, "f_silu": f_silu_, "f_quant": f_quant,
                "f_down": f_down, "f_norm": f_norm,
            }, clear)


N_POOL = 3 + 2 * 6


def tables():
    p, t = np.arange(P)[:, None], np.arange(P)[None, :]
    half = DH // 2
    freq = (1.0 / 10000.0 ** (np.arange(half, dtype=np.float32) / np.float32(half))).astype(np.float32)
    angle = (np.arange(P, dtype=np.float32)[None, :] * freq[(np.arange(P) % DH) // 2][:, None]).astype(np.float32)
    sign = np.where(p % 2 == 0, -1.0, 1.0)
    parts = {
        "ident": p == t,
        "tri": p < t,
        "causal": p <= t,
        "cos": np.cos(angle), "sin": np.sin(angle) * sign,
        "time": np.broadcast_to(t - MID, (P, P)),
        "headsel": t // DH == p,
        "head8": (p // DH) % 4 == np.arange(4),
        "group32": p // 32 == np.arange(4),
        "head16": (p // R) % 2 == np.arange(2),
        "expert": np.broadcast_to(np.arange(E + 1), (P, E + 1)),
        "cap": np.broadcast_to(np.where(np.arange(E + 1) < E, CAP, 2 * B * P), (P, E + 1)),
    }
    return np.concatenate([np.asarray(parts[k], np.float32) for k in CONSTS], axis=1)


def kernel(**inputs):
    import concourse.bacc as bacc
    from concourse.bass_utils import run_bass_kernel_spmd

    g = {k: np.asarray(v) for k, v in inputs.items()}

    def by_rows(a, chunk=P):
        return a.reshape(-1, chunk, a.shape[1]).transpose(1, 0, 2).reshape(chunk, -1)

    tab = g["L0_attn_rel_table"]
    rel_bd = np.zeros((4, 4, DH, 4, P), np.float32)
    rel_last = np.zeros((4, 4, DH, 4, H), np.float32)
    for grp in range(4):
        for a in range(4):
            rel_bd[grp, a, :, a, :] = tab[:2 * MAX_REL].T
            rel_last[grp, a, :, grp, 4 * grp + a] = tab[2 * MAX_REL]
    rank = {}
    for name in ("Wq", "Wk"):
        bd = np.zeros((H, DH, H, R), np.float32)
        for h in range(H):
            bd[h, :, h, :] = g[f"L1_attn_{name}"][h].T
        rank[name] = bd.reshape(P, H * R)
    swap = np.arange(P) ^ 1
    inw = g["L1_xattn_in_proj_weight"]
    weights = {
        "a0_wq": g["L0_attn_Wq"], "a0_wk": g["L0_attn_Wk"], "a0_wv": g["L0_attn_Wv"],
        "a0_wo": g["L0_attn_Wo"], "a0_rel": rel_bd.reshape(P, 4 * P), "a0_rel_last": rel_last.reshape(P, 4 * H),
        "c0_wq": g["L0_xattn_Wq"], "c0_wk": g["L0_xattn_Wk"], "c0_wv": g["L0_xattn_Wv"],
        "c0_wo": by_rows(g["L0_xattn_Wo"]),
        "m_router": g["L0_ffn_router_w"].T,
        "m_w1": g["L0_ffn_experts_inter"].transpose(1, 0, 2).reshape(P, -1),
        "m_w2": by_rows(g["L0_ffn_experts_out"].reshape(E * HID, P)),
        "a1_wq": g["L1_attn_q_w"].T, "a1_wqs": g["L1_attn_q_w"][swap].T,
        "a1_wk": g["L1_attn_k_w"].T, "a1_wks": g["L1_attn_k_w"][swap].T,
        "a1_wv": g["L1_attn_v_w"].T, "a1_wg": g["L1_attn_g_w"].T,
        "a1_rq": rank["Wq"], "a1_rk": rank["Wk"], "a1_wo": g["L1_attn_out_w"].T,
        "c1_wq": inw[0:P].T, "c1_wk": inw[P:2 * P].T, "c1_wv": inw[2 * P:3 * P].T,
        "c1_wo": g["L1_xattn_out_proj_weight"].T,
        "f_w1": g["L1_ffn_w1"].T, "f_w2": by_rows(g["L1_ffn_w2"].T),
    }
    inb = g["L1_xattn_in_proj_bias"]
    columns = {
        "a0_bq": g["L0_attn_bq"].reshape(P, 1), "a0_bk": g["L0_attn_bk"].reshape(P, 1),
        "c1_bq": inb[0:P].reshape(P, 1), "c1_bk": inb[P:2 * P].reshape(P, 1),
        "a1_gb": g["L1_attn_g_b"].reshape(2, P).T,
        "a1_decay": g["L1_attn_base_decay_logits"].reshape(2, P).T,
        "f_conv": by_rows(g["L1_ffn_conv_w"].reshape(HID, 3)),
        "f_convb": g["L1_ffn_conv_b"].reshape(HC, P).T,
    }
    rows = {
        "a0_bv": g["L0_attn_bv"], "a0_bo": g["L0_attn_bo"], "m_rb": g["L0_ffn_router_b"],
        "a1_bo": g["L1_attn_out_b"], "a1_lng": g["L1_attn_ln_g"], "a1_lnb": g["L1_attn_ln_b"],
        "c1_bv": inb[2 * P:3 * P], "c1_bo": g["L1_xattn_out_proj_bias"],
    }
    arrays = {
        "x": g["x"].reshape(NP, 2, P, P),
        "xT": g["x"].transpose(0, 2, 1).reshape(NP, 2, P, P),
        "cT": g["ctx_1024"].transpose(0, 2, 1).reshape(NP, 2, P, C),
        "weights": np.concatenate([weights[k] for k in WEIGHTS], axis=1),
        "columns": np.concatenate([columns[k] for k in COLUMNS], axis=1),
        "rows": np.concatenate([rows[k] for k in ROWS]),
        "consts": tables(),
    }
    arrays = {k: np.ascontiguousarray(v) for k, v in arrays.items()}
    nc = bacc.Bacc("TRN2", target_bir_lowering=False, num_devices=1)
    args = [nc.dram_tensor(k, v.shape, F32, kind="ExternalInput").ap() for k, v in arrays.items()]
    out = nc.dram_tensor("out", (NP, 2, P, P), F32, kind="ExternalOutput").ap()
    rel_dram = nc.dram_tensor("rel_dram", (NP, 2, P * RROW), F32, kind="Internal").ap()
    decoder(nc, *args, out, rel_dram)
    r = run_bass_kernel_spmd(nc, [arrays], core_ids=[0])
    return r.results[0]["out"].reshape(B, P, P)
```

```python
from contextlib import ExitStack

import numpy as np

import concourse.bass as bass
from concourse import mybir

F32 = mybir.dt.float32
BF16 = mybir.dt.bfloat16
U32 = mybir.dt.uint32
ALU = mybir.AluOpType
ACT = mybir.ActivationFunctionType
AX = mybir.AxisListType

P = 128
B = 16
NP = B // 2
C = 77
H = 16
DH = P // H
XH = 64
XC = H * XH // P
MAX_REL = 64
M = 2 * P - 1
RROW = H * M
E = 7
HID = 512
HC = HID // P
CAP = B * P // (E + 1)
R = 16
MID = P // 2
EPS = 1e-5
CP = 96
EXP_MAX = 1e18
KEY_BANK = (1, 3)
HALVES = (slice(0, HID // 2), slice(HID // 2, HID))
REL_BANK = (3, 0, 1, 3)
ROUND = 1.5 * 2.0 ** 23
QMAX = 127.0

WEIGHTS = {
    "a0_wq": P, "a0_wk": P, "a0_wv": P, "a0_rel": 4 * P, "a0_rel_last": 4 * H,
    "c0_wk": H * XH, "c0_wv": H * XH, "c1_wk": P, "c1_wv": P,
    "a0_wo": P, "c0_wq": H * XH, "c0_wo": XC * P,
    "m_router": E + 1, "m_w1": E * HID, "m_w2": E * HC * P,
    "a1_wq": P, "a1_wqs": P, "a1_wk": P, "a1_wks": P, "a1_wv": P, "a1_wg": H * R,
    "a1_rq": 2 * P, "a1_rk": 2 * P, "a1_wo": P,
    "c1_wq": P, "c1_wo": P, "f_w1": HID, "f_w2": HC * P,
}
PARTS = ("a0_wq", "a0_wo", "m_router")
COLUMNS = {"a0_bq": 1, "a0_bk": 1, "c1_bq": 1, "c1_bk": 1, "a1_gb": 2, "a1_decay": 2,
           "f_conv": 3 * HC, "f_convb": HC}
ROWS = {"a0_bv": P, "a0_bo": P, "m_rb": E + 1, "a1_bo": P, "a1_lng": P, "a1_lnb": P,
        "c1_bv": P, "c1_bo": P}
CONSTS = {"ident": P, "tri": P, "causal": P, "cos": P, "sin": P, "time": P, "headsel": P,
          "head8": 4, "group32": 4, "head16": 2, "expert": E + 1, "cap": E + 1}


def offsets(sizes):
    at, found = 0, {}
    for name, n in sizes.items():
        found[name] = (at, at + n)
        at += n
    return found, at


W_AT, W_N = offsets(WEIGHTS)
C_AT, C_N = offsets(COLUMNS)
R_AT, R_N = offsets(ROWS)
K_AT, K_N = offsets(CONSTS)



SECOND = ("d_qk d_gv d_gate d_fade d_rank d_s0 d_s1 d_s2 d_s3 d_values a_qkv d_out d_ln d_ln2 rel0 "
          "rel1 rel2 rel3 d_norm e_q rel_last e_s0 e_s1 e_s2 e_t0 e_s3 e_t1 e_t2 e_t3 e_sums "
          "e_values e_spread e_div e_out e_ln keys_k f_in f_scale keys_v f_up keys1 f_conv f_exp0 "
          "f_exp1 f_silu0 f_silu1 f_silu2 f_quant f_down f_norm").split()
NEXT = ["a_qkv", "rel0", "rel1", "rel2", "rel3", "rel_last", "keys_k", "keys_v", "keys1"]
HALVES_OF = {
    "pe": ("a_s0 d_qk d_gv a_s1 a_s2 d_rank a_t0 a_s3 d_s0 d_s1 d_s2 d_s3 a_t1 a_t2 a_t3 "
            "d_values a_qkv d_out a_sums a_values rel0 rel1 a_spread rel2 rel3 d_norm a_out e_q "
            "rel_last e_s0 a_norm e_s1 e_s2 b_q e_t0 e_s3 e_t1 e_t2 b_s0 b_s1 e_t3 b_s2 e_sums "
            "e_values b_t0 e_spread b_s3 b_t1 b_t2 e_out b_t3 keys_k b_values f_in f_scale b_out "
            "keys_v f_up b_norm c_route c_up0 keys1 c_up1 c_down0 c_up2 c_rank c_down1 c_up3 "
            "c_down2 c_up4 c_down3 c_up5 c_down4 c_up6 f_silu1 f_silu2 c_down5 c_down6 f_quant "
            "f_down c_norm").split(),
    "act": ("d_gv d_gate a_s0 a_s1 a_s2 a_t0 a_s3 a_t2 d_values a_qkv rel0 d_ln a_sums a_spread "
            "d_ln2 rel1 rel2 d_norm rel3 e_q a_ln a_norm e_s0 e_s1 e_s2 b_q e_t0 e_s3 e_t2 b_s0 "
            "b_s1 e_sums b_s2 e_spread b_t0 b_s3 b_t2 e_ln b_values keys_k f_in f_scale b_ln "
            "b_norm c_route c_up0 c_up2 f_conv c_up4 f_exp0 f_exp1 f_silu0 f_silu1 c_up6 f_quant "
            "c_ln f_down c_norm").split(),
    "dve": ("a_s0 d_qk d_gate a_s1 a_s2 d_fade d_rank a_s3 d_s0 d_s2 d_s1 d_s3 a_t1 a_t3 a_sums "
            "d_out a_qkv d_ln a_div d_ln2 a_out rel_last a_ln e_s0 e_s1 e_s2 b_q e_s3 e_t1 b_s0 "
            "b_s1 e_t3 e_sums b_u0 b_s2 b_u1 b_s3 b_u2 e_div b_t1 b_u3 e_out b_t3 e_ln f_in "
            "b_values b_out b_ln keys_v c_route f_up c_pick c_up1 keys1 c_keep c_up3 f_conv "
            "f_exp0 c_sum0 f_exp1 f_silu0 c_up5 f_silu1 f_quant c_sum1 c_sum2 f_down c_ln f_norm").split(),
    "pool": ("d_norm a_s0 rel_last c_norm f_norm").split(),
}


def stages(names, s, pair):
    return [(name, s, pair) for name in names]


def half(order, s, pair, other_pair):
    return [(name, s, pair + (name in NEXT)) if name in SECOND else (name, 1 - s, other_pair)
            for name in order]


def before_loop(order):
    scores = NEXT[:NEXT.index("rel_last") + 1]
    first = [stage for stage in half(order, 1, -1, 0)
             if (stage[0] not in SECOND or stage[0] in NEXT) and stage[0] not in scores]
    names = [name for name, _, _ in first]
    at = names.index("c_up3") if "c_up3" in names else len(names)
    return (stages(NEXT, 0, 0) + stages(scores, 1, 0) + stages(["weights"], 1, 0) + first[:at]
            + stages(["ternary_sum", "ternary"], 0, 0) + first[at:] + stages(["ternary_over"], 0, 0))


def in_loop(order, it):
    return half(order, 0, it, it) + half(order, 1, it, it + 1)


def after_loop(order):
    return ([stage for stage in half(order, 0, NP - 1, NP - 1) if stage[0] not in NEXT]
            + [stage for stage in half(order, 1, NP - 1, NP)
               if stage[0] in SECOND and stage[0] not in NEXT])


def decoder(nc, x_in, xT_in, cT_in, weights, columns, rows, consts, out, rel_dram):
    with ExitStack() as ctx:
        def sb(name, shape, dt=F32):
            return ctx.enter_context(nc.sbuf_tensor(name, shape, dt))

        def per_seq(name, shape, dt=F32):
            return [sb(f"{name}{s}", shape, dt) for s in range(2)]

        def sem(name):
            return ctx.enter_context(nc.semaphore(name))

        bank = [[ctx.enter_context(nc.psum_tensor(f"bank{s}{i}", [P, 512], F32)) for i in range(4)]
                for s in range(2)]

        w_sb = sb("w_sb", [P, W_N])
        col_sb = sb("col_sb", [P, C_N])
        row_sb = sb("row_sb", [P, R_N])
        k_sb = sb("k_sb", [P, K_N])
        ident_bf = sb("ident_bf", [P, P], BF16)
        ones = sb("ones", [P, P])
        eps = sb("eps", [P, 1])
        bqm0 = sb("bqm0", [P, 4])
        bqm1 = sb("bqm1", [P, 4])
        head8s = sb("head8s", [P, 4])
        ngb = sb("ngb", [P, 2])
        loglam = sb("loglam", [P, 2])
        nloglam = sb("nloglam", [P, 2])
        dq = sb("dq", [P, 2, P])
        dqm = sb("dqm", [P, 2, 2, P])
        dk = sb("dk", [P, 2, P])
        w1q = sb("w1q", [P, HID], BF16)
        w2q = sb("w2q", [P, HC * P], BF16)
        wabs = sb("wabs", [P, 2])
        wmean = sb("wmean", [P, 2])
        wscale = sb("wscale", [P, 2])
        routed = sb("routed", [P, E + 1])
        rext = sb("rext", [P, H, M])
        rel = sb("rel", [P, H, P])

        def w(name, a=0, b=None):
            lo, hi = W_AT[name]
            return w_sb[:, lo + a:(hi if b is None else lo + b)]

        def col(name, i=0):
            return col_sb[:, C_AT[name][0] + i:C_AT[name][0] + i + 1]

        def row(name):
            return row_sb[:, R_AT[name][0]:R_AT[name][1]]

        def const(name, a=0, b=None):
            lo, hi = K_AT[name]
            return k_sb[:, lo + a:(hi if b is None else lo + b)]

        ident = const("ident")

        x_ld = per_seq("x_ld", [P, P])
        xT_ld = per_seq("xT_ld", [P, P])
        cT = per_seq("cT", [P, CP])
        probs_sb = per_seq("probs_sb", [P, H * P])
        pT = per_seq("pT", [P, H, P])
        qm = per_seq("qm", [P, 4, P])
        kbd = per_seq("kbd", [P, 4, P])
        va = per_seq("va", [P, 4, 160])
        ve = per_seq("ve", [P, 4, 160])
        k0bd = per_seq("k0bd", [P, XC, 2, C])
        v0 = per_seq("v0", [P, H, XH])
        k1bd = per_seq("k1bd", [P, 4, C])
        nmx = per_seq("nmx", [P, H])
        psum_ = per_seq("psum_", [P, H])
        rr = per_seq("rr", [P, H])
        rrT = per_seq("rrT", [H, P])
        rbc = per_seq("rbc", [P, P])
        q0 = per_seq("q0", [P, XC, P])
        oT = per_seq("oT", [P, XC, P])
        xb = per_seq("xb", [P, P])
        xb2 = per_seq("xb2", [P, P])
        y = per_seq("y", [P, P])
        y2 = per_seq("y2", [P, P])
        x = per_seq("x", [P, P])
        out_sb = per_seq("out_sb", [P, P])
        xT = per_seq("xT", [P, P])
        stats = per_seq("stats", [P, 6])
        mv = per_seq("mv", [P, 2])
        lnv = per_seq("lnv", [P, 1])
        rstd = per_seq("rstd", [P, 1])
        lg = per_seq("lg", [P, 8])
        top = per_seq("top", [P, 8])
        nmax = per_seq("nmax", [P, 1])
        esum = per_seq("esum", [P, 1])
        wts = per_seq("wts", [P, 8])
        topi = per_seq("topi", [P, 8], U32)
        topf = per_seq("topf", [P, 2])
        sel = per_seq("sel", [P, 8])
        sel2 = per_seq("sel2", [P, 8])
        picked = per_seq("picked", [P, 8])
        keep = per_seq("keep", [P, 8])
        wpass = per_seq("wpass", [P, 1])
        scol = per_seq("scol", [P, 8])
        xq = per_seq("xq", [P, P], BF16)
        xqT = per_seq("xqT", [P, P], BF16)
        hp = per_seq("hp", [P, HC, P + 2])
        hid = [[q0[s][:, 4 * i:4 * i + 4, :].rearrange("p c i -> p (c i)") for s in range(2)]
               for i in range(2)]
        sc = [probs_sb[s][:, :].rearrange("p (h j) -> p h j", h=H) for s in range(2)]
        scx = [probs_sb[s][:, 0:H * C].rearrange("p (h j) -> p h j", h=H) for s in range(2)]
        t1 = [q0[s][:, 0:2, :] for s in range(2)]
        t2 = [q0[s][:, 2:4, :] for s in range(2)]
        qk = [q0[s][:, 4:6, :] for s in range(2)]
        eg = [q0[s][:, 6:8, :] for s in range(2)]
        qd = [kbd[s].rearrange("p (c a) t -> p c a t", c=2) for s in range(2)]
        kdm = [oT[s][:, :, :].rearrange("p (g c) t -> p g c t", g=4) for s in range(2)]

        qm1 = [q0[s][:, 0:4, :] for s in range(2)]
        diag, scbc = ([pT[s][:, i, :] for s in range(2)] for i in (4, 5))
        hq, hqT = ([pT[s][:, i:i + 2, :].rearrange("p h i -> p (h i)").bitcast(BF16) for s in range(2)]
                   for i in (0, 2))

        def down_out(s, e):
            return bank[s][1 if e == E - 1 else 2 + e // 4][:, (e % 4) * P:(e % 4 + 1) * P]

        def heads(v):
            return v.rearrange("p q (a c) -> p q a c", c=40)[:, :, :, 0:DH]

        def by_head(ap):
            return ap.rearrange("p (q a d) -> p q a d", q=4, a=4)

        ld_w = sem("ld_w")
        ld_part = [sem(f"ld_part{i}") for i in range(len(PARTS))]
        ld_x, ld_xT, ld_c = ([sem(f"{k}{s}") for s in range(2)] for k in ("ld_x", "ld_xT", "ld_c"))
        ld_rel, st_rel = sem("ld_rel"), sem("st_rel")
        st_out = [sem(f"st_out{s}") for s in range(2)]
        pre_pool, pre_dve, pre_act, pre_pe = sem("pre_pool"), sem("pre_dve"), sem("pre_act"), sem("pre_pe")
        r_s, r_mid, r_last, r_left, r_right = (sem(n) for n in (
            "r_s", "r_mid", "r_last", "r_left", "r_right"))
        x_keys, x_k0, x_values, x_v0, x_kv1, x_kv1_ready = (sem(n) for n in (
            "x_keys", "x_k0", "x_values", "x_v0", "x_kv1", "x_kv1_ready"))
        a_qkv, a_qm, a_kv = sem("a_qkv"), sem("a_qm"), sem("a_kv")
        scores = {k: sem(f"{k}_scores") for k in "abe"}
        maxed = {k: sem(f"{k}_maxed") for k in "abe"}
        exped = {k: sem(f"{k}_exped") for k in "abe"}
        b_scaled = sem("b_scaled")
        probsT = {k: sem(f"{k}_probsT") for k in "abe"}
        probsT_even = {k: sem(f"{k}_probsT_even") for k in "abe"}
        probsT_odd = {k: sem(f"{k}_probsT_odd") for k in "abe"}
        recips, recipsT, recipsT_sb, spread, spread_sb = (
            {k: sem(f"{k}_{name}") for k in "ae"}
            for name in ("recips", "recipsT", "recipsT_sb", "spread", "spread_sb"))
        values = {k: sem(f"{k}_values") for k in "abde"}
        oT_ready = {k: sem(f"{k}_oT_ready") for k in "abde"}
        oT_ready2 = sem("b_oT_ready2")
        proj = {k: sem(f"{k}_proj") for k in "abdef"}
        b_q, b_q_lo, b_q_hi = sem("b_q"), sem("b_q_lo"), sem("b_q_hi")
        e_q, e_qm = sem("e_q"), sem("e_qm")
        var = {k: sem(f"{k}_var") for k in "abcdDef"}
        inv = {k: sem(f"{k}_inv") for k in "abcdDef"}
        normed = {k: sem(f"{k}_normed") for k in "abcDef"}
        xT_ps = {k: sem(f"{k}_xT_ps") for k in "abcD"}
        xT_ready = {k: sem(f"{k}_xT_ready") for k in "abcD"}
        xb_ready = {k: sem(f"{k}_xb") for k in "ade"}
        c_logits, c_shift, c_exp, c_pick, c_rank, c_keep = (sem(n) for n in (
            "c_logits", "c_shift", "c_exp", "c_pick", "c_rank", "c_keep"))
        c_up = sem("c_up")
        c_hid = [sem("c_hid_even"), sem("c_hid_odd")]
        c_down = [sem("c_down_lo"), sem("c_down_hi"), sem("c_down_last")]
        d_qk, d_gv, d_gate0, d_gate1, d_gate, d_v, d_rope, d_rank, d_qkd = (sem(n) for n in (
            "d_qk", "d_gv", "d_gate0", "d_gate1", "d_gate", "d_v", "d_rope", "d_rank", "d_qkd"))
        d_att, d_masked = sem("d_att"), sem("d_masked")
        (f_xq, f_xqT, f_xqT_sb, f_h, f_hp, f_conv0, f_conv, f_exp, f_exp1, f_sig, f_silu, f_hT, f_hq,
         f_hqT, f_hqT_sb) = (sem(n) for n in (
             "f_xq", "f_xqT", "f_xqT_sb", "f_h", "f_hp", "f_conv0", "f_conv", "f_exp",
             "f_exp1", "f_sig", "f_silu", "f_hT", "f_hq", "f_hqT", "f_hqT_sb"))
        f_diag, f_scale, f_scbc = sem("f_diag"), sem("f_scale"), sem("f_scbc")
        banks_free = sem("banks_free")
        dve_step, act_step = sem("dve_step"), sem("act_step")

        def counter(eng):
            held = {}

            def n(s, pair, per=1, step=None):
                value = pair * (2 * per) + (per * s + (per if step is None else step))
                if isinstance(pair, int):
                    return max(value, 0)
                key = (id(pair), per, s, step)
                if key not in held:
                    held[key] = (pair, eng.snap(value))
                return held[key][1]
            return n

        def transfers(eng, pair):
            return 16 * (pair + 1) if isinstance(pair, int) else eng.snap((pair + 1) * 16)

        def run(eng, order, table, clear=None):
            def go(halves):
                for name, s, pair in halves:
                    if name in table:
                        table[name](s, pair)
            go(before_loop(order))
            if clear:
                clear()
            with eng.Fori(0, NP - 1) as it:
                if clear:
                    clear()
                nxt = eng.snap(it + 1)
                pairs = {0: it, 1: nxt}
                go([(name, s, pairs[pair]) for name, s, pair in in_loop(order, 0)])
            if clear:
                clear()
            go(after_loop(order))

        block = ctx.enter_context(nc.Block())

        @block.sync
        def _(sp):
            n = counter(sp)

            def loaded_before(s, pair):
                sp.wait_ge(x_kv1, n(s, pair, step=-1))
                sp.dma_start(cT[s][:, 0:C], cT_in[pair, s]).then_inc(ld_c[s], 16)
                sp.wait_ge(a_qkv, n(s, pair, step=-1))
                sp.dma_start(xT_ld[s][:], xT_in[pair, s]).then_inc(ld_xT[s], 16)
                sp.wait_ge(xb_ready["a"], n(s, pair, step=-1))
                sp.dma_start(x_ld[s][:], x_in[pair, s]).then_inc(ld_x[s], 16)

            def store_rel(s, pair):
                sp.wait_ge(r_left, n(s, pair))
                sp.wait_ge(r_right, n(s, pair))
                sp.dma_start(rel_dram[pair, s].rearrange("(i c) -> i c", c=RROW),
                             rext[:, :, :].rearrange("p h m -> p (h m)")).then_inc(st_rel, 16)

            def load_rel(s, pair):
                sp.wait_ge(maxed["a"], n(s, pair, per=4, step=0))
                sp.wait_ge(st_rel, n(s, pair, per=16))
                skewed = rel_dram[pair, s, P - 1:P - 1 + P * (RROW - 1)].rearrange(
                    "(i c) -> i c", c=RROW - 1)
                sp.dma_start(rel[:, 0:H - 1, :], skewed[:, 0:(H - 1) * M].rearrange(
                    "i (h m) -> i h m", m=M)[:, :, 0:P]).then_inc(ld_rel, 16)
                sp.dma_start(rel[:, H - 1, :], skewed[:, (H - 1) * M:(H - 1) * M + P]
                             ).then_inc(ld_rel, 16)

            sp.dma_start(xT_ld[0][:], xT_in[0, 0]).then_inc(ld_xT[0], 16)
            sp.dma_start(k_sb[:], consts).then_inc(ld_w, 16)
            sp.dma_start(col_sb[:], columns).then_inc(ld_w, 16)
            sp.dma_start(row_sb[:], rows.partition_broadcast(P)).then_inc(ld_w, 16)
            ends = [W_AT[name][0] for name in PARTS[1:]] + [W_N]
            for i, (name, end) in enumerate(zip(PARTS, ends)):
                part = slice(W_AT[name][0], end)
                sp.dma_start(w_sb[:, part], weights[:, part]).then_inc(ld_part[i], 16)
                if i == 0:
                    sp.dma_start(cT[0][:, 0:C], cT_in[0, 0]).then_inc(ld_c[0], 16)
                    sp.dma_start(x_ld[0][:], x_in[0, 0]).then_inc(ld_x[0], 16)
                    loaded_before(1, 0)
            store_rel(0, 0)
            load_rel(0, 0)
            store_rel(1, 0)
            with sp.Fori(0, NP - 1) as it:
                nxt = sp.snap(it + 1)
                for s, pair, per in ((0, nxt, 4), (0, nxt, 16), (1, it, 4), (1, it, 16)):
                    n(s, pair, per, 0 if per == 4 else None)
                loaded_before(0, nxt)
                load_rel(1, it)
                store_rel(0, nxt)
                loaded_before(1, nxt)
                load_rel(0, nxt)
                store_rel(1, nxt)
            load_rel(1, NP - 1)

        @block.gpsimd
        def _(pool):
            G = nc.gpsimd
            n = counter(pool)
            G.memset(ones[:], 1.0).then_inc(pre_pool, 1)
            G.memset(eps[:], EPS).then_inc(pre_pool, 1)
            G.memset(routed[:], 0.0).then_inc(pre_pool, 1)
            for s in range(2):
                for t in (va, ve, k0bd, v0, hp):
                    G.memset(t[s][:], 0.0).then_inc(pre_pool, 1)
                G.memset(cT[s][:, C:CP], 0.0).then_inc(pre_pool, 1)

            def rel_left(s, pair):
                pool.wait_ge(r_mid, n(s, pair, 4))
                lo = rext[:, :, MAX_REL - 1:MAX_REL].broadcast_to([P, H, MAX_REL - 1])
                G.tensor_tensor(rext[:, :, 0:MAX_REL - 1], lo, ones[:, 0:1].unsqueeze(2).broadcast_to(
                    [P, H, MAX_REL - 1]), ALU.mult).then_inc(r_left, 1)

            def residual(k, src, before, bias, dst=xb):
                def f(s, pair):
                    before(s, pair)
                    G.tensor_tensor(dst[s][:], src[s][:], row(bias), ALU.add).then_inc(xb_ready[k], 1)
                return f

            def before_a(s, pair):
                pool.wait_ge(ld_x[s], transfers(pool, pair))
                pool.wait_ge(x_kv1, n(s, pair))

            def d_residuals(s, pair):
                pool.wait_ge(normed["c"], n(s, pair))
                G.tensor_tensor(xb[s][:], x[s][:], row("a1_bo"), ALU.add).then_inc(xb_ready["d"], 1)
                G.tensor_tensor(xb2[s][:], x[s][:], row("a1_lnb"), ALU.add).then_inc(xb_ready["d"], 1)

            def store(s, pair):
                pool.wait_ge(normed["f"], n(s, pair))
                G.dma_start(out[pair, s], out_sb[s][:]).then_inc(st_out[s], 16)
                pool.wait_ge(st_out[s], transfers(pool, pair))

            pool.wait_ge(ld_w, 48)
            pool.wait_ge(pre_pool, 1)
            run(pool, HALVES_OF["pool"], {
                "rel_last": rel_left,
                "a_s0": residual("a", x_ld, before_a, "a0_bo"),
                "c_norm": d_residuals,
                "d_norm": residual("e", x, lambda s, pair: pool.wait_ge(normed["D"], n(s, pair)), "c1_bo"),
                "f_norm": store,
            })
            pool.wait_ge(st_out[0], 16 * NP)
            pool.wait_ge(st_out[1], 16 * NP)

        @block.tensor
        def _(pe):
            n = counter(pe)

            def mm(out_, lhsT, rhs, start=True, stop=True):
                return pe.matmul(out_, lhsT, rhs, start=start, stop=stop)

            pe.wait_ge(pre_pool, N_POOL)
            pe.wait_ge(ld_w, 48)
            pe.wait_ge(ld_part[0], 16)
            pe.wait_ge(pre_dve, 1)

            def more_weights(s, pair):
                pe.wait_ge(ld_part[s], 16)

            def c_weights(s, pair):
                if isinstance(pair, int) and (s, pair) == (0, 0):
                    pe.wait_ge(ld_part[2], 16)

            def ternary(s, pair):
                pe.wait_ge(pre_dve, 2)
                pe.wait_ge(r_right, 2)
                mm(bank[1][0][:, 0:2], ones[:], wabs[:]).then_inc(pre_pe, 1)

            def ternary_over(s, pair):
                pe.wait_ge(pre_dve, 4)

            def rel_scores(g):
                def f(s, pair):
                    if g == 0:
                        pe.wait_ge(a_qm, n(s, pair))
                    elif g == 2:
                        pe.wait_ge(a_kv, n(s, pair))
                    elif g == 3:
                        pe.wait_ge(r_mid, n(s, pair, 4, 1))
                    mm(bank[s][REL_BANK[g]][:], qm[s][:, g, :], w("a0_rel")).then_inc(r_s, 1)
                return f

            def rel_last(s, pair):
                pe.wait_ge(r_mid, n(s, pair, 4, 2))
                for g in range(4):
                    last = mm(bank[s][0][:, 0:H], qm[s][:, g, :], w("a0_rel_last", g * H, (g + 1) * H),
                              start=(g == 0), stop=(g == 3))
                last.then_inc(r_last, 1)

            def keys_k(s, pair):
                pe.wait_ge(ld_c[s], transfers(pe, pair))
                pe.wait_ge(r_mid, n(s, pair, 4))
                for c in range(XC):
                    last = mm(bank[s][KEY_BANK[c // 4]][:, (c % 4) * CP:(c % 4 + 1) * CP],
                              w("c0_wk", c * P, (c + 1) * P), cT[s][:])
                last.then_inc(x_keys, 1)

            def keys_v(s, pair):
                pe.wait_ge(x_k0, n(s, pair))
                for c in range(2):
                    last = mm(bank[s][KEY_BANK[c]][0:C, :], cT[s][:, 0:C],
                              w("c0_wv", c * 512, (c + 1) * 512))
                last.then_inc(x_values, 1)

            def keys1(s, pair):
                pe.wait_ge(x_v0, n(s, pair))
                mm(bank[s][3][:, 0:CP], w("c1_wk"), cT[s][:])
                mm(bank[s][3][0:C, P:2 * P], cT[s][:, 0:C], w("c1_wv")).then_inc(x_kv1, 1)

            def a_qkv_(s, pair):
                pe.wait_ge(ld_xT[s], transfers(pe, pair))
                mm(bank[s][3][:, 0:P], w("a0_wq"), xT_ld[s][:])
                mm(bank[s][1][:, P:2 * P], w("a0_wk"), xT_ld[s][:])
                mm(bank[s][1][:, 2 * P:3 * P], xT_ld[s][:], w("a0_wv")).then_inc(a_qkv, 1)

            def a_scores(g):
                def f(s, pair):
                    if g == 0:
                        pe.wait_ge(banks_free, n(s, pair))
                        pe.wait_ge(r_right, n(s, pair))
                        pe.wait_ge(x_kv1_ready, n(s, pair))
                    mm(bank[s][g][:], qm[s][:, g, :], kbd[s][:, :, :]).then_inc(scores["a"], 1)
                return f

            def transposes(k, ready, g):
                def f(s, pair):
                    nk, src = (P, sc) if k == "a" else (C, scx)
                    pe.wait_ge(ready, n(s, pair, 4, g + 1))
                    for a in range(4):
                        last = pe.transpose(bank[s][g][0:nk, a * P:(a + 1) * P],
                                            src[s][:, 4 * g + a, :], ident)
                    last.then_inc(probsT[k], 1)
                return f

            def sums(k):
                def f(s, pair):
                    pe.wait_ge(recips[k], n(s, pair))
                    pe.wait_ge(probsT_odd[k], n(s, pair, 2, 2))
                    pe.transpose(bank[s][3][0:H, 0:P], rr[s][:], ident).then_inc(recipsT[k], 1)
                return f

            def spread_out(k):
                def f(s, pair):
                    pe.wait_ge(recipsT_sb[k], n(s, pair))
                    mm(bank[s][3][:, P:2 * P], const("headsel")[0:H, :], rrT[s][:]).then_inc(spread[k], 1)
                return f

            def head_products(s, v, src):
                for h in range(H):
                    q, a = h // 4, h % 4
                    last = mm(bank[s][0][32 * q:32 * q + 32, 0:P], v[s][:, q, 32 * a:32 * a + 32],
                              src[s][:, h, :], start=(a == 0), stop=(a == 3))
                return last

            def values_(k, v):
                def f(s, pair):
                    pe.wait_ge(probsT_even[k], n(s, pair, 2, 2))
                    pe.wait_ge(probsT_odd[k], n(s, pair, 2, 2))
                    head_products(s, v, pT).then_inc(values[k], 1)
                return f

            def project(k, weight):
                def f(s, pair):
                    pe.wait_ge(oT_ready[k], n(s, pair))
                    mm(bank[s][2][:, 0:P], oT[s][:, 0, :], weight).then_inc(proj[k], 1)
                return f

            def transpose_x(k, b):
                def f(s, pair):
                    pe.wait_ge(normed[k], n(s, pair))
                    pe.transpose(bank[s][b][:, 0:P], x[s][:], ident).then_inc(xT_ps[k], 1)
                return f

            def b_q_(s, pair):
                pe.wait_ge(xT_ready["a"], n(s, pair))
                for c in range(XC):
                    last = mm(bank[s][c // 4][:, (c % 4) * P:(c % 4 + 1) * P],
                              w("c0_wq", c * P, (c + 1) * P), xT[s][:])
                last.then_inc(b_q, 1)

            def b_scores(g):
                def f(s, pair):
                    if g == 0:
                        pe.wait_ge(b_q_lo, n(s, pair))
                        pe.wait_ge(b_q_hi, n(s, pair))
                        pe.wait_ge(x_k0, n(s, pair))
                    for c in (2 * g, 2 * g + 1):
                        last = mm(bank[s][g][:, (c % 2) * 2 * C:(c % 2 + 1) * 2 * C],
                                  q0[s][:, c, :], k0bd[s][:, c, :, :])
                    last.then_inc(scores["b"], 1)
                return f

            def b_values(s, pair):
                pe.wait_ge(probsT_even["b"], n(s, pair, 2, 2))
                pe.wait_ge(probsT_odd["b"], n(s, pair, 2, 2))
                for h in range(H):
                    c, half = h // 2, h % 2
                    last = mm(bank[s][c // 4][half * XH:(half + 1) * XH, (c % 4) * P:(c % 4 + 1) * P],
                              v0[s][:, h, :], pT[s][:, h, :])
                last.then_inc(values["b"], 1)

            def b_out(s, pair):
                pe.wait_ge(oT_ready["b"], n(s, pair))
                pe.wait_ge(oT_ready2, n(s, pair))
                for c in range(XC):
                    last = mm(bank[s][2][:, 0:P], oT[s][:, c, :], w("c0_wo", c * P, (c + 1) * P),
                              start=(c == 0), stop=(c == XC - 1))
                last.then_inc(proj["b"], 1)

            def c_route(s, pair):
                pe.wait_ge(xT_ready["b"], n(s, pair))
                c_weights(s, pair)
                mm(bank[s][3][:, 0:E + 1], xT[s][:], w("m_router")).then_inc(c_logits, 1)

            def c_up_(e):
                def f(s, pair):
                    if e == 0:
                        pe.wait_ge(xT_ready["b"], n(s, pair))
                    for c in range(HC):
                        last = mm(bank[s][e % 2][:, c * P:(c + 1) * P],
                                  w("m_w1", e * HID + c * P, e * HID + (c + 1) * P), xT[s][:])
                    last.then_inc(c_up, 1)
                return f

            def c_rank_(s, pair):
                pe.wait_ge(c_pick, n(s, pair))
                mm(bank[s][3][:, 0:E + 1], const("tri"), picked[s][:], stop=False)
                mm(bank[s][3][:, 0:E + 1], ones[:], routed[:], start=False).then_inc(c_rank, 1)

            def c_down_(e):
                def f(s, pair):
                    pe.wait_ge(c_hid[e % 2], n(s, pair, (E + 1 - e % 2) // 2, e // 2 + 1))
                    if e == 4:
                        pe.wait_ge(c_keep, n(s, pair))
                    for c in range(HC):
                        last = mm(down_out(s, e),
                                  hid[e % 2][s][:, c * P:(c + 1) * P],
                                  w("m_w2", (e * HC + c) * P, (e * HC + c + 1) * P),
                                  start=(c == 0), stop=(c == HC - 1))
                    if e in (3, E - 2, E - 1):
                        last.then_inc(c_down[(3, E - 2, E - 1).index(e)], 1)
                return f

            def d_qk_(s, pair):
                pe.wait_ge(xT_ready["c"], n(s, pair))
                for i, name in enumerate(("a1_wq", "a1_wk", "a1_wqs", "a1_wks")):
                    last = mm(bank[s][0][:, i * P:(i + 1) * P], w(name), xT[s][:])
                last.then_inc(d_qk, 1)

            def d_gv_(s, pair):
                mm(bank[s][1][:, 0:P], w("a1_wg", 0, P), xT[s][:])
                mm(bank[s][1][:, P:2 * P], w("a1_wg", P, 2 * P), xT[s][:])
                mm(bank[s][1][:, 2 * P:3 * P], xT[s][:], w("a1_wv")).then_inc(d_gv, 1)

            def d_rank_(s, pair):
                pe.wait_ge(d_rope, n(s, pair))
                for i, name in enumerate(("a1_rq", "a1_rk")):
                    for c in range(2):
                        last = mm(bank[s][2][:, (2 * i + c) * P:(2 * i + c + 1) * P],
                                  w(name, c * P, (c + 1) * P), qk[s][:, i, :])
                last.then_inc(d_rank, 1)

            def d_scores(g):
                def f(s, pair):
                    pe.wait_ge(d_qkd, n(s, pair, 4, g + 1 if g < 2 else 4))
                    if g == 0:
                        pe.wait_ge(d_v, n(s, pair))
                    for c in range(2):
                        last = mm(bank[s][g][:, c * 2 * P:(c + 1) * 2 * P], kdm[s][:, g, c, :],
                                  qd[s][:, c, :, :])
                    last.then_inc(d_att, 1)
                return f

            def d_values(s, pair):
                pe.wait_ge(d_masked, n(s, pair, 4, 4))
                for h in range(H):
                    c, g, a = h // 8, h % 8 // 2, h % 2
                    q, i = h // 4, h % 4
                    last = mm(bank[s][0][32 * q:32 * q + 32, 0:P], va[s][:, q, 32 * i:32 * i + 32],
                              sc[s][:, 4 * g + 2 * c + a, :], start=(i == 0), stop=(i == 3))
                last.then_inc(values["d"], 1)

            def e_q_(s, pair):
                pe.wait_ge(xT_ready["D"], n(s, pair))
                mm(bank[s][2][:, 0:P], w("c1_wq"), xT[s][:]).then_inc(e_q, 1)

            def e_scores(g):
                def f(s, pair):
                    if g == 0:
                        pe.wait_ge(e_qm, n(s, pair))
                        pe.wait_ge(x_kv1_ready, n(s, pair))
                        if not isinstance(pair, int):
                            pe.wait_ge(r_right, n(s, pair, step=3))
                    mm(bank[s][g][:, 0:4 * C], qm1[s][:, g, :], k1bd[s][:, :, :]).then_inc(scores["e"], 1)
                return f

            def f_in(s, pair):
                pe.wait_ge(f_xq, n(s, pair))
                pe.transpose(bank[s][2][:].bitcast(BF16)[:, 0:P], xq[s][:], ident_bf[:]).then_inc(f_xqT, 1)

            def f_scale_(s, pair):
                pe.wait_ge(f_diag, n(s, pair))
                mm(bank[s][0][:, 0:P], ones[:], diag[s]).then_inc(f_scale, 1)

            def f_up(s, pair):
                pe.wait_ge(f_xqT_sb, n(s, pair))
                for c in range(HC):
                    last = mm(bank[s][2][:, c * P:(c + 1) * P], w1q[:, c * P:(c + 1) * P], xqT[s][:])
                last.then_inc(f_h, 1)

            def f_silu_(i):
                def f(s, pair):
                    pe.wait_ge(f_silu, n(s, pair, 2, i + 1))
                    for c in (2 * i, 2 * i + 1):
                        last = pe.transpose(bank[s][3][:, c * P:(c + 1) * P],
                                            hid[0][s][:, c * P:(c + 1) * P], ident)
                    last.then_inc(f_hT, 1)
                return f

            def f_quant(s, pair):
                pe.wait_ge(f_hq, n(s, pair))
                for c in range(HC):
                    last = pe.transpose(bank[s][0][:].bitcast(BF16)[:, c * P:(c + 1) * P],
                                        hq[s][:, c * P:(c + 1) * P], ident_bf[:])
                last.then_inc(f_hqT, 1)

            def f_down(s, pair):
                pe.wait_ge(f_hqT_sb, n(s, pair))
                for c in range(HC):
                    last = mm(bank[s][1][:, 0:P], hqT[s][:, c * P:(c + 1) * P],
                              w2q[:, c * P:(c + 1) * P], start=(c == 0), stop=(c == HC - 1))
                last.then_inc(proj["f"], 1)

            run(pe, HALVES_OF["pe"], {
                "weights": more_weights, "ternary": ternary, "ternary_over": ternary_over,
                **{f"rel{g}": rel_scores(g) for g in range(4)}, "rel_last": rel_last,
                "keys_k": keys_k, "keys_v": keys_v, "keys1": keys1, "a_qkv": a_qkv_, 
                **{f"a_s{g}": a_scores(g) for g in range(4)},
                **{f"a_t{g}": transposes("a", exped["a"], g) for g in range(4)}, "a_sums": sums("a"), "a_values": values_("a", va),
                "a_spread": spread_out("a"), "e_spread": spread_out("e"),
                "a_out": project("a", w("a0_wo")), "a_norm": transpose_x("a", 3),
                "b_q": b_q_, **{f"b_s{g}": b_scores(g) for g in range(4)},
                **{f"b_t{g}": transposes("b", b_scaled, g) for g in range(4)}, "b_values": b_values,
                "b_out": b_out, "b_norm": transpose_x("b", 3),
                "c_route": c_route, "c_rank": c_rank_,
                **{f"c_up{e}": c_up_(e) for e in range(E)},
                **{f"c_down{e}": c_down_(e) for e in range(E)},
                "c_norm": transpose_x("c", 0),
                "d_qk": d_qk_, "d_gv": d_gv_, "d_rank": d_rank_, **{f"d_s{g}": d_scores(g) for g in range(4)}, "d_values": d_values,
                "d_out": project("d", w("a1_wo")), "d_norm": transpose_x("D", 2),
                "e_q": e_q_, **{f"e_s{g}": e_scores(g) for g in range(4)},
                **{f"e_t{g}": transposes("e", exped["e"], g) for g in range(4)}, "e_sums": sums("e"),
                "e_values": values_("e", ve), "e_out": project("e", w("c1_wo")),
                "f_in": f_in, "f_scale": f_scale_, "f_up": f_up, "f_silu1": f_silu_(0), "f_silu2": f_silu_(1), "f_quant": f_quant, "f_down": f_down,
            })

        @block.scalar
        def _(act):
            A = nc.scalar
            n = counter(act)
            act.preload_act_table_set("natural_log_exp_and_others")
            steps = [0]

            def step(ins):
                steps[0] += 1
                ins.then_inc(act_step, 1)
                act.wait_ge(act_step, steps[0])

            def clear():
                act.sem_clear(act_step)
                steps[0] = 0

            act.wait_ge(ld_w, 48)
            act.wait_ge(pre_dve, 1)
            dlo = C_AT["a1_decay"][0]
            step(A.activation(loglam[:], col_sb[:, dlo:dlo + 2], ACT.Exp, scale=-1.0))
            step(A.activation(nloglam[:], loglam[:], ACT.Ln, bias=1.0))
            step(A.activation(loglam[:], nloglam[:], ACT.Copy, scale=-1.0))
            for c in range(2):
                A.activation(dq[:, c, :], const("time"), ACT.Exp, scale=loglam[:, c:c + 1])
                last = A.activation(dk[:, c, :], const("time"), ACT.Exp, scale=nloglam[:, c:c + 1])
            last.then_inc(pre_act, 1)

            def queries(came, b, dst, ready, biases):
                def f(s, pair):
                    act.wait_ge(came, n(s, pair))
                    for g in range(4):
                        last = A.activation(dst[s][:, g, :], bank[s][b][:, 0:P], ACT.Identity,
                                            bias=biases[:, g:g + 1], scale=const("group32", g, g + 1))
                    last.then_inc(ready, 1)
                return f

            def rel_mid(g):
                def f(s, pair):
                    if g == 0:
                        act.wait_ge(st_rel, n(s, pair, per=16, step=0))
                    act.wait_ge(r_s, n(s, pair, 4, g + 1))
                    A.activation(rext[:, 4 * g:4 * g + 4, MAX_REL - 1:MAX_REL - 1 + P],
                                 bank[s][REL_BANK[g]][:].rearrange("p (a r) -> p a r", a=4),
                                 ACT.Copy).then_inc(r_mid, 1)
                return f

            def keys_k(s, pair):
                act.wait_ge(x_keys, n(s, pair))
                for half in range(2):
                    part = slice(half * XH, half * XH + XH)
                    for b in range(2):
                        last = A.activation(
                            k0bd[s][part, 4 * b:4 * b + 4, half, :],
                            bank[s][KEY_BANK[b]][part, 0:4 * CP].rearrange("p (c j) -> p c j", c=4)[:, :, 0:C],
                            ACT.Copy, scale=XH ** -0.5)
                last.then_inc(x_k0, 1)

            def exps(k, g):
                def f(s, pair):
                    act.wait_ge(maxed[k], n(s, pair, 4, g + 1))
                    for a in range(4):
                        h = 4 * g + a
                        dst = (sc if k == "a" else scx)[s][:, h, :]
                        src = dst if k == "a" else bank[s][g][:, a * C:(a + 1) * C]
                        last = A.activation(dst, src, ACT.Exp, bias=nmx[s][:, h:h + 1],
                                            accum_out=psum_[s][:, h:h + 1])
                    last.then_inc(exped[k], 1)
                return f

            def copy_probsT(k, nk, g):
                def f(s, pair):
                    act.wait_ge(probsT[k], n(s, pair, 4, g + 1))
                    A.activation(pT[s][0:nk, 4 * g:4 * g + 4, :], bank[s][g][0:nk, :].rearrange(
                        "p (a i) -> p a i", a=4), ACT.Copy).then_inc(probsT_even[k], 1)
                return f

            def sums(k):
                def f(s, pair):
                    act.wait_ge(recipsT[k], n(s, pair))
                    A.activation(rrT[s][:], bank[s][3][0:H, 0:P], ACT.Copy).then_inc(recipsT_sb[k], 1)
                return f

            def spreads(k):
                def f(s, pair):
                    act.wait_ge(spread[k], n(s, pair))
                    A.activation(rbc[s][:], bank[s][3][:, P:2 * P], ACT.Copy).then_inc(spread_sb[k], 1)
                return f

            def copy_T(ps, dst, b, ready):
                def f(s, pair):
                    act.wait_ge(ps, n(s, pair))
                    A.activation(dst(s), bank[s][b][:, 0:P], ACT.Copy).then_inc(ready, 1)
                return f

            def deviation(k):
                def f(s, pair):
                    act.wait_ge(var[k], n(s, pair))
                    step(A.activation(lnv[s][:], mv[s][:, 1:2], ACT.Ln, bias=eps[:]))
                    A.activation(rstd[s][:], lnv[s][:], ACT.Exp, scale=-0.5).then_inc(inv[k], 1)
                return f

            def f_down(s, pair):
                act.wait_ge(var["f"], n(s, pair))
                A.activation(lnv[s][:], mv[s][:, 1:2], ACT.Ln, bias=eps[:]).then_inc(banks_free, 1)
                act.wait_ge(banks_free, n(s, pair, step=3))
                A.activation(rstd[s][:], lnv[s][:], ACT.Exp, scale=-0.5).then_inc(inv["f"], 1)

            def copy_wide(came, dst, ready):
                def f(s, pair):
                    act.wait_ge(came, n(s, pair))
                    A.activation(dst[s][:, 0:4, :], bank[s][0][:].rearrange("p (c i) -> p c i", c=4),
                                 ACT.Copy).then_inc(ready, 1)
                return f

            def c_exp_(s, pair):
                act.wait_ge(c_shift, n(s, pair))
                A.activation(lg[s][:], lg[s][:], ACT.Exp, bias=nmax[s][:],
                             accum_out=esum[s][:]).then_inc(c_exp, 1)

            def hidden(e):
                def f(s, pair):
                    act.wait_ge(c_up, n(s, pair, E, e + 1))
                    A.activation(hid[0][s], bank[s][0][:], ACT.Relu).then_inc(c_hid[e % 2], 1)
                return f

            def d_gates(s, pair):
                act.wait_ge(d_gv, n(s, pair))
                for c in range(2):
                    last = A.activation(eg[s][:, c, :], bank[s][1][:, c * P:(c + 1) * P], ACT.Exp,
                                        bias=ngb[:, c:c + 1], scale=-1.0)
                last.then_inc(d_gate0, 1)
                A.activation(heads(va[s]), by_head(bank[s][1][:, 2 * P:3 * P]), ACT.Copy).then_inc(d_v, 1)

            def d_gate_(s, pair):
                act.wait_ge(d_gate1, n(s, pair))
                step(A.activation(eg[s], eg[s], ACT.Ln))
                A.activation(eg[s], eg[s], ACT.Exp, scale=-1.0).then_inc(d_gate, 1)

            def f_in(s, pair):
                act.wait_ge(f_xqT, n(s, pair))
                A.activation(xqT[s][:], bank[s][2][:].bitcast(BF16)[:, 0:P], ACT.Copy
                             ).then_inc(f_xqT_sb, 1)

            def f_scale_(s, pair):
                act.wait_ge(f_scale, n(s, pair))
                A.activation(scbc[s], bank[s][0][:, 0:P], ACT.Copy, scale=wmean[:, 0:1]).then_inc(f_scbc, 1)

            def f_conv_(s, pair):
                act.wait_ge(f_hp, n(s, pair))
                for c in range(HC):
                    A.activation(hid[0][s][:, c * P:(c + 1) * P], hp[s][:, c, 1:P + 1],
                                 ACT.Identity, bias=col("f_convb", c),
                                 scale=col("f_conv", 3 * c + 1)).then_inc(f_conv0, 1)

            def f_exp_(i):
                def f(s, pair):
                    act.wait_ge(f_conv, n(s, pair, 2, i + 1))
                    A.activation(hid[1][s][:, HALVES[i]], hid[0][s][:, HALVES[i]], ACT.Exp, scale=-1.0
                                 ).then_inc(f_exp, 1)
                return f

            def f_silu_(i):
                def f(s, pair):
                    part = hid[1][s][:, HALVES[i]]
                    act.wait_ge(f_exp1, n(s, pair, 2, i + 1))
                    step(A.activation(part, part, ACT.Ln))
                    A.activation(part, part, ACT.Exp, scale=-1.0).then_inc(f_sig, 1)
                return f

            def f_quant(s, pair):
                act.wait_ge(f_hqT, n(s, pair))
                A.activation(hqT[s], bank[s][0][:].bitcast(BF16)[:, 0:HID], ACT.Copy
                             ).then_inc(f_hqT_sb, 1)

            act.wait_ge(pre_pool, N_POOL)
            for s in range(2):
                A.activation(lnv[s][:], eps[:], ACT.Copy).then_inc(banks_free, 1)
            xT_of = lambda s: xT[s][:]
            run(act, HALVES_OF["act"], {
                **{f"rel{g}": rel_mid(g) for g in range(4)}, "keys_k": keys_k, "a_qkv": queries(a_qkv, 3, qm, a_qm, bqm0),
                **{f"a_s{g}": exps("a", g) for g in range(4)}, **{f"a_t{g}": copy_probsT("a", P, g) for g in (0, 2)}, "a_sums": sums("a"),
                "a_spread": spreads("a"),
                "a_ln": deviation("a"), "a_norm": copy_T(xT_ps["a"], xT_of, 3, xT_ready["a"]),
                "b_q": copy_wide(b_q, q0, b_q_lo), **{f"b_s{g}": exps("b", g) for g in range(4)},
                **{f"b_t{g}": copy_probsT("b", C, g) for g in (0, 2)}, "b_values": copy_wide(values["b"], oT, oT_ready["b"]),
                "b_ln": deviation("b"), "b_norm": copy_T(xT_ps["b"], xT_of, 3, xT_ready["b"]),
                "c_route": c_exp_, **{f"c_up{e}": hidden(e) for e in range(0, E, 2)},
                "c_ln": deviation("c"), "c_norm": copy_T(xT_ps["c"], xT_of, 0, xT_ready["c"]),
                "d_gv": d_gates, "d_gate": d_gate_, "d_values": copy_T(values["d"], lambda s: oT[s][:, 0, :], 0,
                                                     oT_ready["d"]),
                "d_ln": deviation("d"), "d_ln2": deviation("D"),
                "d_norm": copy_T(xT_ps["D"], xT_of, 2, xT_ready["D"]),
                "e_q": queries(e_q, 2, qm1, e_qm, bqm1), **{f"e_s{g}": exps("e", g) for g in range(4)},
                **{f"e_t{g}": copy_probsT("e", C, g) for g in (0, 2)}, "e_sums": sums("e"), "e_spread": spreads("e"),
                "e_ln": deviation("e"),
                "ternary_over": lambda s, pair: act.wait_ge(pre_dve, 4),
                "f_in": f_in, "f_scale": f_scale_, "f_conv": f_conv_, "f_exp0": f_exp_(0), "f_exp1": f_exp_(1),
                "f_silu0": f_silu_(0), "f_silu1": f_silu_(1), "f_quant": f_quant,
                "f_down": f_down,
            }, clear)

        @block.vector
        def _(dve):
            V = nc.vector
            n = counter(dve)
            steps = [0]

            def mark(ins):
                steps[0] += 1
                ins.then_inc(dve_step, 1)
                return steps[0]

            def after(count):
                dve.wait_ge(dve_step, count)

            def step(ins):
                after(mark(ins))

            def clear():
                dve.sem_clear(dve_step)
                steps[0] = 0

            dve.wait_ge(ld_w, 48)
            step(V.tensor_scalar(ngb[:], col_sb[:, C_AT["a1_gb"][0]:C_AT["a1_gb"][1]], -1.0, None, ALU.mult))
            step(V.tensor_scalar(bqm0[:], const("group32"), col("a0_bq"), None, ALU.mult))
            step(V.tensor_scalar(bqm1[:], const("group32"), col("c1_bq"), None, ALU.mult))
            V.tensor_scalar(head8s[:], const("head8"), DH ** -0.5, None, ALU.mult).then_inc(pre_dve, 1)
            dve.wait_ge(pre_act, 1)
            for c in range(2):
                for a in range(2):
                    V.tensor_scalar(dqm[:, c, a, :], dq[:, c, :], const("head16", a, a + 1), None, ALU.mult)
            step(V.tensor_scalar(dk[:], dk[:], DH ** -0.5, None, ALU.mult))
            def ternary_sum(s, pair):
                dve.wait_ge(ld_part[2], 16)
                step(V.tensor_reduce(wabs[:, 0:1], w("f_w1"), AX.X, ALU.add, apply_absolute_value=True))
                V.tensor_reduce(wabs[:, 1:2], w("f_w2"), AX.X, ALU.add, apply_absolute_value=True
                                ).then_inc(pre_dve, 1)

            def ternary(s, pair):
                dve.wait_ge(pre_pe, 1)
                V.tensor_scalar(wmean[:], bank[1][0][:, 0:2], 1.0 / (P * HID), 1e-5, ALU.mult, ALU.max
                                ).then_inc(pre_dve, 1)
                dve.wait_ge(pre_dve, 3)
                step(V.reciprocal(wscale[:], wmean[:]))
                wtmp = q0[1][:, 0:4, :].rearrange("p h i -> p (h i)")
                for i, (name, dst) in enumerate((("f_w1", w1q), ("f_w2", w2q))):
                    step(V.tensor_scalar(wtmp, w(name), wscale[:, i:i + 1], ROUND, ALU.mult, ALU.add))
                    step(V.tensor_scalar(wtmp, wtmp, ROUND, 1.0, ALU.subtract, ALU.min))
                    step(V.tensor_scalar(dst[:], wtmp, -1.0, None, ALU.max))
                V.tensor_copy(ident_bf[:], ident).then_inc(pre_dve, 1)

            def rel_right(s, pair):
                dve.wait_ge(r_last, n(s, pair))
                V.tensor_copy(rext[:, :, MAX_REL - 1 + P:M], bank[s][0][:, 0:H].unsqueeze(2)
                              .broadcast_to([P, H, MAX_REL])).then_inc(r_right, 1)

            def keys_v(s, pair):
                dve.wait_ge(x_values, n(s, pair))
                for c in range(2):
                    last = V.tensor_copy(v0[s][0:C, 8 * c:8 * c + 8, :], bank[s][KEY_BANK[c]][0:C, :].rearrange(
                        "p (h d) -> p h d", d=XH))
                last.then_inc(x_v0, 1)

            def keys1(s, pair):
                dve.wait_ge(x_kv1, n(s, pair))
                for a in range(4):
                    V.tensor_scalar(k1bd[s][:, a, :], bank[s][3][:, 0:C], col("c1_bk"),
                                    head8s[:, a:a + 1], ALU.add, ALU.mult)
                V.tensor_tensor(heads(ve[s])[0:C], by_head(bank[s][3][0:C, P:2 * P]),
                                by_head(row("c1_bv")[0:C, :]), ALU.add).then_inc(x_kv1_ready, 1)

            def a_kv_(s, pair):
                dve.wait_ge(a_qkv, n(s, pair))
                for a in range(4):
                    V.tensor_scalar(kbd[s][:, a, :], bank[s][1][:, P:2 * P], col("a0_bk"),
                                    head8s[:, a:a + 1], ALU.add, ALU.mult)
                V.tensor_tensor(heads(va[s]), by_head(bank[s][1][:, 2 * P:3 * P]), by_head(row("a0_bv")),
                                ALU.add).then_inc(a_kv, 1)

            def maxima(k, g):
                def f(s, pair):
                    nk = P if k == "a" else C
                    ps = bank[s][g][:, 0:4 * nk].rearrange("p (a j) -> p a j", a=4)
                    dve.wait_ge(scores[k], n(s, pair, 4, g + 1))
                    if k == "a":
                        if g == 0:
                            dve.wait_ge(ld_rel, n(s, pair, 32))
                        dst = sc[s][:, 4 * g:4 * g + 4, :]
                        step(V.tensor_tensor(dst, ps, rel[:, 4 * g:4 * g + 4, :], ALU.add))
                        ps = dst
                    V.tensor_reduce(nmx[s][:, 4 * g:4 * g + 4], ps, AX.X, ALU.max, negate=True
                                    ).then_inc(maxed[k], 1)
                return f

            def copy_probsT(k, nk, g):
                def f(s, pair):
                    dve.wait_ge(probsT[k], n(s, pair, 4, g + 1))
                    V.tensor_copy(pT[s][0:nk, 4 * g:4 * g + 4, :], bank[s][g][0:nk, :].rearrange(
                        "p (a i) -> p a i", a=4)).then_inc(probsT_odd[k], 1)
                return f

            def b_scale(g):
                def f(s, pair):
                    dve.wait_ge(exped["b"], n(s, pair, 4, g + 1))
                    part = slice(4 * g, 4 * g + 4)
                    step(V.reciprocal(rr[s][:, part], psum_[s][:, part]))
                    V.tensor_tensor(scx[s][:, part, :], scx[s][:, part, :], rr[s][:, part].unsqueeze(2)
                                    .broadcast_to([P, 4, C]), ALU.mult).then_inc(b_scaled, 1)
                return f

            def sums(k):
                def f(s, pair):
                    dve.wait_ge(exped[k], n(s, pair, 4, 4))
                    V.reciprocal(rr[s][:], psum_[s][:]).then_inc(recips[k], 1)
                return f

            def normalise(k):
                def f(s, pair):
                    dve.wait_ge(values[k], n(s, pair))
                    dve.wait_ge(spread_sb[k], n(s, pair))
                    V.tensor_tensor(oT[s][:, 0, :], bank[s][0][:, 0:P], rbc[s][:], ALU.mult
                                    ).then_inc(oT_ready[k], 1)
                return f

            def moments(k, s):
                step(V.bn_stats(stats[s][:], y[s][:]))
                V.bn_aggr(mv[s][:], stats[s][:]).then_inc(var[k], 1)

            def norm(k, s, pair, dst):
                dve.wait_ge(inv[k], n(s, pair))
                V.tensor_scalar(dst[s][:], y[s][:], mv[s][:, 0:1], rstd[s][:, 0:1], ALU.subtract,
                                ALU.mult).then_inc(normed[k], 1)

            def add(k, other, ready, per):
                def f(s, pair):
                    dve.wait_ge(ready, n(s, pair, per))
                    dve.wait_ge(proj[k], n(s, pair))
                    step(V.tensor_tensor(y[s][:], bank[s][2][:, 0:P], other[s][:], ALU.add))
                    moments(k, s)
                return f

            def norms(k):
                def f(s, pair):
                    norm(k, s, pair, x)
                return f

            def d_ln(s, pair):
                dve.wait_ge(inv["d"], n(s, pair))
                step(V.tensor_scalar(y2[s][:], y[s][:], mv[s][:, 0:1], rstd[s][:, 0:1], ALU.subtract,
                                     ALU.mult))
                step(V.tensor_tensor(y2[s][:], y2[s][:], row("a1_lng"), ALU.mult))
                step(V.tensor_tensor(y[s][:], y2[s][:], xb2[s][:], ALU.add))
                moments("D", s)

            def copy_wide(came, dst, ready):
                def f(s, pair):
                    dve.wait_ge(came, n(s, pair))
                    V.tensor_copy(dst[s][:, 4:8, :], bank[s][1][:].rearrange("p (c i) -> p c i", c=4)
                                  ).then_inc(ready, 1)
                return f

            def c_route(s, pair):
                dve.wait_ge(c_logits, n(s, pair))
                step(V.tensor_tensor(lg[s][:], bank[s][3][:, 0:E + 1], row("m_rb"), ALU.add))
                step(V.max(top[s][:], lg[s][:]))
                V.tensor_scalar(nmax[s][:], top[s][:, 0:1], -1.0, None, ALU.mult).then_inc(c_shift, 1)

            def hidden(e):
                def f(s, pair):
                    dve.wait_ge(c_up, n(s, pair, E, e + 1))
                    V.tensor_scalar(hid[1][s], bank[s][1][:], 0.0, None, ALU.max).then_inc(c_hid[e % 2], 1)
                return f

            def c_pick_(s, pair):
                dve.wait_ge(c_exp, n(s, pair))
                step(V.reciprocal(esum[s][:], esum[s][:]))
                step(V.tensor_scalar(wts[s][:], lg[s][:], esum[s][:, 0:1], None, ALU.mult))
                step(V.max(top[s][:], wts[s][:]))
                step(V.max_index(topi[s][:], top[s][:], wts[s][:]))
                step(V.tensor_copy(topf[s][:], topi[s][:, 0:2]))
                mark(V.tensor_scalar(sel[s][:], const("expert"), topf[s][:, 0:1], None, ALU.is_equal))
                step(V.tensor_scalar(sel2[s][:], const("expert"), topf[s][:, 1:2], None, ALU.is_equal))
                step(V.tensor_tensor(sel[s][:], sel[s][:], sel2[s][:], ALU.add))
                V.scalar_tensor_tensor(out=picked[s][:], in0=wts[s][:], scalar=0.0, in1=sel[s][:],
                                       op0=ALU.is_gt, op1=ALU.mult).then_inc(c_pick, 1)
                dve.wait_ge(c_pick, n(s, pair))
                step(V.tensor_tensor(sel2[s][:], wts[s][:], picked[s][:], ALU.mult))

            def c_keep_(s, pair):
                dve.wait_ge(c_rank, n(s, pair))
                V.tensor_tensor(keep[s][:], bank[s][3][:, 0:E + 1], const("cap"), ALU.is_lt
                                ).then_inc(c_keep, 1)
                dve.wait_ge(c_keep, n(s, pair))
                mark(V.tensor_tensor(routed[:], routed[:], picked[s][:], ALU.add))
                step(V.tensor_tensor(keep[s][:], keep[s][:], sel2[s][:], ALU.mult))
                step(V.tensor_scalar(wpass[s][:], keep[s][:, E:E + 1], 1.0, None, ALU.add))
                step(V.tensor_scalar(y[s][:], x[s][:], wpass[s][:, 0:1], None, ALU.mult))

            def combine(part, experts):
                def f(s, pair):
                    dve.wait_ge(c_down[part], n(s, pair))
                    for e in experts:
                        step(V.scalar_tensor_tensor(out=y[s][:], in0=down_out(s, e),
                                                    scalar=keep[s][:, e:e + 1], in1=y[s][:],
                                                    op0=ALU.mult, op1=ALU.add))
                    if part == 2:
                        moments("c", s)
                return f

            def d_gate_(s, pair):
                dve.wait_ge(d_gate0, n(s, pair))
                V.tensor_scalar(eg[s], eg[s], EXP_MAX, 1.0, ALU.min, ALU.add).then_inc(d_gate1, 1)

            def rope(s, pair):
                dve.wait_ge(d_qk, n(s, pair))
                for i, (t, table) in enumerate(((t1, "cos"), (t2, "sin"))):
                    last = V.tensor_tensor(t[s], bank[s][0][:, i * 2 * P:(i + 1) * 2 * P].rearrange(
                        "p (a t) -> p a t", a=2), const(table).unsqueeze(1).broadcast_to([P, 2, P]),
                        ALU.mult)
                step(last)
                V.tensor_tensor(qk[s], t1[s], t2[s], ALU.add).then_inc(d_rope, 1)

            def d_fade(s, pair):
                dve.wait_ge(d_gate, n(s, pair))
                step(V.tensor_tensor(eg[s], eg[s], dk[:], ALU.mult))

            def d_rank_(s, pair):
                dve.wait_ge(d_rank, n(s, pair))
                kr = bank[s][2][:, 2 * P:4 * P].rearrange("p (c t) -> p c t", c=2)
                for c in range(2):
                    mark(V.tensor_tensor(qd[s][:, c, :, :], bank[s][2][:, c * P:(c + 1) * P].unsqueeze(1)
                                         .broadcast_to([P, 2, P]), dqm[:, c, :, :], ALU.mult))
                for g in range(4):
                    V.scalar_tensor_tensor(out=kdm[s][:, g, :, :], in0=kr, scalar=const("group32", g, g + 1),
                                           in1=eg[s], op0=ALU.mult, op1=ALU.mult).then_inc(d_qkd, 1)

            def d_scores(g):
                def f(s, pair):
                    dve.wait_ge(d_att, n(s, pair, 4, g + 1))
                    V.tensor_tensor(sc[s][:, 4 * g:4 * g + 4, :], bank[s][g][:].rearrange(
                        "p (a t) -> p a t", a=4), const("causal").unsqueeze(1).broadcast_to([P, 4, P]),
                        ALU.mult).then_inc(d_masked, 1)
                return f

            def quantise(s, src, c0, dst):
                step(V.tensor_reduce(scol[s][:, c0:c0 + 1], src, AX.X, ALU.max,
                                     apply_absolute_value=True))
                step(V.tensor_scalar(scol[s][:, c0 + 1:c0 + 2], scol[s][:, c0:c0 + 1], 1e-5, 1.0 / QMAX,
                                     ALU.max, ALU.mult))
                step(V.reciprocal(scol[s][:, c0 + 2:c0 + 3], scol[s][:, c0 + 1:c0 + 2]))
                tmp = probs_sb[s][:, 0:dst.shape[-1]]
                step(V.tensor_scalar(tmp, src, scol[s][:, c0 + 2:c0 + 3], ROUND, ALU.mult, ALU.add))
                return V.tensor_scalar(dst, tmp, ROUND, None, ALU.subtract)

            def f_in(s, pair):
                dve.wait_ge(normed["e"], n(s, pair))
                quantise(s, x[s][:], 0, xq[s][:]).then_inc(f_xq, 1)
                V.tensor_scalar(diag[s], ident, scol[s][:, 1:2], None, ALU.mult).then_inc(f_diag, 1)

            def f_up(s, pair):
                dve.wait_ge(f_scbc, n(s, pair))
                dve.wait_ge(f_h, n(s, pair))
                V.tensor_tensor(hp[s][:, :, 1:P + 1], bank[s][2][:].rearrange("p (c t) -> p c t", c=HC),
                                scbc[s].unsqueeze(1).broadcast_to([P, HC, P]), ALU.mult
                                ).then_inc(f_hp, 1)

            def f_conv_(s, pair):
                def tap(c, i):
                    hc = hid[0][s][:, c * P:(c + 1) * P]
                    return V.scalar_tensor_tensor(out=hc, in0=hp[s][:, c, i:i + P],
                                                  scalar=col("f_conv", 3 * c + i), in1=hc,
                                                  op0=ALU.mult, op1=ALU.add)
                for c in range(HC):
                    dve.wait_ge(f_conv0, n(s, pair, HC, c + 1))
                    first = mark(tap(c, 0))
                    if c > 0:
                        after(first - 1)
                        last = tap(c - 1, 2)
                        if c % 2 == 0:
                            last.then_inc(f_conv, 1)
                after(first)
                tap(HC - 1, 2).then_inc(f_conv, 1)

            def f_exp_(i):
                def f(s, pair):
                    part = hid[1][s][:, HALVES[i]]
                    dve.wait_ge(f_exp, n(s, pair, 2, i + 1))
                    V.tensor_scalar(part, part, EXP_MAX, 1.0, ALU.min, ALU.add).then_inc(f_exp1, 1)
                return f

            def f_silu_(i):
                def f(s, pair):
                    part = hid[0][s][:, HALVES[i]]
                    dve.wait_ge(f_sig, n(s, pair, 2, i + 1))
                    V.tensor_tensor(part, part, hid[1][s][:, HALVES[i]], ALU.mult).then_inc(f_silu, 1)
                return f

            def f_quant(s, pair):
                dve.wait_ge(f_hT, n(s, pair, 2))
                quantise(s, bank[s][3][:], 3, hq[s]).then_inc(f_hq, 1)
                dve.wait_ge(f_hq, n(s, pair))
                step(V.tensor_tensor(scol[s][:, 6:7], scol[s][:, 4:5], wmean[:, 1:2], ALU.mult))

            def f_down(s, pair):
                dve.wait_ge(proj["f"], n(s, pair))
                step(V.scalar_tensor_tensor(out=y[s][:], in0=bank[s][1][:, 0:P], scalar=scol[s][:, 6:7],
                                            in1=x[s][:], op0=ALU.mult, op1=ALU.add))
                moments("f", s)

            def f_norm(s, pair):
                norm("f", s, pair, out_sb)

            dve.wait_ge(pre_pool, N_POOL)
            run(dve, HALVES_OF["dve"], {
                "ternary_sum": ternary_sum, "ternary": ternary, "rel_last": rel_right, "keys_v": keys_v, "keys1": keys1, "a_qkv": a_kv_,
                **{f"a_s{g}": maxima("a", g) for g in range(4)}, **{f"a_t{g}": copy_probsT("a", P, g) for g in (1, 3)}, "a_sums": sums("a"),
                "a_div": normalise("a"), "a_out": add("a", xb, xb_ready["a"], 1), "a_ln": norms("a"),
                "b_q": copy_wide(b_q, q0, b_q_hi), **{f"b_s{g}": maxima("b", g) for g in range(4)}, **{f"b_t{g}": copy_probsT("b", C, g) for g in (1, 3)},
                **{f"b_u{g}": b_scale(g) for g in range(4)},
                "b_values": copy_wide(values["b"], oT, oT_ready2),
                "b_out": add("b", x, normed["a"], 1), "b_ln": norms("b"),
                "c_route": c_route, "c_pick": c_pick_, "c_keep": c_keep_,
                **{f"c_up{e}": hidden(e) for e in range(1, E, 2)},
                "c_sum0": combine(0, range(4)), "c_sum1": combine(1, range(4, E - 1)),
                "c_sum2": combine(2, [E - 1]), "c_ln": norms("c"),
                "d_qk": rope, "d_gate": d_gate_, "d_fade": d_fade, "d_rank": d_rank_, **{f"d_s{g}": d_scores(g) for g in range(4)},
                "d_out": add("d", xb, xb_ready["d"], 2), "d_ln": d_ln, "d_ln2": norms("D"),
                **{f"e_s{g}": maxima("e", g) for g in range(4)}, **{f"e_t{g}": copy_probsT("e", C, g) for g in (1, 3)}, "e_sums": sums("e"),
                "e_div": normalise("e"), "e_out": add("e", xb, xb_ready["e"], 1), "e_ln": norms("e"),
                "f_in": f_in, "f_up": f_up, "f_conv": f_conv_, "f_exp0": f_exp_(0), "f_exp1": f_exp_(1),
                "f_silu0": f_silu_(0), "f_silu1": f_silu_(1), "f_quant": f_quant,
                "f_down": f_down, "f_norm": f_norm,
            }, clear)


N_POOL = 3 + 2 * 6


def tables():
    p, t = np.arange(P)[:, None], np.arange(P)[None, :]
    half = DH // 2
    freq = (1.0 / 10000.0 ** (np.arange(half, dtype=np.float32) / np.float32(half))).astype(np.float32)
    angle = (np.arange(P, dtype=np.float32)[None, :] * freq[(np.arange(P) % DH) // 2][:, None]).astype(np.float32)
    sign = np.where(p % 2 == 0, -1.0, 1.0)
    parts = {
        "ident": p == t,
        "tri": p < t,
        "causal": p <= t,
        "cos": np.cos(angle), "sin": np.sin(angle) * sign,
        "time": np.broadcast_to(t - MID, (P, P)),
        "headsel": t // DH == p,
        "head8": (p // DH) % 4 == np.arange(4),
        "group32": p // 32 == np.arange(4),
        "head16": (p // R) % 2 == np.arange(2),
        "expert": np.broadcast_to(np.arange(E + 1), (P, E + 1)),
        "cap": np.broadcast_to(np.where(np.arange(E + 1) < E, CAP, 2 * B * P), (P, E + 1)),
    }
    return np.concatenate([np.asarray(parts[k], np.float32) for k in CONSTS], axis=1)


def kernel(**inputs):
    import concourse.bacc as bacc
    from concourse.bass_utils import run_bass_kernel_spmd

    g = {k: np.asarray(v) for k, v in inputs.items()}

    def by_rows(a, chunk=P):
        return a.reshape(-1, chunk, a.shape[1]).transpose(1, 0, 2).reshape(chunk, -1)

    tab = g["L0_attn_rel_table"]
    rel_bd = np.zeros((4, 4, DH, 4, P), np.float32)
    rel_last = np.zeros((4, 4, DH, 4, H), np.float32)
    for grp in range(4):
        for a in range(4):
            rel_bd[grp, a, :, a, :] = tab[:2 * MAX_REL].T
            rel_last[grp, a, :, grp, 4 * grp + a] = tab[2 * MAX_REL]
    rank = {}
    for name in ("Wq", "Wk"):
        bd = np.zeros((H, DH, H, R), np.float32)
        for h in range(H):
            bd[h, :, h, :] = g[f"L1_attn_{name}"][h].T
        rank[name] = bd.reshape(P, H * R)
    swap = np.arange(P) ^ 1
    inw = g["L1_xattn_in_proj_weight"]
    weights = {
        "a0_wq": g["L0_attn_Wq"], "a0_wk": g["L0_attn_Wk"], "a0_wv": g["L0_attn_Wv"],
        "a0_wo": g["L0_attn_Wo"], "a0_rel": rel_bd.reshape(P, 4 * P), "a0_rel_last": rel_last.reshape(P, 4 * H),
        "c0_wq": g["L0_xattn_Wq"], "c0_wk": g["L0_xattn_Wk"], "c0_wv": g["L0_xattn_Wv"],
        "c0_wo": by_rows(g["L0_xattn_Wo"]),
        "m_router": g["L0_ffn_router_w"].T,
        "m_w1": g["L0_ffn_experts_inter"].transpose(1, 0, 2).reshape(P, -1),
        "m_w2": by_rows(g["L0_ffn_experts_out"].reshape(E * HID, P)),
        "a1_wq": g["L1_attn_q_w"].T, "a1_wqs": g["L1_attn_q_w"][swap].T,
        "a1_wk": g["L1_attn_k_w"].T, "a1_wks": g["L1_attn_k_w"][swap].T,
        "a1_wv": g["L1_attn_v_w"].T, "a1_wg": g["L1_attn_g_w"].T,
        "a1_rq": rank["Wq"], "a1_rk": rank["Wk"], "a1_wo": g["L1_attn_out_w"].T,
        "c1_wq": inw[0:P].T, "c1_wk": inw[P:2 * P].T, "c1_wv": inw[2 * P:3 * P].T,
        "c1_wo": g["L1_xattn_out_proj_weight"].T,
        "f_w1": g["L1_ffn_w1"].T, "f_w2": by_rows(g["L1_ffn_w2"].T),
    }
    inb = g["L1_xattn_in_proj_bias"]
    columns = {
        "a0_bq": g["L0_attn_bq"].reshape(P, 1), "a0_bk": g["L0_attn_bk"].reshape(P, 1),
        "c1_bq": inb[0:P].reshape(P, 1), "c1_bk": inb[P:2 * P].reshape(P, 1),
        "a1_gb": g["L1_attn_g_b"].reshape(2, P).T,
        "a1_decay": g["L1_attn_base_decay_logits"].reshape(2, P).T,
        "f_conv": by_rows(g["L1_ffn_conv_w"].reshape(HID, 3)),
        "f_convb": g["L1_ffn_conv_b"].reshape(HC, P).T,
    }
    rows = {
        "a0_bv": g["L0_attn_bv"], "a0_bo": g["L0_attn_bo"], "m_rb": g["L0_ffn_router_b"],
        "a1_bo": g["L1_attn_out_b"], "a1_lng": g["L1_attn_ln_g"], "a1_lnb": g["L1_attn_ln_b"],
        "c1_bv": inb[2 * P:3 * P], "c1_bo": g["L1_xattn_out_proj_bias"],
    }
    arrays = {
        "x": g["x"].reshape(NP, 2, P, P),
        "xT": g["x"].transpose(0, 2, 1).reshape(NP, 2, P, P),
        "cT": g["ctx_1024"].transpose(0, 2, 1).reshape(NP, 2, P, C),
        "weights": np.concatenate([weights[k] for k in WEIGHTS], axis=1),
        "columns": np.concatenate([columns[k] for k in COLUMNS], axis=1),
        "rows": np.concatenate([rows[k] for k in ROWS]),
        "consts": tables(),
    }
    arrays = {k: np.ascontiguousarray(v) for k, v in arrays.items()}
    nc = bacc.Bacc("TRN2", target_bir_lowering=False, num_devices=1)
    args = [nc.dram_tensor(k, v.shape, F32, kind="ExternalInput").ap() for k, v in arrays.items()]
    out = nc.dram_tensor("out", (NP, 2, P, P), F32, kind="ExternalOutput").ap()
    rel_dram = nc.dram_tensor("rel_dram", (NP, 2, P * RROW), F32, kind="Internal").ap()
    decoder(nc, *args, out, rel_dram)
    r = run_bass_kernel_spmd(nc, [arrays], core_ids=[0])
    return r.results[0]["out"].reshape(B, P, P)
```
